# Optimizing a Trainium2 kernel written in Bass

```python
import numpy as np
import jax
import jax.numpy as jnp

def _softmax(x, axis=-1):
    return jax.nn.softmax(x, axis=axis)

def _gelu(x):
    return jax.nn.gelu(x, approximate=True)

def _silu(x):
    return jax.nn.silu(x)

def _sigmoid(x):
    return jax.nn.sigmoid(x)

def _layernorm(x, axis=-1, eps=1e-05):
    m = jnp.mean(x, axis=axis, keepdims=True)
    v = jnp.var(x, axis=axis, keepdims=True)
    return (x - m) / jnp.sqrt(v + eps)

def _scatter_add(tgt, idx, src, axis=0):
    return tgt.at[idx].add(src)

def _segment_sum(src, seg, n):
    return jax.ops.segment_sum(src, seg, n)
kernel_name = 'mk_seq_postln_d1_jaxref_r8_5f2724'

def setup_inputs(seed: int=0):
    np.random.seed(seed)
    _w = jnp.asarray

    def _L0_attn_setup():
        import jax, jax.numpy as jnp
        import numpy as np
        D_MODEL = 128
        N_HEADS = 16
        HEAD_DIM = D_MODEL // N_HEADS
        key = jax.random.key(seed)
        ks = jax.random.split(key, 5)
        x = jax.random.normal(ks[0], (2, 256, D_MODEL), dtype=jnp.float32)
        s_in = 1.0 / np.sqrt(D_MODEL)
        qkv_w = jax.random.uniform(ks[1], (3 * D_MODEL, D_MODEL), jnp.float32, -s_in, s_in)
        qkv_b = jax.random.uniform(ks[2], (3 * D_MODEL,), jnp.float32, -s_in, s_in)
        out_w = jax.random.uniform(ks[3], (D_MODEL, D_MODEL), jnp.float32, -s_in, s_in)
        out_b = jax.random.uniform(ks[4], (D_MODEL,), jnp.float32, -s_in, s_in)
        return {'x': x, 'qkv_w': qkv_w, 'qkv_b': qkv_b, 'out_w': out_w, 'out_b': out_b}
    _L0_attn_in = _L0_attn_setup()

    def _L0_ffn_setup():
        import jax, jax.numpy as jnp
        import numpy as np
        E = 8
        TOPK = 2

        def _moe_forward(x, Wg, W1, W2, W3):
            B, S, D = x.shape
            xt = x.reshape(-1, D)
            T = xt.shape[0]
            logits = xt @ Wg.T
            scores = jax.nn.softmax(logits, axis=-1)
            w, idx = jax.lax.top_k(scores, TOPK)
            w = w / (w.sum(axis=-1, keepdims=True) + 1e-20)
            cw = jnp.zeros((T, E), xt.dtype).at[jnp.arange(T)[:, None], idx].add(w)
            h = jax.nn.silu(jnp.einsum('td,ehd->teh', xt, W1)) * jnp.einsum('td,ehd->teh', xt, W3)
            out = jnp.einsum('teh,edh->ted', h, W2)
            y = jnp.einsum('te,ted->td', cw, out)
            return y.reshape(B, S, D)
        key = jax.random.key(seed)
        k0, k1, k2, k3, k4 = jax.random.split(key, 5)
        B, S, D, H = (1, 256, 128, 352)
        scale = 0.02
        x = jax.random.normal(k0, (B, S, D), jnp.float32)
        Wg = jax.random.normal(k1, (E, D), jnp.float32) * scale
        W1 = jax.random.normal(k2, (E, H, D), jnp.float32) * scale
        W2 = jax.random.normal(k3, (E, D, H), jnp.float32) * scale
        W3 = jax.random.normal(k4, (E, H, D), jnp.float32) * scale
        return {'x': x, 'Wg': Wg, 'W1': W1, 'W2': W2, 'W3': W3}
    _L0_ffn_in = _L0_ffn_setup()
    _d = {'L0_attn_x': _L0_attn_in['x'], 'L0_attn_qkv_w': _L0_attn_in['qkv_w'], 'L0_attn_qkv_b': _L0_attn_in['qkv_b'], 'L0_attn_out_w': _L0_attn_in['out_w'], 'L0_attn_out_b': _L0_attn_in['out_b'], 'L0_ffn_Wg': _L0_ffn_in['Wg'], 'L0_ffn_W1': _L0_ffn_in['W1'], 'L0_ffn_W2': _L0_ffn_in['W2'], 'L0_ffn_W3': _L0_ffn_in['W3']}
    _x0 = _d['L0_attn_x']
    _d['L0_attn_x'] = jax.random.normal(jax.random.fold_in(jax.random.key(seed), 1), (32, 256, 128), dtype=_x0.dtype)
    del _x0
    return _d

def reference(L0_attn_x, L0_attn_qkv_w, L0_attn_qkv_b, L0_attn_out_w, L0_attn_out_b, L0_ffn_Wg, L0_ffn_W1, L0_ffn_W2, L0_ffn_W3):

    def _L0_attn_ref(x, qkv_w, qkv_b, out_w, out_b):
        import jax, jax.numpy as jnp
        import numpy as np
        D_MODEL = 128
        N_HEADS = 16
        HEAD_DIM = D_MODEL // N_HEADS
        B, L, D = x.shape
        qkv = x @ qkv_w.T + qkv_b
        q, k, v = jnp.split(qkv, 3, axis=-1)
        q = q.reshape(B, L, N_HEADS, HEAD_DIM).transpose(0, 2, 1, 3)
        k = k.reshape(B, L, N_HEADS, HEAD_DIM).transpose(0, 2, 1, 3)
        v = v.reshape(B, L, N_HEADS, HEAD_DIM).transpose(0, 2, 1, 3)
        att = jnp.einsum('bhqd,bhkd->bhqk', q, k) / np.sqrt(HEAD_DIM)
        causal = jnp.tril(jnp.ones((L, L), dtype=bool))
        att = jnp.where(causal[None, None], att, -jnp.inf)
        att = jax.nn.softmax(att, axis=-1)
        out = jnp.einsum('bhqk,bhkd->bhqd', att, v)
        out = out.transpose(0, 2, 1, 3).reshape(B, L, D)
        return out @ out_w.T + out_b

    def _L0_ffn_ref(x, Wg, W1, W2, W3):
        import jax, jax.numpy as jnp
        import numpy as np
        E = 8
        TOPK = 2

        def _moe_forward(x, Wg, W1, W2, W3):
            B, S, D = x.shape
            xt = x.reshape(-1, D)
            T = xt.shape[0]
            logits = xt @ Wg.T
            scores = jax.nn.softmax(logits, axis=-1)
            w, idx = jax.lax.top_k(scores, TOPK)
            w = w / (w.sum(axis=-1, keepdims=True) + 1e-20)
            cw = jnp.zeros((T, E), xt.dtype).at[jnp.arange(T)[:, None], idx].add(w)
            h = jax.nn.silu(jnp.einsum('td,ehd->teh', xt, W1)) * jnp.einsum('td,ehd->teh', xt, W3)
            out = jnp.einsum('teh,edh->ted', h, W2)
            y = jnp.einsum('te,ted->td', cw, out)
            return y.reshape(B, S, D)
        return _moe_forward(x, Wg, W1, W2, W3)
    x = L0_attn_x
    x = _layernorm(x + _L0_attn_ref(x, L0_attn_qkv_w, L0_attn_qkv_b, L0_attn_out_w, L0_attn_out_b), axis=-1)
    x = _layernorm(x + _L0_ffn_ref(x, L0_ffn_Wg, L0_ffn_W1, L0_ffn_W2, L0_ffn_W3), axis=-1)
    return x

_drawn_inputs = setup_inputs


def setup_inputs(seed=0):
    import zlib

    import numpy as np

    out = dict(_drawn_inputs(seed))
    spreads = {}
    factors = {'L0_ffn_Wg': 8.0, 'L0_ffn_W1': 8.0, 'L0_ffn_W2': 8.0, 'L0_ffn_W3': 8.0}
    for name, (base, spread) in spreads.items():
        noise = np.random.default_rng([zlib.crc32(name.encode()), seed]).standard_normal(out[name].shape)
        drawn = base * np.exp(spread * noise) if base else spread * noise
        out[name] = jnp.asarray(drawn.astype(out[name].dtype))
    for name, factor in factors.items():
        out[name] = (out[name] * factor).astype(out[name].dtype)
    return out
```

```python
import numpy as np
from contextlib import ExitStack

import concourse.bass as bass
from concourse import mybir

F32 = mybir.dt.float32
F32R = mybir.dt.float32r
BF16 = mybir.dt.bfloat16
I32 = mybir.dt.int32
ALU = mybir.AluOpType
ACT = mybir.ActivationFunctionType
AX = mybir.AxisListType

P = 128
D = 128
L = 256
BLOCKS = L // P
HEADS, HEAD_DIM = 16, 8
GROUP = 4
GROUPS = HEADS // GROUP
QUAD = 32
PARTS = 3
ROWS = PARTS * HEAD_DIM
SHIFT_ROW = ROWS
MASKED = -1.0e30
EXPERTS, TOPK, HIDDEN = 8, 2, 352
TAKEN = -3.0e38
EPS = 1e-5
LAG = 2


def selectors():
    parts = {"qh": (0, 1), "ql": (2,), "kh": (0, 2), "kl": (1,)}
    out = np.zeros((P, GROUPS, len(parts), P), np.float32)
    for g in range(GROUPS):
        for s, rows in enumerate(parts.values()):
            for j in range(GROUP):
                for r in rows:
                    for d in range(HEAD_DIM):
                        out[(g * GROUP + j) * HEAD_DIM + d, g, s, j * QUAD + r * HEAD_DIM + d] = 1
    return out.reshape(P, -1)


class Visit:

    def __init__(self, eng, n, b=None, base=None, u=0):
        self.eng, self.n, self.b, self.base, self.u = eng, n, b, base, u
        self.values = {}
        self.alone = eng.engine in (mybir.EngineType.SP, mybir.EngineType.Pool)

    def ring(self, off, size=2):
        return ((self.b if self.b is not None else self.u) + off) % size

    def has(self, off):
        return self.b is None or 0 <= self.b + off < self.n

    def value(self, scale, plus):
        if (scale, plus) not in self.values:
            self.values[scale, plus] = self.eng.snap(self.base * scale + plus)
        return self.values[scale, plus]

    def index(self, off, scale=1):
        if self.b is not None:
            return (self.b + off) * scale
        return self.value(scale, (self.u + off) * scale)

    def wait(self, sem, off, per=1):
        if self.b is None or 0 <= self.b + off < self.n:
            self.eng.wait_ge(sem, self.index(off + 1, per))
            if self.alone:
                self.settle()

    def settle(self):
        if self.b is None:
            self.eng.nop(nofuse=True)

    def wait_landed(self, sems, off, dmas=1):
        size, per = len(sems), 16 * dmas
        if self.b is None:
            lap = self.value(per // size, ((self.u + off) // size + 1) * per)
            self.eng.wait_ge(sems[self.ring(off, size)], lap)
            if self.alone:
                self.settle()
        elif 0 <= self.b + off < self.n:
            self.eng.wait_ge(sems[self.ring(off, size)], ((self.b + off) // size + 1) * per)


def visits(eng, n, body, unroll, lead, tail, ahead):
    first = -(-tail // unroll) * unroll
    count = max(0, (n - ahead - first) // unroll)
    for b in range(-lead, first):
        body(Visit(eng, n, b=b))
    if count:
        with eng.Fori(0, count) as i:
            base = eng.snap(i * unroll + first)
            values = {}
            for u in range(unroll):
                turn = Visit(eng, n, base=base, u=u)
                turn.values = values
                body(turn)
    for b in range(first + count * unroll, n + tail):
        body(Visit(eng, n, b=b))


TASKS = [
    [("pack_k0", 1), ("pack_k1", 1), ("project", -2), ("shift2", 0)],
    [("pack_q0", 1), ("pack_q1", 1), ("values", 1), ("heads0", -1), ("shift3", 0)],
    [("heads1", -1), ("split", 2), ("centred", -2), ("shift0", 1)],
    [("mixed", -1), ("router", -2), ("shift1", 1)],
]
ORDER = [t for step in TASKS for t in step]
BANK_OF = {t[0]: i % 2 for i, t in enumerate(ORDER)}


def attention(nc, x, xt, wqkv, bqk, bv, wo, bo, wg, sel, cst, consts, kept):
    y_all, mv_all, logits = kept["y"], kept["mv"], kept["logits"]
    tokens = x.shape[0]
    n = tokens // L
    x_v = x.rearrange("(b k p) d -> b p k d", k=BLOCKS, p=P)
    xt_v = xt.rearrange("d (b t) -> b d t", t=L)

    ctx = ExitStack()
    with ctx:
        def sb(name, shape, dt=F32):
            return ctx.enter_context(nc.sbuf_tensor(name, shape, dt))

        def sem(name):
            return ctx.enter_context(nc.semaphore(name))

        wqkv_sb = sb("wqkv_sb", [P, 3 * D])
        bqk_sb = sb("bqk_sb", [P, 2])
        bv_sb = sb("bv_sb", [P, D])
        wo_sb = sb("wo_sb", [P, D])
        bo_sb = sb("bo_sb", [P, BLOCKS * D])
        wg_sb = sb("wg_sb", [P, EXPERTS])
        sel_f = sb("sel_f", [P, GROUPS * 4 * P])
        sel_r = sb("sel_r", [P, GROUPS, 4, P], F32R)
        ident = cst[:, 0:P]
        ones_rows = cst[:, 2 * P:2 * P + 1]
        ident_bf = sb("ident_bf", [P, P], BF16)
        mask_bf = sb("mask_bf", [P, GROUP, P], BF16)

        x_sb = sb("x_sb", [P, 2, BLOCKS * D])
        xt_sb = sb("xt_sb", [P, 2, L])
        xb = sb("xb", [P, BLOCKS * D])
        split = {k: sb(k, [P, L], F32R) for k in ("qh", "ql", "kh", "kl")}
        q_dense = sb("q_dense", [P, 2, GROUPS, L], F32R)
        k_dense = sb("k_dense", [P, 2, GROUPS, L], F32R)
        q_pad = sb("q_pad", [P, 2, GROUPS, GROUP, L], F32R)
        k_pad = sb("k_pad", [P, 2, GROUPS, GROUP, L], F32R)
        v_ext = sb("v_ext", [P, 2, BLOCKS, HEADS, QUAD])
        neg_max = sb("neg_max", [P, 2, BLOCKS, GROUP])
        shift = sb("shift", [P, 2, 2, GROUP, BLOCKS], F32R)
        shift_t = sb("shift_t", [2 * BLOCKS * GROUP, 2, P], F32R)
        probs = sb("probs", [P, 2, 3 * 512])
        out_t = sb("out_t", [P, 2, GROUPS, L])
        rsum = sb("rsum", [P, 2, HEADS])
        heads = sb("heads", [P, BLOCKS, D])
        heads_t = sb("heads_t", [P, L])
        y = sb("y", [P, BLOCKS, D])
        stats = sb("stats", [P, BLOCKS, 6])
        mv = sb("mv", [P, BLOCKS, 2])
        yc = sb("yc", [P, BLOCKS, D])
        yc_t = sb("yc_t", [P, L])

        ps_s = ctx.enter_context(nc.psum_tensor("ps_s", [P, 2, 512], F32))
        ps_st = ctx.enter_context(nc.psum_tensor("ps_st", [P, 3, 512], F32))
        ps_o = ctx.enter_context(nc.psum_tensor("ps_o", [P, 512], F32))
        ps_m = ctx.enter_context(nc.psum_tensor("ps_m", [P, 2, 512], F32))

        loaded = sem("loaded")
        consts_ready = sem("consts_ready")
        zeroed = sem("zeroed")
        x_landed, xt_landed, k_pad_landed, q_pad_landed = (
            [sem(f"{name}{i}") for i in range(2)] for name in ("x_landed", "xt_landed", "k_pad_landed", "q_pad_landed"))
        s_done = [[sem(f"s_done{g}{k}") for k in range(3)] for g in range(GROUPS)]
        max_done = [[sem(f"max_done{g}{k}") for k in range(3)] for g in range(GROUPS)]
        shift_hi = [sem(f"shift_hi{g}") for g in range(GROUPS)]
        shift_ready = [sem(f"shift_ready{g}") for g in range(GROUPS)]
        shift_landed = [sem(f"shift_landed{g}") for g in range(GROUPS)]
        st_done = [sem(f"st_done{g}") for g in range(GROUPS)]
        exp_done = [sem(f"exp_done{g}") for g in range(GROUPS)]
        masked = [sem(f"masked{g}") for g in range(GROUPS)]
        pv_done = [sem(f"pv_done{g}") for g in range(GROUPS)]
        out_t_ready = [sem(f"out_t_ready{g}") for g in range(GROUPS)]
        made = {t: sem(f"made_{t}") for t, _ in ORDER}
        taken = {t: sem(f"taken_{t}") for t, _ in ORDER}
        high_ready = sem("high_ready")
        rsum_ready = [sem(f"rsum_ready{i}") for i in range(BLOCKS)]
        xb_ready = sem("xb_ready")
        stats_ready, mv_ready, yc_ready, y_kept = map(sem, ("stats_ready", "mv_ready", "yc_ready", "y_kept"))

        block = ctx.enter_context(nc.Block())

        def scores_group(g):
            return (g + LAG) % GROUPS, (g + LAG) // GROUPS

        def values_group(g):
            return (g - 1) % GROUPS, (g - 1) // GROUPS

        S_BANK = [[(3 * g + k) % 2 for k in range(3)] for g in range(GROUPS)]
        N_CONST_LOADS = 8

        @block.sync
        def _(sp):
            for dst, src in ((wqkv_sb[:], wqkv), (bqk_sb[:], bqk), (bv_sb[:], bv), (wo_sb[:], wo), (bo_sb[:], bo),
                             (wg_sb[:], wg), (sel_f[:], sel), (cst[:], consts)):
                sp.dma_start(dst, src).then_inc(loaded, 16)

            def visit(it):
                def load_xt(off):
                    sp.dma_start(xt_sb[:, it.ring(off), :], xt_v[it.index(off)]).then_inc(xt_landed[it.ring(off)], 16)

                if it.b == -2:
                    load_xt(2)
                    load_xt(3)
                for g in range(GROUPS):
                    if g == 0 and it.has(1):
                        p = it.ring(1)
                        it.wait(taken["pack_k0"], 1)
                        it.wait(taken["pack_k1"], 1)
                        it.wait(s_done[GROUPS - 1][2], -1)
                        if it.b == -1:
                            sp.wait_ge(zeroed, 1)
                        for j in range(GROUP):
                            r = slice(QUAD * j, QUAD * j + ROWS)
                            sp.dma_start(k_pad[r, p, :, j, :].bitcast(F32), k_dense[r, p, :, :].bitcast(F32)).then_inc(k_pad_landed[p], 16)
                    if g == 1 and it.has(1):
                        p = it.ring(1)
                        it.wait(taken["pack_q0"], 1)
                        it.wait(taken["pack_q1"], 1)
                        it.wait(st_done[GROUPS - 1], -1)
                        if it.b == -1:
                            sp.wait_ge(zeroed, 2)
                        for j in range(GROUP):
                            r = slice(QUAD * j, QUAD * j + ROWS)
                            sp.dma_start(q_pad[r, p, :, j, :].bitcast(F32), q_dense[r, p, :, :].bitcast(F32)).then_inc(q_pad_landed[p], 16)
                    if g == 2 and it.has(3) and not it.b == -2:
                        it.wait(made["values"], 1)
                        load_xt(3)
                    if g == 3 and it.has(0):
                        it.wait(xb_ready, -2)
                        sp.dma_start(x_sb[:, it.ring(0), :].rearrange("p (k d) -> p k d", k=BLOCKS),
                                     x_v[it.index(0)]).then_inc(x_landed[it.ring(0)], 16)
                    h, off = scores_group(g)
                    if it.has(off):
                        p = it.ring(off)
                        it.wait(taken[f"shift{h}"], off)
                        it.wait(st_done[h], off - 2)
                        sp.dma_start(
                            q_pad[SHIFT_ROW:SHIFT_ROW + 2, p, h, :, :].bitcast(F32).rearrange(
                                "s j (k q) -> s (j k) q", k=BLOCKS),
                            shift_t[:, h % 2, :].bitcast(F32)).then_inc(shift_landed[h], 16)

            visits(sp, n, visit, unroll=2, lead=2, tail=3, ahead=3)

        @block.gpsimd
        def _(pool):
            pool.memset(k_pad[:].bitcast(F32), 0.0).then_inc(zeroed, 1)
            pool.memset(q_pad[:].bitcast(F32), 0.0).then_inc(zeroed, 1)
            pool.memset(v_ext[:], 0.0).then_inc(zeroed, 1)
            pool.wait_ge(zeroed, 3)
            pool.memset(v_ext[:, :, :, :, HEAD_DIM:HEAD_DIM + 1], 1.0).then_inc(zeroed, 1)

            def visit(it):
                for g in range(GROUPS):
                    if it.has(0):
                        it.wait(exp_done[g], 0)
                        low = probs[:, g % 2, 0:GROUP * L].rearrange("p (h q) -> p h q", q=L)[:, :, 0:P]
                        high = probs[:, g % 2, GROUP * L:].rearrange("p (h q) -> p h q", q=P)
                        for part in (low, high):
                            last = pool.affine_select(out=part, in_=part, compare_op=ALU.is_ge, fill=0.0, base=0,
                                                      pattern=[[0, GROUP], [1, P]], channel_multiplier=-1)
                        last.then_inc(masked[g], 1)
                    if g == 0 and it.has(-2):
                        it.wait(mv_ready, -2)
                        for k in range(BLOCKS):
                            last = pool.tensor_scalar(yc[:, k, :], y[:, k, :], mv[:, k, 0:1], None, ALU.subtract)
                        last.then_inc(yc_ready, 1)
                        it.wait(yc_ready, -2)
                        pool.tensor_copy(y_all[:].rearrange("p t d -> p (t d)")[
                            :, bass.ds(it.index(-2, BLOCKS * D), BLOCKS * D)],
                            yc[:].rearrange("p k d -> p (k d)"))
                        pool.tensor_copy(mv_all[:].rearrange("p t d -> p (t d)")[
                            :, bass.ds(it.index(-2, BLOCKS * 2), BLOCKS * 2)],
                            mv[:].rearrange("p k d -> p (k d)")).then_inc(y_kept, 1)
                    if g == 1 and it.has(-1):
                        it.wait_landed(x_landed, -1)
                        it.wait(taken["project"], -2)
                        pool.tensor_tensor(xb[:], x_sb[:, it.ring(-1), :], bo_sb[:], ALU.add).then_inc(xb_ready, 1)

            pool.wait_ge(loaded, 16 * N_CONST_LOADS)
            visits(pool, n, visit, unroll=2, lead=2, tail=3, ahead=3)

        @block.scalar
        def _(act):
            act.wait_ge(loaded, 16 * N_CONST_LOADS)

            def copy_out(it, task, off, dst, src, bias=None):
                it.wait(made[task], off)
                if bias is None:
                    act.activation(dst, src, ACT.Copy).then_inc(taken[task], 1)
                else:
                    act.activation(dst, src, ACT.Identity, bias=bias).then_inc(taken[task], 1)

            def task(it, name, off):
                p = it.ring(off)
                bank = ps_m[:, BANK_OF[name], :]
                if name in ("pack_k0", "pack_k1"):
                    h = 2 * int(name[-1])
                    it.wait_landed(k_pad_landed, off - 2, GROUP)
                    it.wait(st_done[GROUPS - 1], off - 2)
                    copy_out(it, name, off, k_dense[:, p, h:h + 2, :].rearrange("p g t -> p (g t)"), bank, ones_rows)
                if name in ("pack_q0", "pack_q1"):
                    h = 2 * int(name[-1])
                    it.wait_landed(q_pad_landed, off - 2, GROUP)
                    it.wait(s_done[GROUPS - 1][2], off - 2)
                    copy_out(it, name, off, q_dense[:, p, h:h + 2, :].rearrange("p g t -> p (g t)"), bank)
                if name == "split":
                    it.wait(made["split"], off)
                    it.wait(made["pack_q1"], off - 1)
                    act.activation(split["qh"][:], bank[:, 0:L], ACT.Identity, bias=bqk_sb[:, 0:1])
                    act.activation(split["kh"][:], bank[:, L:2 * L], ACT.Identity,
                                   bias=bqk_sb[:, 1:2]).then_inc(high_ready, 1)
                if name.startswith("shift"):
                    h = int(name[-1])
                    it.wait(shift_landed[(h + 2) % GROUPS], off if h >= 2 else off - 1, 16)
                    copy_out(it, name, off, shift_t[:, h % 2, :], bank[0:2 * BLOCKS * GROUP, 0:P])
                if name == "mixed":
                    it.wait(made["project"], off - 1)
                    copy_out(it, name, off, heads_t[:], bank[:, 0:L])
                if name == "centred":
                    it.wait(made["router"], off - 1)
                    copy_out(it, name, off, yc_t[:], bank[:, 0:L])
                if name == "router":
                    copy_out(it, name, off, logits[:].rearrange("p t e -> p (t e)")[
                        :, bass.ds(it.index(off, EXPERTS * BLOCKS), EXPERTS * BLOCKS)], bank[:, 0:EXPERTS * BLOCKS])

            def visit(it):
                for g in range(GROUPS):
                    if it.has(0):
                        it.wait(st_done[g], 0)
                        it.wait(pv_done[(g + 2) % GROUPS], 0 if g >= 2 else -1)
                        act.activation(probs[:, g % 2, :], ps_st[:].rearrange("p k f -> p (k f)"), ACT.Exp,
                                       scale=float(HEAD_DIM) ** -0.5).then_inc(exp_done[g], 1)
                    for name, off in TASKS[g][:2]:
                        if it.has(off):
                            task(it, name, off)
                    h, off = values_group(g)
                    if it.has(off):
                        p = it.ring(off)
                        it.wait(pv_done[h], off)
                        it.wait(made["heads1"], off - 2)
                        act.activation(out_t[:, p, h, :], ps_o[:, 0:L], ACT.Copy).then_inc(out_t_ready[h], 1)
                    for name, off in TASKS[g][2:]:
                        if it.has(off):
                            task(it, name, off)

            visits(act, n, visit, unroll=2, lead=2, tail=3, ahead=3)

        @block.vector
        def _(dve):
            dve.wait_ge(loaded, 16 * N_CONST_LOADS)
            nc.vector.tensor_copy(sel_r[:].rearrange("p g s m -> p (g s m)"), sel_f[:]).then_inc(consts_ready, 1)
            nc.vector.tensor_copy(ident_bf[:], ident).then_inc(consts_ready, 1)
            for j in range(GROUP):
                nc.vector.tensor_copy(mask_bf[:, j, :], cst[:, P:2 * P]).then_inc(consts_ready, 1)

            def task(it, name, off):
                p = it.ring(off)
                bank = ps_m[:, BANK_OF[name], :]
                if name == "split":
                    it.wait(high_ready, off)
                    nc.vector.scalar_tensor_tensor(split["ql"][:], bank[:, 0:L], bqk_sb[:, 0:1],
                                                   split["qh"][:].bitcast(F32), ALU.add, ALU.subtract)
                    nc.vector.scalar_tensor_tensor(split["kl"][:], bank[:, L:2 * L], bqk_sb[:, 1:2],
                                                   split["kh"][:].bitcast(F32), ALU.add,
                                                   ALU.subtract).then_inc(taken[name], 1)
                if name == "values":
                    it.wait(made[name], off)
                    it.wait(pv_done[GROUPS - 1], off - 2)
                    if it.b is not None and it.b + off < 2:
                        dve.wait_ge(zeroed, 4)
                    for k in range(BLOCKS):
                        last = nc.vector.tensor_tensor(
                            v_ext[:, p, k, :, 0:HEAD_DIM],
                            bank[:, k * D:(k + 1) * D].rearrange("p (h d) -> p h d", d=HEAD_DIM),
                            bv_sb[:].rearrange("p (h d) -> p h d", d=HEAD_DIM), ALU.add)
                    last.then_inc(taken[name], 1)
                if name in ("heads0", "heads1"):
                    k = int(name[-1])
                    it.wait(made[name], off)
                    v = bank.rearrange("p (h d) -> p h d", d=QUAD)
                    nc.vector.reciprocal(rsum[:, k, :].rearrange("p (h o) -> p h o", o=1),
                                         v[:, :, HEAD_DIM:HEAD_DIM + 1]).then_inc(rsum_ready[k], 1)
                    it.wait(rsum_ready[k], off)
                    it.wait(made["mixed"], off - 1)
                    nc.vector.tensor_tensor(
                        heads[:, k, :].rearrange("p (h d) -> p h d", d=HEAD_DIM), v[:, :, 0:HEAD_DIM],
                        rsum[:, k, :].rearrange("p (h o) -> p h o", o=1).to_broadcast([P, HEADS, HEAD_DIM]),
                        ALU.mult).then_inc(taken[name], 1)
                if name == "project":
                    it.wait(made[name], off)
                    it.wait(xb_ready, off)
                    it.wait(y_kept, off - 1)
                    nc.vector.tensor_tensor(y[:].rearrange("p k d -> p (k d)"), bank[:, 0:BLOCKS * D], xb[:],
                                            ALU.add).then_inc(taken[name], 1)
                    it.wait(taken[name], off)
                    for k in range(BLOCKS):
                        last = nc.vector.bn_stats(stats[:, k, :], y[:, k, :])
                    last.then_inc(stats_ready, 1)
                    it.wait(stats_ready, off)
                    it.settle()
                    for k in range(BLOCKS):
                        last = nc.vector.bn_aggr(mv[:, k, :], stats[:, k, :])
                    last.then_inc(mv_ready, 1)

            def visit(it):
                for g in range(GROUPS):
                    h, off = scores_group(g)
                    if it.has(off):
                        for k in range(3):
                            it.wait(s_done[h][k], off)
                            bank = ps_s[:, S_BANK[h][k], :]
                            src = bank.rearrange("p (h t) -> p h t", t=P if k == 0 else L)
                            dst = neg_max[:, h % 2, 0, :] if k == 0 else neg_max[:, h % 2, 1, 2 * k - 2:2 * k]
                            nc.vector.tensor_reduce(out=dst, in_=src, axis=AX.X, op=ALU.max,
                                                    negate=True).then_inc(max_done[h][k], 1)
                        it.wait(made[f"shift{(h + 2) % GROUPS}"], off if h >= 2 else off - 1)
                        it.wait(max_done[h][2], off)
                        m = neg_max[:, h % 2, :, :].rearrange("p k j -> p j k")
                        nc.vector.tensor_copy(shift[:, h % 2, 0, :, :], m).then_inc(shift_hi[h], 1)
                        it.wait(shift_hi[h], off)
                        nc.vector.tensor_tensor(shift[:, h % 2, 1, :, :], m, shift[:, h % 2, 0, :, :].bitcast(F32),
                                                ALU.subtract).then_inc(shift_ready[h], 1)
                    for name, off in TASKS[g]:
                        if it.has(off) and name in ("split", "values", "heads0", "heads1", "project"):
                            task(it, name, off)

            visits(dve, n, visit, unroll=2, lead=2, tail=3, ahead=3)

        @block.tensor
        def _(pe):
            pe.wait_ge(loaded, 16 * N_CONST_LOADS)
            pe.wait_ge(consts_ready, 2 + GROUP)
            mm = nc.tensor.matmul

            def task(it, name, off):
                p = it.ring(off)
                bank = ps_m[:, BANK_OF[name], :]
                at = ORDER.index((name, off))
                if it.b is None:
                    before, boff = ORDER[(at - 2) % len(ORDER)]
                    it.wait(taken[before], boff if at >= 2 else boff - 1)
                else:
                    found = False
                    for back in range(2, 4 * len(ORDER), 2):
                        before, boff = ORDER[(at - back) % len(ORDER)]
                        boff += (at - back) // len(ORDER)
                        if not found and it.has(boff):
                            it.wait(taken[before], boff)
                            found = True
                if name == "split":
                    it.wait_landed(xt_landed, off)
                    for i in range(2):
                        last = mm(bank[:, i * L:(i + 1) * L], wqkv_sb[:, i * D:(i + 1) * D], xt_sb[:, p, :],
                                  start=True, stop=True)
                if name == "values":
                    for k in range(BLOCKS):
                        last = mm(bank[:, k * D:(k + 1) * D], xt_sb[:, p, k * P:(k + 1) * P], wqkv_sb[:, 2 * D:],
                                  start=True, stop=True)
                if name.startswith("pack"):
                    it.wait(taken["split"], off)
                    hi, lo, s = ("kh", "kl", 2) if "k" in name[5:] else ("qh", "ql", 0)
                    for i in range(2):
                        g = 2 * int(name[-1]) + i
                        mm(bank[:, i * L:(i + 1) * L], sel_r[:, g, s, :], split[hi][:], start=True, stop=False)
                        last = mm(bank[:, i * L:(i + 1) * L], sel_r[:, g, s + 1, :], split[lo][:], start=False,
                                  stop=True)
                if name.startswith("shift"):
                    h = int(name[-1])
                    it.wait(shift_ready[h], off)
                    last = nc.tensor.transpose(bank[0:2 * BLOCKS * GROUP, 0:P],
                                               shift[:, h % 2, :, :, :].rearrange("p s j k -> p (s j k)").bitcast(F32), ident)
                if name in ("heads0", "heads1"):
                    k = int(name[-1])
                    it.wait(out_t_ready[GROUPS - 1], off)
                    for g in range(GROUPS):
                        last = nc.tensor.transpose(bank[:, g * P:(g + 1) * P], out_t[:, p, g, k * P:(k + 1) * P], ident)
                if name == "mixed":
                    it.wait(taken["heads0"], off)
                    it.wait(taken["heads1"], off)
                    for k in range(BLOCKS):
                        last = nc.tensor.transpose(bank[:, k * P:(k + 1) * P], heads[:, k, :], ident)
                if name == "project":
                    it.wait(taken["mixed"], off)
                    for k in range(BLOCKS):
                        last = mm(bank[:, k * D:(k + 1) * D], heads_t[:, k * P:(k + 1) * P], wo_sb[:], start=True,
                                  stop=True)
                if name == "centred":
                    it.wait(yc_ready, off)
                    for k in range(BLOCKS):
                        last = nc.tensor.transpose(bank[:, k * P:(k + 1) * P], yc[:, k, :], ident)
                if name == "router":
                    it.wait(taken["centred"], off)
                    for k in range(BLOCKS):
                        last = mm(bank[:, EXPERTS * k:EXPERTS * (k + 1)], yc_t[:, k * P:(k + 1) * P], wg_sb[:], start=True, stop=True)
                last.then_inc(made[name], 1)

            def scores(it, h, off, k):
                p = it.ring(off)
                if k == 0:
                    if h == 0:
                        it.wait_landed(k_pad_landed, off, GROUP)
                        it.wait(taken["pack_q0"], off)
                    if h == 2:
                        it.wait(taken["pack_q1"], off)
                back = 3 * h + k - 2
                it.wait(max_done[(back // 3) % GROUPS][back % 3], off if back >= 0 else off - 1)
                bank = ps_s[:, S_BANK[h][k], :]
                if k == 0:
                    mm(bank, q_dense[:, p, h, 0:P], k_pad[:, p, h, :, 0:P], start=True, stop=False)
                    last = mm(bank, ident_bf[:], mask_bf[:], start=False, stop=True)
                else:
                    mm(bank, q_dense[:, p, h, P:L], k_pad[:, p, h, 2 * k - 2:2 * k, :], start=True, stop=False)
                    last = mm(bank.rearrange("p (j t) -> p j t", t=L)[:, :, P:L], ident_bf[:], mask_bf[:, 0:2, :],
                              start=False, stop=True)
                last.then_inc(s_done[h][k], 1)

            def products(it, g):
                p = it.ring(0)
                if g == 0:
                    it.wait_landed(q_pad_landed, 0, GROUP)
                it.wait(shift_landed[g], 0, 16)
                it.wait(exp_done[g - 1], 0 if g else -1)
                for i in range(2):
                    mm(ps_st[:, i, :], k_dense[:, p, g, 0:P], q_pad[:, p, g, 2 * i:2 * i + 2, :], start=True, stop=True)
                mm(ps_st[:, 2, :], k_dense[:, p, g, P:L], q_pad[:, p, g, :, P:L], start=True,
                   stop=True).then_inc(st_done[g], 1)

            def weighted(it, h, off):
                p = it.ring(off)
                it.wait(masked[h], off)
                if h == 0:
                    it.wait(taken["values"], off)
                it.wait(out_t_ready[h - 1], off if h else off - 1)
                for k in range(BLOCKS):
                    for j in range(GROUP):
                        cols = slice(j * L, (j + 1) * L) if k == 0 else slice(GROUP * L + j * P, GROUP * L + (j + 1) * P)
                        last = mm(ps_o[QUAD * j:QUAD * (j + 1), k * P:L], v_ext[:, p, k, h * GROUP + j, :],
                                  probs[:, h % 2, cols], start=(k == 0), stop=(k == BLOCKS - 1))
                last.then_inc(pv_done[h], 1)

            def visit(it):
                for g in range(GROUPS):
                    h, off = scores_group(g)
                    if it.has(off):
                        scores(it, h, off, 0)
                        scores(it, h, off, 1)
                    if it.has(0):
                        products(it, g)
                    if it.has(off):
                        scores(it, h, off, 2)
                    for name, toff in TASKS[g][:2]:
                        if it.has(toff):
                            task(it, name, toff)
                    vh, voff = values_group(g)
                    if it.has(voff):
                        weighted(it, vh, voff)
                    for name, toff in TASKS[g][2:]:
                        if it.has(toff):
                            task(it, name, toff)
                if it.b == 1:
                    it.wait(taken["mixed"], -1)
                    it.wait(taken["shift1"], 1)
                    it.wait(taken["shift0"], 1)

            visits(pe, n, visit, unroll=2, lead=2, tail=3, ahead=3)


def routing(nc, consts_at, w1, w3, w2, kept, x1_rows):
    y_all, mv_all, logits = kept["y"], kept["mv"], kept["logits"]
    weight, pairs, expert_of = kept["weight"], kept["pairs"], kept["expert_of"]
    tiles = logits.shape[1]
    places = pairs.shape[1]
    tokens = tiles * P
    E = EXPERTS
    STORE = 8

    ctx = ExitStack()
    with ctx:
        def sb(name, shape, dt=F32):
            return ctx.enter_context(nc.sbuf_tensor(name, shape, dt))

        def sem(name):
            return ctx.enter_context(nc.semaphore(name))

        var_eps, std, rstd = (sb(k, [P, tiles]) for k in ("var_eps", "std", "rstd"))
        lg, lg2, hit, diff = (sb(k, [P, tiles, E]) for k in ("lg", "lg2", "hit", "diff"))
        oh = [sb(f"oh{k}", [P, tiles, E]) for k in range(TOPK)]
        top = [sb(f"top{k}", [P, tiles]) for k in range(TOPK)]
        first = sb("first", [P, tiles])
        gap = sb("gap", [P, tiles])
        expo = sb("expo", [P, tiles, E])
        e_gap = sb("e_gap", [P, tiles])
        total, rtotal, den = (sb(k, [P, tiles]) for k in ("total", "rtotal", "den"))
        score = [sb(f"score{k}", [P, tiles]) for k in range(TOPK)]
        chosen = sb("chosen", [P, E, tiles], BF16)
        ones_bf = sb("ones_bf", [P, P], BF16)
        before_bf = sb("before_bf", [P, P], BF16)
        iota_bf = sb("iota_bf", [P, max(P, places)], BF16)
        ones = sb("ones", [P, tiles])
        in_tile = sb("in_tile", [P, E, tiles])
        prior = sb("prior", [P, E, tiles])
        place = sb("place", [P, E, tiles])
        count, needed, ends, starts = (sb(k, [P, E]) for k in ("count", "needed", "ends", "starts"))
        needed_i = sb("needed_i", [P, E], I32)
        at_place = sb("at_place", [P, TOPK, tiles])
        at_i = sb("at_i", [P, TOPK, tiles], I32)
        low_i, high_i = (sb(k, [P, TOPK, tiles], I32) for k in ("low_i", "high_i"))
        low, high = (sb(k, [P, TOPK, tiles]) for k in ("low", "high"))
        ge_end = sb("ge_end", [P, places, E])
        expert_f = sb("expert_f", [P, places])
        one_hot = sb("one_hot", [P, 2, TOPK, P], BF16)
        marked = sb("marked", [P, 2, TOPK, 2, places], BF16)
        found = sb("found", [P, 2, places])
        empty, row, over = (sb(k, [P, places]) for k in ("empty", "row", "over"))

        ps_before = ctx.enter_context(nc.psum_tensor("ps_before", [P, 512], F32))
        ps_total = ctx.enter_context(nc.psum_tensor("ps_total", [P, 512], F32))
        ps_pairs = ctx.enter_context(nc.psum_tensor("ps_pairs", [P, 512], F32))

        step = sem("step")
        var_ready, std_ready, rstd_ready, gaps_ready, exps_ready = map(
            sem, ("var_ready", "std_ready", "rstd_ready", "gaps_ready", "exps_ready"))
        chosen_ready, counted, hot_ready, pairs_done = map(sem, ("chosen_ready", "counted", "hot_ready", "pairs_done"))
        scaled, x1_stored, weights_landed = sem("scaled"), sem("x1_stored"), sem("weights_landed")
        PICKS = {f"hot_used{k}": sem(f"hot_used{k}") for k in range(TOPK)}

        block = ctx.enter_context(nc.Block())

        @block.sync
        def _(sp):
            sp.dma_start(kept["w1"][:], w1).then_inc(weights_landed, 16)
            sp.dma_start(kept["w3"][:], w3).then_inc(weights_landed, 16)
            for i, c in enumerate(range(0, HIDDEN, P)):
                n = min(P, HIDDEN - c)
                sp.dma_start(kept["w2"][0:n, i * EXPERTS * D:(i + 1) * EXPERTS * D], w2[c:c + n, :]).then_inc(
                    weights_landed, 16)
            rows = x1_rows.rearrange("(c t p) d -> c p t d", p=P, t=STORE)
            with sp.Fori(0, tiles // STORE) as c:
                ready, landed = sp.snap(c + 1), sp.snap(c * 16 + 16)
                sp.wait_ge(scaled, ready)
                sp.dma_start(rows[c], y_all[:].rearrange("p (c t) d -> p c t d", t=STORE)[:, c, :, :]).then_inc(
                    x1_stored, 16)
                sp.wait_ge(x1_stored, landed)
                sp.nop(nofuse=True)
            sp.wait_ge(weights_landed, 16 * (2 + -(-HIDDEN // P)))

        @block.scalar
        def _(act):
            act.wait_ge(var_ready, 1)
            act.activation(std[:], var_eps[:], ACT.Sqrt).then_inc(std_ready, 1)
            act.wait_ge(gaps_ready, 1)
            act.activation(expo[:].rearrange("p t e -> p (t e)"), diff[:].rearrange("p t e -> p (t e)"),
                           ACT.Exp).then_inc(exps_ready, 1)
            act.activation(e_gap[:], gap[:], ACT.Exp).then_inc(exps_ready, 1)
            act.wait_ge(rstd_ready, 1)
            with act.Fori(0, tiles // STORE) as c:
                for t in range(STORE):
                    at = c * STORE + t
                    last = act.activation(y_all[:].rearrange("p t d -> p (t d)")[:, bass.ds(at * D, D)],
                                          y_all[:].rearrange("p t d -> p (t d)")[:, bass.ds(at * D, D)],
                                          ACT.Identity, scale=rstd[:, bass.ds(at, 1)])
                last.then_inc(scaled, 1)

        @block.vector
        def _(dve):
            v = nc.vector
            done = [0]

            def chain(instruction):
                done[0] += 1
                instruction.then_inc(step, 1)
                dve.wait_ge(step, done[0])

            def over_experts(a):
                return a.rearrange("p (t o) -> p t o", o=1).to_broadcast([P, tiles, E])

            numbers = consts_at("less_8").rearrange("p (o e) -> p o e", o=1).to_broadcast([P, tiles, E])
            v.memset(ones_bf[:], 1.0)
            v.memset(ones[:], 1.0)
            v.tensor_copy(iota_bf[:], consts_at("iota"))
            v.tensor_copy(before_bf[:], consts_at("before"))
            v.tensor_scalar(var_eps[:], mv_all[:, :, 1], EPS, None, ALU.add).then_inc(var_ready, 1)
            dve.wait_ge(std_ready, 1)
            v.reciprocal(rstd[:], std[:]).then_inc(rstd_ready, 1)
            dve.wait_ge(rstd_ready, 1)
            chain(v.tensor_tensor(lg[:], logits[:], over_experts(rstd[:]), ALU.mult))
            cur = lg
            for k in range(TOPK):
                chain(v.tensor_reduce(out=top[k][:], in_=cur[:], axis=AX.X, op=ALU.max))
                chain(v.tensor_tensor(hit[:], cur[:], over_experts(top[k][:]), ALU.is_equal))
                chain(v.tensor_tensor(hit[:], hit[:], numbers, ALU.mult))
                chain(v.tensor_reduce(out=first[:], in_=hit[:], axis=AX.X, op=ALU.min))
                chain(v.tensor_tensor(oh[k][:], numbers, over_experts(first[:]), ALU.is_equal))
                if k == 0:
                    chain(v.scalar_tensor_tensor(lg2[:].rearrange("p t e -> p (t e)"),
                                                 oh[0][:].rearrange("p t e -> p (t e)"), TAKEN,
                                                 lg[:].rearrange("p t e -> p (t e)"), ALU.mult, ALU.add))
                    cur = lg2
            chain(v.tensor_tensor(gap[:], top[1][:], top[0][:], ALU.subtract))
            v.tensor_tensor(diff[:], lg[:], over_experts(top[0][:]), ALU.subtract).then_inc(gaps_ready, 1)
            v.tensor_tensor(chosen[:].rearrange("p e t -> p t e"), oh[0][:], oh[1][:], ALU.add).then_inc(chosen_ready, 1)

            dve.wait_ge(counted, 2)
            flat = "p e t -> p (e t)"
            chain(v.tensor_copy(in_tile[:].rearrange(flat), ps_total[:, 0:E * tiles]))
            chain(v.tensor_reduce(out=count[:], in_=in_tile[:], axis=AX.X, op=ALU.add))
            chain(v.tensor_scalar(needed_i[:], count[:], 1.0 / P, (P - 1.0) / (2 * P), ALU.mult, ALU.add))
            chain(v.tensor_copy(needed[:], needed_i[:]))
            chain(v.tensor_tensor_scan(ends[:], ones[:, 0:E], needed[:], 0.0, ALU.mult, ALU.add))
            chain(v.tensor_tensor(starts[:], ends[:], needed[:], ALU.subtract))
            chain(v.tensor_scalar(starts[:], starts[:], float(P), None, ALU.mult))
            for e in range(E):
                last = v.tensor_tensor_scan(prior[:, e, :], ones[:], in_tile[:, e, :], starts[:, e:e + 1],
                                            ALU.mult, ALU.add)
            chain(last)
            chain(v.tensor_tensor(prior[:], prior[:], in_tile[:], ALU.subtract))
            chain(v.tensor_tensor(place[:].rearrange(flat), prior[:].rearrange(flat), ps_before[:, 0:E * tiles], ALU.add))
            for k in range(TOPK):
                chain(v.tensor_tensor(hit[:], oh[k][:], place[:].rearrange("p e t -> p t e"), ALU.mult))
                chain(v.tensor_reduce(out=at_place[:, k, :], in_=hit[:], axis=AX.X, op=ALU.add))
            chain(v.tensor_copy(at_i[:], at_place[:]))
            v.tensor_single_scalar(out=low_i[:], in_=at_i[:], scalar=P - 1, op=ALU.bitwise_and)
            chain(v.tensor_single_scalar(out=high_i[:], in_=at_i[:], scalar=7, op=ALU.arith_shift_right))
            v.tensor_copy(low[:], low_i[:])
            chain(v.tensor_copy(high[:], high_i[:]))

            chain(v.tensor_tensor(
                ge_end[:], consts_at("iota")[:, 0:places].rearrange("p (i o) -> p i o", o=1).to_broadcast([P, places, E]),
                ends[:].rearrange("p (o e) -> p o e", o=1).to_broadcast([P, places, E]), ALU.is_ge))
            chain(v.tensor_reduce(out=expert_f[:], in_=ge_end[:], axis=AX.X, op=ALU.add))
            chain(v.tensor_scalar(expert_of[:], expert_f[:], E - 1.0, None, ALU.min))

            dve.wait_ge(exps_ready, 2)
            chain(v.tensor_reduce(out=total[:], in_=expo[:], axis=AX.X, op=ALU.add))
            chain(v.reciprocal(score[0][:], total[:]))
            chain(v.tensor_tensor(score[1][:], e_gap[:], score[0][:], ALU.mult))
            chain(v.tensor_tensor(den[:], score[0][:], score[1][:], ALU.add))
            chain(v.tensor_scalar(den[:], den[:], 1e-20, None, ALU.add))
            chain(v.reciprocal(rtotal[:], den[:]))
            for k in range(TOPK):
                chain(v.tensor_tensor(weight[:, k, :], score[k][:], rtotal[:], ALU.mult))

            def pair(t, u, wait):
                for k in range(TOPK):
                    if wait is not None:
                        dve.wait_ge(PICKS[f"hot_used{k}"], wait)
                    def at(a):
                        return a[:, k, t:t + 1] if isinstance(t, int) else a[:, k, bass.ds(t, 1)]
                    number = consts_at("numbers")[:, k * tiles:(k + 1) * tiles]
                    number = number[:, t:t + 1] if isinstance(t, int) else number[:, bass.ds(t, 1)]
                    v.tensor_scalar(one_hot[:, u, k, :], iota_bf[:, 0:P], at(low), None, ALU.is_equal)
                    v.tensor_scalar(marked[:, u, k, 0, :], iota_bf[:, 0:places], at(high), number, ALU.is_equal, ALU.mult)
                    v.tensor_scalar(marked[:, u, k, 1, :], iota_bf[:, 0:places], at(high), consts_at("partition"), ALU.is_equal,
                                    ALU.mult).then_inc(hot_ready, 1)

            pair(0, 0, None)
            pair(1, 1, None)
            with dve.Fori(0, tiles // 2 - 1) as i:
                for u in range(2):
                    pair(dve.snap(i * 2 + (2 + u)), u, dve.snap(i * 2 + (1 + u)))

            dve.wait_ge(pairs_done, 1)
            chain(v.tensor_copy(found[:].rearrange("p s i -> p (s i)"), ps_pairs[:, 0:2 * places]))
            v.tensor_scalar(empty[:], found[:, 0, :], 0.0, None, ALU.is_equal)
            chain(v.scalar_tensor_tensor(row[:], found[:, 0, :], float(P), found[:, 1, :], ALU.mult, ALU.add))
            chain(v.tensor_scalar(over[:], row[:], float(P + tokens), -float(tokens), ALU.is_ge, ALU.mult))
            chain(v.scalar_tensor_tensor(over[:], row[:], -float(P), over[:], ALU.add, ALU.add))
            chain(v.tensor_scalar(pairs[:, :, 0], over[:], 0.0, None, ALU.max))
            chain(v.tensor_tensor(empty[:], empty[:], consts_at("spare"), ALU.mult))
            chain(v.tensor_tensor(row[:], row[:], empty[:], ALU.add))
            chain(v.tensor_scalar(pairs[:, :, 1], row[:], -float(P), None, ALU.add))

        @block.tensor
        def _(pe):
            mm = nc.tensor.matmul
            pe.wait_ge(chosen_ready, 1)
            rhs = chosen[:].rearrange("p e t -> p (e t)")
            mm(ps_total[:, 0:E * tiles], ones_bf[:], rhs, start=True, stop=True).then_inc(counted, 1)
            mm(ps_before[:, 0:E * tiles], before_bf[:], rhs, start=True, stop=True).then_inc(counted, 1)

            def pair(u, ready, first=False, last=False):
                for k in range(TOPK):
                    pe.wait_ge(hot_ready, ready[k])
                    ins = mm(ps_pairs[:, 0:2 * places], one_hot[:, u, k, :],
                             marked[:, u, k, :, :].rearrange("p s i -> p (s i)"),
                             start=first and k == 0, stop=last and k == TOPK - 1)
                    ins.then_inc(pairs_done if last and k == TOPK - 1 else PICKS[f"hot_used{k}"], 1)

            pair(0, (1, 2), first=True)
            pair(1, (3, 4))
            with pe.Fori(0, tiles // 2 - 2) as i:
                for u in range(2):
                    pair(u, [pe.snap(i * 4 + (5 + 2 * u + k)) for k in range(TOPK)])
            pair(0, (2 * tiles - 3, 2 * tiles - 2))
            pair(1, (2 * tiles - 1, 2 * tiles), last=True)


def experts(nc, ident, kept, x1_rows, out_rows):
    w1, w3, w2, pairs, expert_of = (kept[k] for k in ("w1", "w3", "w2", "pairs", "expert_of"))
    n = pairs.shape[1]
    RING, IDX = 4, 8
    CHUNKS = [(c, min(P, HIDDEN - c)) for c in range(0, HIDDEN, P)]

    ctx = ExitStack()
    with ctx:
        def sb(name, shape, dt=F32):
            return ctx.enter_context(nc.sbuf_tensor(name, shape, dt))

        def sem(name):
            return ctx.enter_context(nc.semaphore(name))

        idx = sb("idx", [P, IDX, 2], I32)
        xg = sb("xg", [P, RING, D])
        xg_t = sb("xg_t", [P, 2, P])
        act_a = sb("act_a", [P, 2, HIDDEN])
        h = sb("h", [P, 2, len(CHUNKS) * P])
        h_t = sb("h_t", [P, 2, len(CHUNKS) * P])
        rows_out = sb("rows_out", [P, RING, D])
        ps_a = ctx.enter_context(nc.psum_tensor("ps_a", [P, 2, 512], F32))
        ps_b = ctx.enter_context(nc.psum_tensor("ps_b", [P, 2, 512], F32))
        ps_h = ctx.enter_context(nc.psum_tensor("ps_h", [P, 2, 512], F32))
        ps_x = ctx.enter_context(nc.psum_tensor("ps_x", [P, 512], F32))
        ps_y = ctx.enter_context(nc.psum_tensor("ps_y", [P, 512], F32))

        padded = sem("padded")
        idx_ready, x_turned, x_taken, a_done, b_done, a_taken, h_ready, h_turned, h_taken, y_done, y_taken = map(
            sem, ("idx_ready", "x_turned", "x_taken", "a_done", "b_done", "a_taken", "h_ready", "h_turned", "h_taken",
                  "y_done", "y_taken"))
        gathered = [sem(f"gathered{i}") for i in range(RING)]
        scattered = [sem(f"scattered{i}") for i in range(RING)]

        block = ctx.enter_context(nc.Block())
        pace = dict(unroll=IDX, lead=4, tail=2, ahead=4)

        @block.gpsimd
        def _(pool):
            def visit(it):
                if it.has(3):
                    it.wait(idx_ready, 3)
                    it.wait(x_turned, 3 - RING)
                    pool.indirect_dma_start(
                        out=xg[:, it.ring(3, RING), :], out_offset=None, in_=x1_rows,
                        in_offset=bass.IndirectOffsetOnAxis(ap=idx[:, it.ring(3, IDX), 0:1], axis=0),
                    ).then_inc(gathered[it.ring(3, RING)], 16)
                if it.has(-2):
                    it.wait(y_taken, -2)
                    pool.indirect_dma_start(
                        out=out_rows, out_offset=bass.IndirectOffsetOnAxis(ap=idx[:, it.ring(-2, IDX), 1:2], axis=0),
                        in_=rows_out[:, it.ring(-2, RING), :], in_offset=None,
                    ).then_inc(scattered[it.ring(-2, RING)], 16)

            visits(pool, n, visit, **pace)
            for i in range(RING):
                pool.wait_ge(scattered[i], 16 * (n // RING))

        @block.scalar
        def _(act):
            def visit(it):
                if it.has(0):
                    it.wait(a_done, 0)
                    it.wait(h_ready, -2)
                    act.activation(act_a[:, it.ring(0), :], ps_a[:, it.ring(0), 0:HIDDEN], ACT.Silu).then_inc(a_taken, 1)
                if it.has(1):
                    it.wait(x_turned, 1)
                    it.wait(b_done, -1)
                    act.activation(xg_t[:, it.ring(1), :], ps_x[:, 0:P], ACT.Copy).then_inc(x_taken, 1)
                if it.has(-2):
                    it.wait(y_done, -2)
                    it.wait_landed(scattered, -2 - RING)
                    act.activation(rows_out[:, it.ring(-2, RING), :], ps_y[:, 0:D], ACT.Copy).then_inc(y_taken, 1)

            visits(act, n, visit, **pace)

        @block.vector
        def _(dve):
            for u in range(2):
                nc.vector.memset(h[:, u, HIDDEN:], 0.0).then_inc(padded, 1)

            def visit(it):
                if it.has(4):
                    it.wait_landed(scattered, 4 - IDX)
                    nc.vector.tensor_copy(idx[:, it.ring(4, IDX), :].rearrange("p (o s) -> p o s", o=1),
                                          pairs[:, bass.ds(it.index(4), 1), :]).then_inc(idx_ready, 1)
                if it.has(-1):
                    it.wait(h_turned, -1)
                    it.wait(y_done, -3)
                    nc.vector.tensor_copy(h_t[:, it.ring(-1), :], ps_h[:, it.ring(-1), 0:len(CHUNKS) * P]).then_inc(
                        h_taken, 1)
                if it.has(0):
                    it.wait(a_taken, 0)
                    it.wait(b_done, 0)
                    it.wait(h_turned, -2)
                    nc.vector.tensor_tensor(h[:, it.ring(0), 0:HIDDEN], act_a[:, it.ring(0), :],
                                            ps_b[:, it.ring(0), 0:HIDDEN], ALU.mult).then_inc(h_ready, 1)

            visits(dve, n, visit, **pace)

        @block.tensor
        def _(pe):
            mm = nc.tensor.matmul
            pe.wait_ge(padded, 2)

            def visit(it):
                if it.has(0):
                    e = pe.value_load(expert_of[0:1, bass.ds(it.index(0), 1)], min_val=0, max_val=EXPERTS - 1)
                    cols = bass.ds(e * HIDDEN, HIDDEN)
                    it.wait(x_taken, 0)
                    it.wait(a_taken, -2)
                    mm(ps_a[:, it.ring(0), 0:HIDDEN], xg_t[:, it.ring(0), :], w1[:, cols], start=True,
                       stop=True).then_inc(a_done, 1)
                    it.wait(h_ready, -2)
                    mm(ps_b[:, it.ring(0), 0:HIDDEN], xg_t[:, it.ring(0), :], w3[:, cols], start=True,
                       stop=True).then_inc(b_done, 1)
                if it.has(1):
                    it.wait_landed(gathered, 1)
                    it.wait(x_taken, 0)
                    nc.tensor.transpose(ps_x[:, 0:P], xg[:, it.ring(1, RING), :], ident).then_inc(x_turned, 1)
                if it.has(-2):
                    e = pe.value_load(expert_of[0:1, bass.ds(it.index(-2), 1)], min_val=0, max_val=EXPERTS - 1)
                    it.wait(h_taken, -2)
                    it.wait(y_taken, -3)
                    for i, (c, rows) in enumerate(CHUNKS):
                        last = mm(ps_y[:, 0:D], h_t[0:rows, it.ring(-2), c:c + P],
                                  w2[0:rows, bass.ds(e * D + i * EXPERTS * D, D)],
                                  start=(i == 0), stop=(i == len(CHUNKS) - 1))
                    last.then_inc(y_done, 1)
                if it.has(-1):
                    it.wait(h_ready, -1)
                    it.wait(h_taken, -3)
                    for c, _ in CHUNKS:
                        last = nc.tensor.transpose(ps_h[:, it.ring(-1), c:c + P], h[:, it.ring(-1), c:c + P], ident)
                    last.then_inc(h_turned, 1)

            visits(pe, n, visit, **pace)


def combine(nc, kept, picked_rows, out):
    x1, weight = kept["y"], kept["weight"]
    tiles = x1.shape[1]
    C = 4
    n = tiles // C
    x1_flat = x1[:].rearrange("p t d -> p (t d)")
    picked = [picked_rows[k * tiles * P:(k + 1) * tiles * P, :].rearrange("(c t p) d -> c p t d", p=P, t=C)
              for k in range(TOPK)]
    out_v = out.rearrange("(c t p) d -> c p t d", p=P, t=C)

    ctx = ExitStack()
    with ctx:
        def sb(name, shape, dt=F32):
            return ctx.enter_context(nc.sbuf_tensor(name, shape, dt))

        def sem(name):
            return ctx.enter_context(nc.semaphore(name))

        pick = sb("pick", [P, 4, TOPK, C, D])
        z = sb("z", [P, 2, C, D])
        part = sb("part", [P, 2, C, D])
        zn = sb("zn", [P, 2, C, D])
        st = sb("st", [P, 2, C, 6])
        mv2 = sb("mv2", [P, 2, C, 2])
        ve, sd, rs, nm = (sb(k, [P, 2, C]) for k in ("ve", "sd", "rs", "nm"))
        landed = [sem(f"landed{i}") for i in range(4)]
        stored = [sem(f"stored{i}") for i in range(2)]
        first_done, z_done, st_done2, mv_done, ve_done, sd_done, rs_done, nm_done, zn_done = map(
            sem, ("first_done", "z_done", "st_done2", "mv_done", "ve_done", "sd_done", "rs_done", "nm_done", "zn_done"))
        block = ctx.enter_context(nc.Block())
        pace = dict(unroll=4, lead=3, tail=2, ahead=3)

        @block.sync
        def _(sp):
            def visit(it):
                if it.has(3):
                    it.wait(z_done, 3 - 4)
                    for k in range(TOPK):
                        sp.dma_start(pick[:, it.ring(3, 4), k, :, :], picked[k][it.index(3)]).then_inc(
                            landed[it.ring(3, 4)], 16)
                if it.has(-1):
                    it.wait(zn_done, -1)
                    sp.dma_start(out_v[it.index(-1)], zn[:, it.ring(-1), :, :]).then_inc(stored[it.ring(-1)], 16)

            visits(sp, n, visit, **pace)
            for i in range(2):
                sp.wait_ge(stored[i], 16 * (n // 2))

        @block.vector
        def _(dve):
            v = nc.vector

            def visit(it):
                if it.has(0):
                    r = it.ring(0)
                    it.wait_landed(landed, 0, TOPK)
                    for t in range(C):
                        at = it.index(0, C * D) + t * D
                        last = v.scalar_tensor_tensor(part[:, r, t, :], pick[:, it.ring(0, 4), 0, t, :],
                                                      weight[:, 0, bass.ds(it.index(0, C) + t, 1)],
                                                      x1_flat[:, bass.ds(at, D)], ALU.mult, ALU.add)
                    last.then_inc(first_done, 1)
                    it.wait(first_done, 0)
                    it.wait(zn_done, -2)
                    for t in range(C):
                        last = v.scalar_tensor_tensor(z[:, r, t, :], pick[:, it.ring(0, 4), 1, t, :],
                                                      weight[:, 1, bass.ds(it.index(0, C) + t, 1)],
                                                      part[:, r, t, :], ALU.mult, ALU.add)
                    last.then_inc(z_done, 1)
                    it.wait(z_done, 0)
                    for t in range(C):
                        last = v.bn_stats(st[:, r, t, :], z[:, r, t, :])
                    last.then_inc(st_done2, 1)
                    it.wait(st_done2, 0)
                    it.settle()
                    for t in range(C):
                        last = v.bn_aggr(mv2[:, r, t, :], st[:, r, t, :])
                    last.then_inc(mv_done, 1)
                    it.wait(mv_done, 0)
                    v.tensor_scalar(ve[:, r, :], mv2[:, r, :, 1], EPS, None, ALU.add).then_inc(ve_done, 1)
                if it.has(-1):
                    r = it.ring(-1)
                    it.wait(sd_done, -1)
                    v.reciprocal(rs[:, r, :], sd[:, r, :]).then_inc(rs_done, 1)
                    it.wait(rs_done, -1)
                    v.scalar_tensor_tensor(nm[:, r, :], mv2[:, r, :, 0], -1.0, rs[:, r, :], ALU.mult,
                                           ALU.mult).then_inc(nm_done, 1)

            visits(dve, n, visit, **pace)

        @block.scalar
        def _(act):
            def visit(it):
                if it.has(0):
                    it.wait(ve_done, 0)
                    act.activation(sd[:, it.ring(0), :], ve[:, it.ring(0), :], ACT.Sqrt).then_inc(sd_done, 1)
                if it.has(-1):
                    r = it.ring(-1)
                    it.wait(nm_done, -1)
                    it.wait_landed(stored, -3)
                    for t in range(C):
                        last = act.activation(zn[:, r, t, :], z[:, r, t, :], ACT.Identity, scale=rs[:, r, t:t + 1],
                                              bias=nm[:, r, t:t + 1])
                    last.then_inc(zn_done, 1)

            visits(act, n, visit, **pace)


def build(nc, x, xt, wqkv, bqk, bv, wo, bo, wg, sel, consts, w1, w3, w2, out):
    tokens = x.shape[0]
    tiles = tokens // P
    places = -(-(tiles * TOPK + EXPERTS - 1) // 8) * 8
    x1_rows = nc.dram_tensor("x1_rows", (tokens, D), F32).ap()
    picked_rows = nc.dram_tensor("picked_rows", (TOPK * tokens + places * P, D), F32).ap()

    ctx = ExitStack()
    with ctx:
        def sb(name, shape, dt=F32):
            return ctx.enter_context(nc.sbuf_tensor(name, shape, dt))

        cst = sb("cst", [P, consts.shape[1]])
        at = columns(tiles, places)

        def consts_at(name):
            return cst[:, at[name][0]:at[name][1]]

        kept = {
            "y": sb("y_all", [P, tiles, D]), "mv": sb("mv_all", [P, tiles, 2]),
            "logits": sb("logits", [P, tiles, EXPERTS]), "weight": sb("weight", [P, TOPK, tiles]),
            "pairs": sb("pairs", [P, places, 2], I32), "expert_of": sb("expert_of", [P, places], I32),
        }
        attention(nc, x, xt, wqkv, bqk, bv, wo, bo, wg, sel, cst, consts, kept)
        kept.update(w1=sb("w1_sb", [P, EXPERTS * HIDDEN]), w3=sb("w3_sb", [P, EXPERTS * HIDDEN]),
                    w2=sb("w2_sb", [P, -(-HIDDEN // P) * EXPERTS * D]))
        routing(nc, consts_at, w1, w3, w2, kept, x1_rows)
        experts(nc, consts_at("ident"), kept, x1_rows, picked_rows)
        combine(nc, kept, picked_rows, out)


def columns(tiles, places):
    widths = {"ident": P, "mask": P, "shift_rows": 1, "before": P, "iota": max(P, places), "less_8": EXPERTS,
              "numbers": TOPK * tiles, "partition": 1, "spare": places}
    at, out = 0, {}
    for name, width in widths.items():
        out[name] = (at, at + width)
        at += width
    out["end"] = (at, at)
    return out


def table(tiles, places):
    at = columns(tiles, places)
    out = np.zeros((P, at["end"][0]), np.float32)

    def put(name, value):
        out[:, at[name][0]:at[name][1]] = value

    put("ident", np.eye(P))
    put("mask", np.triu(np.full((P, P), MASKED), 1))
    out[SHIFT_ROW:SHIFT_ROW + 2, at["shift_rows"][0]] = 1
    put("before", np.triu(np.ones((P, P)), 1))
    put("iota", np.arange(at["iota"][1] - at["iota"][0]))
    put("less_8", np.arange(EXPERTS) - EXPERTS)
    put("numbers", 1 + np.arange(TOPK * tiles))
    put("partition", np.arange(P)[:, None])
    put("spare", P + TOPK * tiles * P + np.arange(P)[:, None] + P * np.arange(places))
    return out


def layout(inputs):
    def f(a):
        return np.ascontiguousarray(np.asarray(a))

    x = f(inputs["L0_attn_x"]).reshape(-1, D)
    tiles = x.shape[0] // P
    places = -(-(tiles * TOPK + EXPERTS - 1) // 8) * 8
    w = f(inputs["L0_attn_qkv_w"])
    b = f(inputs["L0_attn_qkv_b"])
    return {
        "x": x, "xt": f(x.T), "wqkv": f(w.T), "bqk": f(b[:2 * D].reshape(2, D).T),
        "bv": f(np.broadcast_to(b[2 * D:], (P, D))), "wo": f(np.asarray(inputs["L0_attn_out_w"]).T),
        "bo": f(np.broadcast_to(np.tile(np.asarray(inputs["L0_attn_out_b"]), BLOCKS), (P, BLOCKS * D))),
        "wg": f(np.asarray(inputs["L0_ffn_Wg"]).T), "sel": selectors(), "consts": table(tiles, places),
        "w1": f(np.asarray(inputs["L0_ffn_W1"]).transpose(2, 0, 1).reshape(D, -1)),
        "w3": f(np.asarray(inputs["L0_ffn_W3"]).transpose(2, 0, 1).reshape(D, -1)),
        "w2": f(np.asarray(inputs["L0_ffn_W2"]).transpose(2, 0, 1).reshape(HIDDEN, -1)),
    }


def kernel(**inputs):
    import concourse.bacc as bacc
    from concourse.bass_utils import run_bass_kernel_spmd

    nc = bacc.Bacc("TRN2", target_bir_lowering=False, num_devices=1)
    arrays = layout(inputs)
    shape = np.asarray(inputs["L0_attn_x"]).shape
    args = {name: nc.dram_tensor(name, a.shape, mybir.dt.from_np(a.dtype), kind="ExternalInput").ap()
            for name, a in arrays.items()}
    out = nc.dram_tensor("out", (shape[0] * shape[1], D), F32, kind="ExternalOutput").ap()
    build(nc, out=out, **args)
    got = run_bass_kernel_spmd(nc, [arrays], core_ids=[0])
    return np.asarray(got.results[0]["out"]).reshape(shape)
```

```python
import numpy as np
from contextlib import ExitStack

import concourse.bass as bass
from concourse import mybir

F32 = mybir.dt.float32
F32R = mybir.dt.float32r
BF16 = mybir.dt.bfloat16
I32 = mybir.dt.int32
ALU = mybir.AluOpType
ACT = mybir.ActivationFunctionType
AX = mybir.AxisListType

P = 128
D = 128
L = 256
BLOCKS = L // P
HEADS, HEAD_DIM = 16, 8
GROUP = 4
GROUPS = HEADS // GROUP
QUAD = 32
PARTS = 3
ROWS = PARTS * HEAD_DIM
SHIFT_ROW = ROWS
MASKED = -1.0e30
EXPERTS, TOPK, HIDDEN = 8, 2, 352
TAKEN = -3.0e38
EPS = 1e-5
LAG = 2


def selectors():
    parts = {"qh": (0, 1), "ql": (2,), "kh": (0, 2), "kl": (1,)}
    out = np.zeros((P, GROUPS, len(parts), P), np.float32)
    for g in range(GROUPS):
        for s, rows in enumerate(parts.values()):
            for j in range(GROUP):
                for r in rows:
                    for d in range(HEAD_DIM):
                        out[(g * GROUP + j) * HEAD_DIM + d, g, s, j * QUAD + r * HEAD_DIM + d] = 1
    return out.reshape(P, -1)


class Visit:

    def __init__(self, eng, n, b=None, base=None, u=0):
        self.eng, self.n, self.b, self.base, self.u = eng, n, b, base, u
        self.values = {}
        self.alone = eng.engine in (mybir.EngineType.SP, mybir.EngineType.Pool)

    def ring(self, off, size=2):
        return ((self.b if self.b is not None else self.u) + off) % size

    def has(self, off):
        return self.b is None or 0 <= self.b + off < self.n

    def value(self, scale, plus):
        if (scale, plus) not in self.values:
            self.values[scale, plus] = self.eng.snap(self.base * scale + plus)
        return self.values[scale, plus]

    def index(self, off, scale=1):
        if self.b is not None:
            return (self.b + off) * scale
        return self.value(scale, (self.u + off) * scale)

    def wait(self, sem, off, per=1):
        if self.b is None or 0 <= self.b + off < self.n:
            self.eng.wait_ge(sem, self.index(off + 1, per))
            if self.alone:
                self.settle()

    def settle(self):
        if self.b is None:
            self.eng.nop(nofuse=True)

    def wait_landed(self, sems, off, dmas=1):
        size, per = len(sems), 16 * dmas
        if self.b is None:
            lap = self.value(per // size, ((self.u + off) // size + 1) * per)
            self.eng.wait_ge(sems[self.ring(off, size)], lap)
            if self.alone:
                self.settle()
        elif 0 <= self.b + off < self.n:
            self.eng.wait_ge(sems[self.ring(off, size)], ((self.b + off) // size + 1) * per)


def visits(eng, n, body, unroll, lead, tail, ahead):
    first = -(-tail // unroll) * unroll
    count = max(0, (n - ahead - first) // unroll)
    for b in range(-lead, first):
        body(Visit(eng, n, b=b))
    if count:
        with eng.Fori(0, count) as i:
            base = eng.snap(i * unroll + first)
            values = {}
            for u in range(unroll):
                turn = Visit(eng, n, base=base, u=u)
                turn.values = values
                body(turn)
    for b in range(first + count * unroll, n + tail):
        body(Visit(eng, n, b=b))


TASKS = [
    [[("pack_k0", 1)], [("pack_k1", 1)], [("project", -2)]],
    [[("pack_q0", 1)], [("pack_q1", 1)], [("values", 1), ("heads0", -1)]],
    [[("heads1", -1)], [("split", 2)], [("centred", -2)]],
    [[("mixed", -1)], [], [("router", -2)]],
]
ORDER = [t for step in TASKS for part in step for t in part]
BANK_OF = {t[0]: i % 2 for i, t in enumerate(ORDER)}


def attention(nc, x, xt, wqkv, bqk, bv, wo, bo, wg, sel, cst, consts, kept):
    y_all, mv_all, choice = kept["y"], kept["mv"], kept["choice"]
    tokens = x.shape[0]
    n = tokens // L
    x_v = x.rearrange("(b k p) d -> b p k d", k=BLOCKS, p=P)
    xt_v = xt.rearrange("d (b t) -> b d t", t=L)

    spent = kept["spent"]
    ctx = ExitStack()
    with ctx:
        def sb(name, shape, dt=F32):
            return ctx.enter_context(nc.sbuf_tensor(name, shape, dt))

        def sem(name):
            spent.append(nc.alloc_semaphore(name=name))
            return spent[-1]

        wqkv_sb = sb("wqkv_sb", [P, 3 * D])
        bqk_sb = sb("bqk_sb", [P, 2])
        bv_sb = sb("bv_sb", [P, D])
        wo_sb = sb("wo_sb", [P, D])
        bo_sb = sb("bo_sb", [P, BLOCKS * D])
        wg_sb = sb("wg_sb", [P, EXPERTS])
        sel_f = sb("sel_f", [P, GROUPS * 4 * P])
        sel_r = sb("sel_r", [P, GROUPS, 4, P], F32R)
        ident = cst[:, 0:P]
        ones_rows = cst[:, 2 * P:2 * P + 1]
        less_8 = kept["less_8"]
        ident_bf = sb("ident_bf", [P, P], BF16)
        mask_bf = sb("mask_bf", [P, GROUP, P], BF16)

        x_sb = sb("x_sb", [P, 2, BLOCKS * D])
        xt_sb = sb("xt_sb", [P, 2, L])
        xb = sb("xb", [P, BLOCKS * D])
        split = {k: sb(k, [P, L], F32R) for k in ("qh", "ql", "kh", "kl")}
        q_dense = sb("q_dense", [P, 2, GROUPS, L], F32R)
        k_dense = sb("k_dense", [P, 2, GROUPS, L], F32R)
        q_pad = sb("q_pad", [P, 2, GROUPS, GROUP, L], F32R)
        k_pad = sb("k_pad", [P, 2, GROUPS, GROUP, L], F32R)
        v_ext = sb("v_ext", [P, 2, BLOCKS, HEADS, QUAD])
        neg_max = sb("neg_max", [P, 2, BLOCKS, GROUP])
        shift = sb("shift", [P, 2, 2, GROUP, BLOCKS], F32R)
        shift_t = sb("shift_t", [2 * BLOCKS * GROUP, 2, P], F32R)
        probs = sb("probs", [P, 2, 3 * 512])
        out_t = sb("out_t", [P, 2, GROUPS, L])
        rsum = sb("rsum", [P, 2, HEADS])
        heads = sb("heads", [P, BLOCKS, D])
        heads_t = sb("heads_t", [P, L])
        y = sb("y", [P, BLOCKS, D])
        stats = sb("stats", [P, BLOCKS, 6])
        mv = sb("mv", [P, BLOCKS, 2])
        yc = sb("yc", [P, BLOCKS, D])
        yc_t = sb("yc_t", [P, L])
        chosen = sb("chosen_b", [P, 2, BLOCKS, choice.shape[2]])
        hit = sb("hit_b", [P, 2, BLOCKS, EXPERTS])
        rest = sb("rest_b", [P, BLOCKS, EXPERTS])

        ps_s = ctx.enter_context(nc.psum_tensor("ps_s", [P, 2, 512], F32))
        ps_st = ctx.enter_context(nc.psum_tensor("ps_st", [P, 3, 512], F32))
        ps_o = ctx.enter_context(nc.psum_tensor("ps_o", [P, 512], F32))
        ps_m = ctx.enter_context(nc.psum_tensor("ps_m", [P, 2, 512], F32))

        loaded = sem("loaded")
        consts_ready = sem("consts_ready")
        zeroed = sem("zeroed")
        x_landed, xt_landed, k_pad_landed, q_pad_landed = (
            [sem(f"{name}{i}") for i in range(2)] for name in ("x_landed", "xt_landed", "k_pad_landed", "q_pad_landed"))
        s_done = [[sem(f"s_done{g}{k}") for k in range(3)] for g in range(GROUPS)]
        max_done = [[sem(f"max_done{g}{k}") for k in range(3)] for g in range(GROUPS)]
        shift_hi = [sem(f"shift_hi{g}") for g in range(GROUPS)]
        shift_ready = [sem(f"shift_ready{g}") for g in range(GROUPS)]
        shift_landed = [sem(f"shift_landed{g}") for g in range(GROUPS)]
        st_done = [sem(f"st_done{g}") for g in range(GROUPS)]
        exp_done = [sem(f"exp_done{g}") for g in range(GROUPS)]
        masked = [sem(f"masked{g}") for g in range(GROUPS)]
        pv_done = [sem(f"pv_done{g}") for g in range(GROUPS)]
        out_t_ready = [sem(f"out_t_ready{g}") for g in range(GROUPS)]
        made = {t: sem(f"made_{t}") for t, _ in ORDER}
        shift_made = [sem(f"shift_made{g}") for g in range(GROUPS)]
        shift_taken = [sem(f"shift_taken{g}") for g in range(GROUPS)]
        taken = {t: sem(f"taken_{t}") for t, _ in ORDER}
        high_ready = sem("high_ready")
        rsum_ready = [sem(f"rsum_ready{i}") for i in range(BLOCKS)]
        xb_ready = sem("xb_ready")
        stats_ready, mv_ready, yc_ready, y_kept = map(sem, ("stats_ready", "mv_ready", "yc_ready", "y_kept"))

        CHOICE_STEPS = 10
        pick_marked = sem("pick_marked")
        choice_step = [sem(f"choice_step{i}") for i in range(CHOICE_STEPS)]

        block = ctx.enter_context(nc.Block())

        def scores_group(g):
            return (g + LAG) % GROUPS, (g + LAG) // GROUPS

        def shift_group(g):
            return (g - 1 + LAG) % GROUPS, (g - 1 + LAG) // GROUPS

        def two_before(sem_of, it, h, off):
            it.wait(sem_of[(h + 2) % GROUPS], off if h >= 2 else off - 1)

        def values_group(g):
            return (g - 1) % GROUPS, (g - 1) // GROUPS

        def shift_columns(h):
            return ps_o[0:2 * BLOCKS * GROUP, L + (h % 2) * P:L + (h % 2 + 1) * P]

        S_BANK = [[(3 * g + k) % 2 for k in range(3)] for g in range(GROUPS)]
        N_CONST_LOADS = 8

        @block.sync
        def _(sp):
            for dst, src in ((wqkv_sb[:], wqkv), (bqk_sb[:], bqk), (bv_sb[:], bv), (wo_sb[:], wo), (bo_sb[:], bo),
                             (wg_sb[:], wg), (sel_f[:], sel), (cst[:], consts)):
                sp.dma_start(dst, src).then_inc(loaded, 16)

            def visit(it):
                def load_xt(off):
                    sp.dma_start(xt_sb[:, it.ring(off), :], xt_v[it.index(off)]).then_inc(xt_landed[it.ring(off)], 16)

                if it.b == -2:
                    load_xt(2)
                    load_xt(3)
                for g in range(GROUPS):
                    h, off = shift_group(g)
                    if it.has(off):
                        p = it.ring(off)
                        it.wait(shift_taken[h], off)
                        it.wait(st_done[h], off - 2)
                        sp.dma_start(
                            q_pad[SHIFT_ROW:SHIFT_ROW + 2, p, h, :, :].bitcast(F32).rearrange(
                                "s j (k q) -> s (j k) q", k=BLOCKS),
                            shift_t[:, h % 2, :].bitcast(F32)).then_inc(shift_landed[h], 16)
                    if g == 0 and it.has(1):
                        p = it.ring(1)
                        it.wait(taken["pack_k0"], 1)
                        it.wait(taken["pack_k1"], 1)
                        it.wait(s_done[GROUPS - 1][2], -1)
                        if it.b == -1:
                            sp.wait_ge(zeroed, 1)
                        for j in range(GROUP):
                            r = slice(QUAD * j, QUAD * j + ROWS)
                            sp.dma_start(k_pad[r, p, :, j, :].bitcast(F32), k_dense[r, p, :, :].bitcast(F32)).then_inc(k_pad_landed[p], 16)
                    if g == 1 and it.has(1):
                        p = it.ring(1)
                        it.wait(taken["pack_q0"], 1)
                        it.wait(taken["pack_q1"], 1)
                        it.wait(st_done[GROUPS - 1], -1)
                        if it.b == -1:
                            sp.wait_ge(zeroed, 2)
                        for j in range(GROUP):
                            r = slice(QUAD * j, QUAD * j + ROWS)
                            sp.dma_start(q_pad[r, p, :, j, :].bitcast(F32), q_dense[r, p, :, :].bitcast(F32)).then_inc(q_pad_landed[p], 16)
                    if g == 2 and it.has(3) and not it.b == -2:
                        it.wait(made["values"], 1)
                        load_xt(3)
                    if g == 3 and it.has(0):
                        it.wait(xb_ready, -2)
                        sp.dma_start(x_sb[:, it.ring(0), :].rearrange("p (k d) -> p k d", k=BLOCKS),
                                     x_v[it.index(0)]).then_inc(x_landed[it.ring(0)], 16)
            visits(sp, n, visit, unroll=2, lead=2, tail=3, ahead=3)

        @block.gpsimd
        def _(pool):
            pool.memset(k_pad[:].bitcast(F32), 0.0).then_inc(zeroed, 1)
            pool.memset(q_pad[:].bitcast(F32), 0.0).then_inc(zeroed, 1)
            pool.memset(v_ext[:], 0.0).then_inc(zeroed, 1)
            pool.wait_ge(zeroed, 3)
            pool.memset(v_ext[:, :, :, :, HEAD_DIM:HEAD_DIM + 1], 1.0).then_inc(zeroed, 1)

            def visit(it):
                for g in range(GROUPS):
                    if it.has(0):
                        it.wait(exp_done[g], 0)
                        low = probs[:, g % 2, 0:GROUP * L].rearrange("p (h q) -> p h q", q=L)[:, :, 0:P]
                        high = probs[:, g % 2, GROUP * L:].rearrange("p (h q) -> p h q", q=P)
                        for part in (low, high):
                            last = pool.affine_select(out=part, in_=part, compare_op=ALU.is_ge, fill=0.0, base=0,
                                                      pattern=[[0, GROUP], [1, P]], channel_multiplier=-1)
                        last.then_inc(masked[g], 1)
                    if g == 0 and it.has(-2):
                        it.wait(mv_ready, -2)
                        for k in range(BLOCKS):
                            last = pool.tensor_scalar(yc[:, k, :], y[:, k, :], mv[:, k, 0:1], None, ALU.subtract)
                        last.then_inc(yc_ready, 1)
                        it.wait(yc_ready, -2)
                        pool.tensor_copy(y_all[:].rearrange("p t d -> p (t d)")[
                            :, bass.ds(it.index(-2, BLOCKS * D), BLOCKS * D)],
                            yc[:].rearrange("p k d -> p (k d)"))
                        pool.tensor_copy(mv_all[:].rearrange("p t d -> p (t d)")[
                            :, bass.ds(it.index(-2, BLOCKS * 2), BLOCKS * 2)],
                            mv[:].rearrange("p k d -> p (k d)")).then_inc(y_kept, 1)
                    if g == 1 and it.has(-1):
                        it.wait_landed(x_landed, -1)
                        it.wait(taken["project"], -2)
                        pool.tensor_tensor(xb[:], x_sb[:, it.ring(-1), :], bo_sb[:], ALU.add).then_inc(xb_ready, 1)

            pool.wait_ge(loaded, 16 * N_CONST_LOADS)
            visits(pool, n, visit, unroll=2, lead=2, tail=3, ahead=3)

        @block.scalar
        def _(act):
            act.wait_ge(loaded, 16 * N_CONST_LOADS)

            def copy_out(it, task, off, dst, src, bias=None):
                it.wait(made[task], off)
                if bias is None:
                    act.activation(dst, src, ACT.Copy).then_inc(taken[task], 1)
                else:
                    act.activation(dst, src, ACT.Identity, bias=bias).then_inc(taken[task], 1)

            def task(it, name, off):
                p = it.ring(off)
                bank = ps_m[:, BANK_OF[name], :]
                if name in ("pack_k0", "pack_k1"):
                    h = 2 * int(name[-1])
                    it.wait_landed(k_pad_landed, off - 2, GROUP)
                    it.wait(st_done[GROUPS - 1], off - 2)
                    copy_out(it, name, off, k_dense[:, p, h:h + 2, :].rearrange("p g t -> p (g t)"), bank, ones_rows)
                if name in ("pack_q0", "pack_q1"):
                    h = 2 * int(name[-1])
                    it.wait_landed(q_pad_landed, off - 2, GROUP)
                    it.wait(s_done[GROUPS - 1][2], off - 2)
                    copy_out(it, name, off, q_dense[:, p, h:h + 2, :].rearrange("p g t -> p (g t)"), bank)
                if name == "split":
                    it.wait(made["split"], off)
                    it.wait(made["pack_q1"], off - 1)
                    act.activation(split["qh"][:], bank[:, 0:L], ACT.Identity, bias=bqk_sb[:, 0:1])
                    act.activation(split["kh"][:], bank[:, L:2 * L], ACT.Identity,
                                   bias=bqk_sb[:, 1:2]).then_inc(high_ready, 1)
                if name == "mixed":
                    it.wait(made["project"], off - 1)
                    copy_out(it, name, off, heads_t[:], bank[:, 0:L])
                if name == "centred":
                    it.wait(made["router"], off - 1)
                    copy_out(it, name, off, yc_t[:], bank[:, 0:L])
                if name == "router":
                    it.wait(choice_step[-1], off - 2)
                    copy_out(it, name, off, chosen[:, p, :, 0:EXPERTS],
                             bank[:, 0:EXPERTS * BLOCKS].rearrange("p (k e) -> p k e", e=EXPERTS))

            def take_shift(it, h, off):
                it.wait(shift_made[h], off)
                it.wait(shift_landed[(h + 2) % GROUPS], off if h >= 2 else off - 1, 16)
                act.activation(shift_t[:, h % 2, :], shift_columns(h), ACT.Copy).then_inc(shift_taken[h], 1)

            def visit(it):
                for g in range(GROUPS):
                    h, off = shift_group(g)
                    if it.has(off):
                        take_shift(it, h, off)
                    if it.has(0):
                        it.wait(st_done[g], 0)
                        it.wait(pv_done[(g + 2) % GROUPS], 0 if g >= 2 else -1)
                        act.activation(probs[:, g % 2, :], ps_st[:].rearrange("p k f -> p (k f)"), ACT.Exp,
                                       scale=float(HEAD_DIM) ** -0.5).then_inc(exp_done[g], 1)
                    for name, off in TASKS[g][0] + TASKS[g][1]:
                        if it.has(off):
                            task(it, name, off)
                    h, off = values_group(g)
                    if it.has(off):
                        p = it.ring(off)
                        it.wait(pv_done[h], off)
                        it.wait(made["heads1"], off - 2)
                        act.activation(out_t[:, p, h, :], ps_o[:, 0:L], ACT.Copy).then_inc(out_t_ready[h], 1)
                    for name, off in TASKS[g][2]:
                        if it.has(off):
                            task(it, name, off)
            visits(act, n, visit, unroll=2, lead=2, tail=3, ahead=3)

        @block.vector
        def _(dve):
            dve.wait_ge(loaded, 16 * N_CONST_LOADS)
            nc.vector.tensor_copy(sel_r[:].rearrange("p g s m -> p (g s m)"), sel_f[:]).then_inc(consts_ready, 1)
            nc.vector.tensor_copy(ident_bf[:], ident).then_inc(consts_ready, 1)
            for j in range(GROUP):
                nc.vector.tensor_copy(mask_bf[:, j, :], cst[:, P:2 * P]).then_inc(consts_ready, 1)

            def task(it, name, off):
                p = it.ring(off)
                bank = ps_m[:, BANK_OF[name], :]
                if name == "split":
                    it.wait(high_ready, off)
                    nc.vector.scalar_tensor_tensor(split["ql"][:], bank[:, 0:L], bqk_sb[:, 0:1],
                                                   split["qh"][:].bitcast(F32), ALU.add, ALU.subtract)
                    nc.vector.scalar_tensor_tensor(split["kl"][:], bank[:, L:2 * L], bqk_sb[:, 1:2],
                                                   split["kh"][:].bitcast(F32), ALU.add,
                                                   ALU.subtract).then_inc(taken[name], 1)
                if name == "values":
                    it.wait(made[name], off)
                    it.wait(pv_done[GROUPS - 1], off - 2)
                    if it.b is not None and it.b + off < 2:
                        dve.wait_ge(zeroed, 4)
                    for k in range(BLOCKS):
                        last = nc.vector.tensor_tensor(
                            v_ext[:, p, k, :, 0:HEAD_DIM],
                            bank[:, k * D:(k + 1) * D].rearrange("p (h d) -> p h d", d=HEAD_DIM),
                            bv_sb[:].rearrange("p (h d) -> p h d", d=HEAD_DIM), ALU.add)
                    last.then_inc(taken[name], 1)
                if name in ("heads0", "heads1"):
                    k = int(name[-1])
                    it.wait(made[name], off)
                    v = bank.rearrange("p (h d) -> p h d", d=QUAD)
                    nc.vector.reciprocal(rsum[:, k, :].rearrange("p (h o) -> p h o", o=1),
                                         v[:, :, HEAD_DIM:HEAD_DIM + 1]).then_inc(rsum_ready[k], 1)
                    it.wait(rsum_ready[k], off)
                    it.wait(made["mixed"], off - 1)
                    nc.vector.tensor_tensor(
                        heads[:, k, :].rearrange("p (h d) -> p h d", d=HEAD_DIM), v[:, :, 0:HEAD_DIM],
                        rsum[:, k, :].rearrange("p (h o) -> p h o", o=1).to_broadcast([P, HEADS, HEAD_DIM]),
                        ALU.mult).then_inc(taken[name], 1)
                if name == "project":
                    it.wait(made[name], off)
                    it.wait(xb_ready, off)
                    it.wait(y_kept, off - 1)
                    nc.vector.tensor_tensor(y[:].rearrange("p k d -> p (k d)"), bank[:, 0:BLOCKS * D], xb[:],
                                            ALU.add).then_inc(taken[name], 1)
                    it.wait(taken[name], off)
                    for k in range(BLOCKS):
                        last = nc.vector.bn_stats(stats[:, k, :], y[:, k, :])
                    last.then_inc(stats_ready, 1)
                    it.wait(stats_ready, off)
                    it.settle()
                    for k in range(BLOCKS):
                        last = nc.vector.bn_aggr(mv[:, k, :], stats[:, k, :])
                    last.then_inc(mv_ready, 1)

            numbers = less_8.rearrange("p (o e) -> p o e", o=1).to_broadcast([P, BLOCKS, EXPERTS])

            def choose(it, step):
                off = -3
                if not it.has(off) or step >= CHOICE_STEPS:
                    return
                v, p = nc.vector, it.ring(off)
                lg = chosen[:, p, :, 0:EXPERTS]
                k, what = divmod(step, 5) if step < CHOICE_STEPS - 1 else (None, None)
                it.wait(choice_step[step - 1] if step else taken["router"], off)

                def column(c):
                    return chosen[:, p, :, EXPERTS + c:EXPERTS + c + 1]

                def over_experts(a):
                    return a.to_broadcast([P, BLOCKS, EXPERTS])

                cur = rest[:] if k == 1 else lg
                if k is None:
                    last = v.tensor_copy(choice[:].rearrange("p t c -> p (t c)")[
                        :, bass.ds(it.index(off, BLOCKS * choice.shape[2]), BLOCKS * choice.shape[2])],
                        chosen[:, p, :, :].rearrange("p k c -> p (k c)"))
                elif what == 0:
                    last = v.tensor_reduce(out=column(k), in_=cur, axis=AX.X, op=ALU.max)
                elif what == 1:
                    last = v.tensor_tensor(hit[:, 0, :, :], cur, over_experts(column(k)), ALU.is_equal)
                elif what == 2:
                    last = v.tensor_tensor(hit[:, 1, :, :], hit[:, 0, :, :], numbers, ALU.mult)
                elif what == 3:
                    last = v.tensor_reduce(out=column(2 + k), in_=hit[:, 1, :, :], axis=AX.X, op=ALU.min)
                elif k == 0:
                    v.tensor_tensor(hit[:, 0, :, :], numbers, over_experts(column(2)), ALU.is_equal).then_inc(
                        pick_marked, 1)
                    it.wait(pick_marked, off)
                    last = v.scalar_tensor_tensor(rest[:], hit[:, 0, :, :], TAKEN, lg, ALU.mult, ALU.add)
                last.then_inc(choice_step[step], 1)

            def visit(it):
                for g in range(GROUPS):
                    h, off = scores_group(g)
                    for k in range(3):
                        choose(it, 3 * g + k)
                        if it.has(off):
                            it.wait(s_done[h][k], off)
                            bank = ps_s[:, S_BANK[h][k], :]
                            src = bank.rearrange("p (h t) -> p h t", t=P if k == 0 else L)
                            dst = neg_max[:, h % 2, 0, :] if k == 0 else neg_max[:, h % 2, 1, 2 * k - 2:2 * k]
                            nc.vector.tensor_reduce(out=dst, in_=src, axis=AX.X, op=ALU.max,
                                                    negate=True).then_inc(max_done[h][k], 1)
                    if it.has(off):
                        two_before(shift_made, it, h, off)
                        it.wait(max_done[h][2], off)
                        m = neg_max[:, h % 2, :, :].rearrange("p k j -> p j k")
                        nc.vector.tensor_copy(shift[:, h % 2, 0, :, :], m).then_inc(shift_hi[h], 1)
                        it.wait(shift_hi[h], off)
                        nc.vector.tensor_tensor(shift[:, h % 2, 1, :, :], m, shift[:, h % 2, 0, :, :].bitcast(F32),
                                                ALU.subtract).then_inc(shift_ready[h], 1)
                    for name, off in TASKS[g][0] + TASKS[g][1] + TASKS[g][2]:
                        if it.has(off) and name in ("split", "values", "heads0", "heads1", "project"):
                            task(it, name, off)

            visits(dve, n, visit, unroll=2, lead=2, tail=3, ahead=3)

        @block.tensor
        def _(pe):
            pe.wait_ge(loaded, 16 * N_CONST_LOADS)
            pe.wait_ge(consts_ready, 2 + GROUP)
            mm = nc.tensor.matmul

            def task(it, name, off):
                p = it.ring(off)
                bank = ps_m[:, BANK_OF[name], :]
                at = ORDER.index((name, off))
                if it.b is None:
                    before, boff = ORDER[(at - 2) % len(ORDER)]
                    it.wait(taken[before], boff if at >= 2 else boff - 1)
                else:
                    found = False
                    for back in range(2, 4 * len(ORDER), 2):
                        before, boff = ORDER[(at - back) % len(ORDER)]
                        boff += (at - back) // len(ORDER)
                        if not found and it.has(boff):
                            it.wait(taken[before], boff)
                            found = True
                if name == "split":
                    it.wait_landed(xt_landed, off)
                    for i in range(2):
                        last = mm(bank[:, i * L:(i + 1) * L], wqkv_sb[:, i * D:(i + 1) * D], xt_sb[:, p, :],
                                  start=True, stop=True)
                if name == "values":
                    for k in range(BLOCKS):
                        last = mm(bank[:, k * D:(k + 1) * D], xt_sb[:, p, k * P:(k + 1) * P], wqkv_sb[:, 2 * D:],
                                  start=True, stop=True)
                if name.startswith("pack"):
                    it.wait(taken["split"], off)
                    hi, lo, s = ("kh", "kl", 2) if "k" in name[5:] else ("qh", "ql", 0)
                    for i in range(2):
                        g = 2 * int(name[-1]) + i
                        mm(bank[:, i * L:(i + 1) * L], sel_r[:, g, s, :], split[hi][:], start=True, stop=False)
                        last = mm(bank[:, i * L:(i + 1) * L], sel_r[:, g, s + 1, :], split[lo][:], start=False,
                                  stop=True)
                if name in ("heads0", "heads1"):
                    k = int(name[-1])
                    it.wait(out_t_ready[GROUPS - 1], off)
                    for g in range(GROUPS):
                        last = nc.tensor.transpose(bank[:, g * P:(g + 1) * P], out_t[:, p, g, k * P:(k + 1) * P], ident)
                if name == "mixed":
                    it.wait(taken["heads0"], off)
                    it.wait(taken["heads1"], off)
                    for k in range(BLOCKS):
                        last = nc.tensor.transpose(bank[:, k * P:(k + 1) * P], heads[:, k, :], ident)
                if name == "project":
                    it.wait(taken["mixed"], off)
                    for k in range(BLOCKS):
                        last = mm(bank[:, k * D:(k + 1) * D], heads_t[:, k * P:(k + 1) * P], wo_sb[:], start=True,
                                  stop=True)
                if name == "centred":
                    it.wait(yc_ready, off)
                    for k in range(BLOCKS):
                        last = nc.tensor.transpose(bank[:, k * P:(k + 1) * P], yc[:, k, :], ident)
                if name == "router":
                    it.wait(taken["centred"], off)
                    for k in range(BLOCKS):
                        last = mm(bank[:, EXPERTS * k:EXPERTS * (k + 1)], yc_t[:, k * P:(k + 1) * P], wg_sb[:], start=True, stop=True)
                last.then_inc(made[name], 1)

            def turn_shift(it, g, h, off):
                it.wait(shift_ready[h], off)
                it.wait(out_t_ready[(g - 2) % GROUPS], (g - 2) // GROUPS)
                if not it.has((g - 2) // GROUPS):
                    before, boff = shift_group(g - 1)
                    it.wait(shift_taken[before], boff)
                nc.tensor.transpose(shift_columns(h), shift[:, h % 2, :, :, :].rearrange("p s j k -> p (s j k)").bitcast(F32),
                                    ident).then_inc(shift_made[h], 1)

            def scores(it, h, off, k):
                p = it.ring(off)
                if k == 0:
                    if h == 0:
                        it.wait_landed(k_pad_landed, off, GROUP)
                        it.wait(taken["pack_q0"], off)
                    if h == 2:
                        it.wait(taken["pack_q1"], off)
                back = 3 * h + k - 2
                it.wait(max_done[(back // 3) % GROUPS][back % 3], off if back >= 0 else off - 1)
                bank = ps_s[:, S_BANK[h][k], :]
                if k == 0:
                    mm(bank, q_dense[:, p, h, 0:P], k_pad[:, p, h, :, 0:P], start=True, stop=False)
                    last = mm(bank, ident_bf[:], mask_bf[:], start=False, stop=True)
                else:
                    mm(bank, q_dense[:, p, h, P:L], k_pad[:, p, h, 2 * k - 2:2 * k, :], start=True, stop=False)
                    last = mm(bank.rearrange("p (j t) -> p j t", t=L)[:, :, P:L], ident_bf[:], mask_bf[:, 0:2, :],
                              start=False, stop=True)
                last.then_inc(s_done[h][k], 1)

            def products(it, g):
                p = it.ring(0)
                if g == 0:
                    it.wait_landed(q_pad_landed, 0, GROUP)
                it.wait(shift_landed[g], 0, 16)
                it.wait(exp_done[g - 1], 0 if g else -1)
                for i in range(2):
                    mm(ps_st[:, i, :], k_dense[:, p, g, 0:P], q_pad[:, p, g, 2 * i:2 * i + 2, :], start=True, stop=True)
                mm(ps_st[:, 2, :], k_dense[:, p, g, P:L], q_pad[:, p, g, :, P:L], start=True,
                   stop=True).then_inc(st_done[g], 1)

            def weighted(it, g, h, off):
                p = it.ring(off)
                it.wait(masked[h], off)
                if h == 0:
                    it.wait(taken["values"], off)
                it.wait(out_t_ready[h - 1], off if h else off - 1)
                sh, soff = shift_group(g)
                it.wait(shift_taken[sh], soff)
                for k in range(BLOCKS):
                    for j in range(GROUP):
                        cols = slice(j * L, (j + 1) * L) if k == 0 else slice(GROUP * L + j * P, GROUP * L + (j + 1) * P)
                        last = mm(ps_o[QUAD * j:QUAD * (j + 1), k * P:L], v_ext[:, p, k, h * GROUP + j, :],
                                  probs[:, h % 2, cols], start=(k == 0), stop=(k == BLOCKS - 1))
                last.then_inc(pv_done[h], 1)

            def tasks(it, g, part):
                for name, off in TASKS[g][part]:
                    if it.has(off):
                        task(it, name, off)

            def visit(it):
                for g in range(GROUPS):
                    h, off = scores_group(g)
                    if it.has(off):
                        scores(it, h, off, 0)
                        scores(it, h, off, 1)
                    sh, soff = shift_group(g)
                    if it.has(soff):
                        turn_shift(it, g, sh, soff)
                    if it.has(0):
                        products(it, g)
                    tasks(it, g, 0)
                    if it.has(off):
                        scores(it, h, off, 2)
                    tasks(it, g, 1)
                    vh, voff = values_group(g)
                    if it.has(voff):
                        weighted(it, g, vh, voff)
                    tasks(it, g, 2)

            visits(pe, n, visit, unroll=2, lead=2, tail=3, ahead=3)


def routing(nc, consts_at, w1, w3, w2, kept, x1_rows):
    y_all, mv_all, choice = kept["y"], kept["mv"], kept["choice"]
    weight, pairs, expert_of = kept["weight"], kept["pairs"], kept["expert_of"]
    tiles = choice.shape[1]
    places = pairs.shape[1]
    tokens = tiles * P
    E = EXPERTS
    STORE = 8
    TURN = 4
    turns = tiles // TURN
    HALF = TURN // 2 * TOPK

    ctx = ExitStack()
    with ctx:
        def sb(name, shape, dt=F32):
            return ctx.enter_context(nc.sbuf_tensor(name, shape, dt))

        def sem(name):
            return ctx.enter_context(nc.semaphore(name))

        std, rstd = (sb(k, [P, tiles]) for k in ("std", "rstd"))
        hit, diff, expo = (sb(k, [P, tiles, E]) for k in ("hit", "diff", "expo"))
        oh = [sb(f"oh{k}", [P, tiles, E]) for k in range(TOPK)]
        gap, e_gap, total, rtotal, den = (sb(k, [P, tiles]) for k in ("gap", "e_gap", "total", "rtotal", "den"))
        score = [sb(f"score{k}", [P, tiles]) for k in range(TOPK)]
        chosen = sb("chosen", [P, E, tiles], BF16)
        ones_bf = sb("ones_bf", [P, P], BF16)
        before_bf = sb("before_bf", [P, P], BF16)
        ones = sb("ones", [P, tiles])
        prior = sb("prior", [P, E, tiles])
        place = sb("place", [P, E, tiles])
        count, needed, ends, starts = (sb(k, [P, E]) for k in ("count", "needed", "ends", "starts"))
        needed_i = sb("needed_i", [P, E], I32)
        at_place = sb("at_place", [P, tiles, TOPK])
        at_i, low_i, high_i = (sb(k, [P, tiles, TOPK], I32) for k in ("at_i", "low_i", "high_i"))
        low = sb("low", [P, tiles * TOPK])
        high = sb("high", [P, 2, tiles * TOPK])
        ge_end = sb("ge_end", [P, places, E])
        expert_f = sb("expert_f", [P, places])
        high_turn = sb("high_turn", [P, 2, 2, TURN * TOPK])
        distance = sb("distance", [P, 2, HALF * P])
        square = sb("square", [P, 2, HALF * P])
        one_hot = sb("one_hot", [P, 2, 2, HALF, P])
        marked = sb("marked", [P, 2, TURN * TOPK, places])
        found, empty, row, over = (sb(k, [P, places]) for k in ("found", "empty", "row", "over"))
        w_raw = [sb(f"w{k}_raw", w1.shape) for k in (1, 3)]

        ps_before = ctx.enter_context(nc.psum_tensor("ps_before", [P, 512], F32))
        ps_total = ctx.enter_context(nc.psum_tensor("ps_total", [P, 512], F32))
        ps_pairs = ctx.enter_context(nc.psum_tensor("ps_pairs", [P, 512], F32))

        step = sem("step")
        ones_ready, picks_marked, std_ready, rstd_ready, gaps_ready, exps_ready = map(
            sem, ("ones_ready", "picks_marked", "std_ready", "rstd_ready", "gaps_ready", "exps_ready"))
        chosen_ready, counted, low_ready, high_ready, pairs_done = map(
            sem, ("chosen_ready", "counted", "low_ready", "high_ready_r", "pairs_done"))
        copied, distance_ready, squared, hot_by_act, hot_by_dve, marked_ready, hot_used = map(
            sem, ("copied", "distance_ready", "squared", "hot_by_act", "hot_by_dve", "marked_ready", "hot_used"))
        scaled, x1_stored, w2_landed, high_done = map(sem, ("scaled", "x1_stored", "w2_landed", "high_done"))
        raw_landed = [sem(f"raw_landed{k}") for k in (1, 3)]

        block = ctx.enter_context(nc.Block())
        pace = dict(unroll=2, lead=1, tail=2, ahead=1)

        @block.sync
        def _(sp):
            for raw, w, landed in zip(w_raw, (w1, w3), raw_landed):
                sp.dma_start(raw[:], w).then_inc(landed, 16)
            for i, c in enumerate(range(0, HIDDEN, P)):
                n = min(P, HIDDEN - c)
                sp.dma_start(kept["w2"][0:n, i * EXPERTS * D:(i + 1) * EXPERTS * D], w2[c:c + n, :]).then_inc(
                    w2_landed, 16)
            rows = x1_rows.rearrange("(c t p) d -> c p t d", p=P, t=STORE)
            with sp.Fori(0, tiles // STORE) as c:
                ready, landed = sp.snap(c * (STORE // TURN) + STORE // TURN), sp.snap(c * 16 + 16)
                sp.wait_ge(scaled, ready)
                sp.dma_start(rows[c], y_all[:].rearrange("p (c t) d -> p c t d", t=STORE)[:, c, :, :]).then_inc(
                    x1_stored, 16)
                sp.wait_ge(x1_stored, landed)
                sp.nop(nofuse=True)
            sp.wait_ge(w2_landed, 16 * -(-HIDDEN // P))

        @block.gpsimd
        def _(pool):
            pool.memset(ones_bf[:], 1.0).then_inc(ones_ready, 1)
            pool.tensor_copy(before_bf[:], consts_at("before")).then_inc(ones_ready, 1)
            pool.memset(ones[:], 1.0).then_inc(ones_ready, 1)
            pool.tensor_copy(high[:, 1, :], consts_at("numbers")).then_inc(high_ready, 1)
            nc.clear_and_free_semaphores(kept["spent"])
            pool.wait_ge(low_ready, 1)
            pool.wait_ge(high_ready, 2)

            def visit(it):
                if it.has(1):
                    r = it.ring(1)
                    it.wait(marked_ready, -1)
                    pool.tensor_copy(high_turn[:, r, :, :],
                                     high[:, :, bass.ds(it.index(1, TURN * TOPK), TURN * TOPK)]).then_inc(copied, 1)
                    it.wait(squared, -1)
                    pool.tensor_tensor(
                        distance[:, r, :].rearrange("p (j q) -> p j q", q=P),
                        consts_at("iota")[:, 0:P].rearrange("p (o q) -> p o q", o=1).to_broadcast([P, HALF, P]),
                        low[:, bass.ds(it.index(1, TURN * TOPK), HALF)].rearrange(
                            "p (j o) -> p j o", o=1).to_broadcast([P, HALF, P]), ALU.subtract).then_inc(distance_ready, 1)

            visits(pool, turns, visit, **pace)
            for i, (raw, high_part, low_part) in enumerate(zip(w_raw, kept["w_high"], kept["w_low"])):
                pool.wait_ge(high_done, i + 1)
                pool.tensor_tensor(low_part[:], raw[:], high_part[:].bitcast(F32), ALU.subtract)

        @block.scalar
        def _(act):
            act.activation(std[:], mv_all[:, :, 1], ACT.Sqrt, bias=consts_at("eps")).then_inc(std_ready, 1)
            act.wait_ge(gaps_ready, 1)
            act.activation(expo[:].rearrange("p t e -> p (t e)"), diff[:].rearrange("p t e -> p (t e)"),
                           ACT.Exp).then_inc(exps_ready, 1)
            act.activation(e_gap[:], gap[:], ACT.Exp).then_inc(exps_ready, 1)
            y_flat = y_all[:].rearrange("p t d -> p (t d)")
            for raw, high_part, landed in zip(w_raw, kept["w_high"], raw_landed):
                act.wait_ge(landed, 16)
                act.activation(high_part[:], raw[:], ACT.Copy).then_inc(high_done, 1)

            def visit(it):
                if it.has(0):
                    for t in range(TURN):
                        rows = y_flat[:, t * D:][:, bass.ds(it.index(0, TURN * D), D)]
                        last = act.activation(rows, rows, ACT.Identity,
                                              scale=rstd[:, t:][:, bass.ds(it.index(0, TURN), 1)])
                    last.then_inc(scaled, 1)
                    r = it.ring(0)
                    it.wait(distance_ready, 0)
                    act.activation(square[:, r, :], distance[:, r, :], ACT.Square).then_inc(squared, 1)
                    it.wait(squared, 0)
                    it.wait(hot_used, -2)
                    act.activation(one_hot[:, r, 0, :, :].rearrange("p j q -> p (j q)"), square[:, r, :], ACT.Relu,
                                   scale=-1.0, bias=1.0).then_inc(hot_by_act, 1)

            visits(act, turns, visit, **pace)

        @block.vector
        def _(dve):
            v = nc.vector
            done = [0]

            def chain(instruction):
                done[0] += 1
                instruction.then_inc(step, 1)
                dve.wait_ge(step, done[0])

            def over_experts(a):
                return a.to_broadcast([P, tiles, E])

            def column(c):
                return choice[:, :, E + c:E + c + 1]

            def spread(a):
                return a.rearrange("p (t o) -> p t o", o=1).to_broadcast([P, tiles, E])

            numbers = consts_at("less_8").rearrange("p (o e) -> p o e", o=1).to_broadcast([P, tiles, E])
            for k in range(TOPK):
                v.tensor_tensor(oh[k][:], numbers, over_experts(column(TOPK + k)), ALU.is_equal).then_inc(picks_marked, 1)
            dve.wait_ge(picks_marked, TOPK)
            v.tensor_tensor(chosen[:].rearrange("p e t -> p t e"), oh[0][:], oh[1][:], ALU.add).then_inc(chosen_ready, 1)
            dve.wait_ge(std_ready, 1)
            v.reciprocal(rstd[:], std[:]).then_inc(rstd_ready, 1)
            v.tensor_tensor(diff[:], choice[:, :, 0:E], over_experts(column(0)), ALU.subtract)
            chain(v.tensor_tensor(gap[:].rearrange("p (t o) -> p t o", o=1), column(1), column(0), ALU.subtract))
            dve.wait_ge(rstd_ready, 1)
            v.tensor_tensor(gap[:], gap[:], rstd[:], ALU.mult)
            v.tensor_tensor(diff[:], diff[:], spread(rstd[:]), ALU.mult).then_inc(gaps_ready, 1)

            dve.wait_ge(counted, 2)
            dve.wait_ge(ones_ready, 3)
            in_tile = ps_total[:, 0:E * tiles].rearrange("p (e t) -> p e t", t=tiles)
            chain(v.tensor_reduce(out=count[:], in_=in_tile, axis=AX.X, op=ALU.add))
            chain(v.tensor_scalar(needed_i[:], count[:], 1.0 / P, (P - 1.0) / (2 * P), ALU.mult, ALU.add))
            chain(v.tensor_copy(needed[:], needed_i[:]))
            chain(v.tensor_tensor_scan(ends[:], ones[:, 0:E], needed[:], 0.0, ALU.mult, ALU.add))
            chain(v.tensor_tensor(starts[:], ends[:], needed[:], ALU.subtract))
            chain(v.tensor_scalar(starts[:], starts[:], float(P), None, ALU.mult))
            for e in range(E):
                last = v.tensor_tensor_scan(prior[:, e, :], ones[:], in_tile[:, e, :], starts[:, e:e + 1],
                                            ALU.mult, ALU.add)
            chain(last)
            flat = "p e t -> p (e t)"
            chain(v.tensor_tensor(place[:].rearrange(flat), prior[:].rearrange(flat), ps_before[:, 0:E * tiles], ALU.add))
            for k in range(TOPK):
                chain(v.tensor_tensor(hit[:], oh[k][:], place[:].rearrange("p e t -> p t e"), ALU.mult))
                chain(v.tensor_reduce(out=at_place[:, :, k], in_=hit[:], axis=AX.X, op=ALU.add))
            chain(v.tensor_copy(at_i[:], at_place[:]))
            v.tensor_single_scalar(out=low_i[:], in_=at_i[:], scalar=P - 1, op=ALU.bitwise_and)
            chain(v.tensor_single_scalar(out=high_i[:], in_=at_i[:], scalar=7, op=ALU.arith_shift_right))
            v.tensor_copy(low[:], low_i[:].rearrange("p t k -> p (t k)")).then_inc(low_ready, 1)
            v.tensor_copy(high[:, 0, :], high_i[:].rearrange("p t k -> p (t k)")).then_inc(high_ready, 1)
            dve.wait_ge(low_ready, 1)

            def visit(it):
                if it.has(0):
                    r = it.ring(0)
                    it.wait(hot_used, -2)
                    v.tensor_tensor(
                        one_hot[:, r, 1, :, :],
                        consts_at("iota")[:, 0:P].rearrange("p (o q) -> p o q", o=1).to_broadcast([P, HALF, P]),
                        low[:, HALF:][:, bass.ds(it.index(0, TURN * TOPK), HALF)].rearrange(
                            "p (j o) -> p j o", o=1).to_broadcast([P, HALF, P]), ALU.is_equal).then_inc(hot_by_dve, 1)
                    it.wait(copied, 0)
                    for j in range(TURN * TOPK):
                        last = v.tensor_scalar(marked[:, r, j, :], consts_at("iota")[:, 0:places],
                                               high_turn[:, r, 0, j:j + 1], high_turn[:, r, 1, j:j + 1],
                                               ALU.is_equal, ALU.mult)
                    last.then_inc(marked_ready, 1)

            visits(dve, turns, visit, **pace)

            chain(v.tensor_tensor(
                ge_end[:], consts_at("iota")[:, 0:places].rearrange("p (i o) -> p i o", o=1).to_broadcast([P, places, E]),
                ends[:].rearrange("p (o e) -> p o e", o=1).to_broadcast([P, places, E]), ALU.is_ge))
            chain(v.tensor_reduce(out=expert_f[:], in_=ge_end[:], axis=AX.X, op=ALU.add))
            v.tensor_scalar(expert_of[:], expert_f[:], E - 1.0, None, ALU.min)

            dve.wait_ge(exps_ready, 2)
            chain(v.tensor_reduce(out=total[:], in_=expo[:], axis=AX.X, op=ALU.add))
            chain(v.reciprocal(score[0][:], total[:]))
            chain(v.tensor_tensor(score[1][:], e_gap[:], score[0][:], ALU.mult))
            chain(v.tensor_tensor(den[:], score[0][:], score[1][:], ALU.add))
            chain(v.tensor_scalar(den[:], den[:], 1e-20, None, ALU.add))
            chain(v.reciprocal(rtotal[:], den[:]))
            for k in range(TOPK):
                v.tensor_tensor(weight[:, k, :], score[k][:], rtotal[:], ALU.mult)

            dve.wait_ge(pairs_done, 1)
            chain(v.tensor_copy(found[:], ps_pairs[:, 0:places]))
            v.tensor_scalar(empty[:], found[:], 0.0, None, ALU.is_equal)
            chain(v.tensor_scalar(over[:], found[:], float(P + tokens), -float(tokens), ALU.is_ge, ALU.mult))
            chain(v.scalar_tensor_tensor(over[:], found[:], -float(P), over[:], ALU.add, ALU.add))
            v.tensor_scalar(pairs[:, :, 0], over[:], 0.0, None, ALU.max)
            chain(v.tensor_tensor(empty[:], empty[:], consts_at("spare"), ALU.mult))
            chain(v.tensor_tensor(row[:], found[:], empty[:], ALU.add))
            v.tensor_scalar(pairs[:, :, 1], row[:], -float(P), None, ALU.add)

        @block.tensor
        def _(pe):
            mm = nc.tensor.matmul
            pe.wait_ge(ones_ready, 2)
            pe.wait_ge(chosen_ready, 1)
            rhs = chosen[:].rearrange("p e t -> p (e t)")
            mm(ps_total[:, 0:E * tiles], ones_bf[:], rhs, start=True, stop=True).then_inc(counted, 1)
            mm(ps_before[:, 0:E * tiles], before_bf[:], rhs, start=True, stop=True).then_inc(counted, 1)

            def visit(it):
                if it.has(0):
                    r = it.ring(0)
                    it.wait(marked_ready, 0)
                    it.wait(hot_by_act, 0)
                    it.wait(hot_by_dve, 0)
                    for j in range(TURN * TOPK):
                        last = mm(ps_pairs[:, 0:places], one_hot[:, r, j // HALF, j % HALF, :], marked[:, r, j, :],
                                  start=it.b == 0 and j == 0, stop=it.b == turns - 1 and j == TURN * TOPK - 1)
                    last.then_inc(hot_used, 1)
                    if it.b == turns - 1:
                        pe.wait_ge(hot_used, turns)
                        pe.nop().then_inc(pairs_done, 1)

            visits(pe, turns, visit, unroll=2, lead=0, tail=2, ahead=1)


def experts(nc, ident, kept, x1_rows, out_rows):
    w2, pairs, expert_of = (kept[k] for k in ("w2", "pairs", "expert_of"))
    n = pairs.shape[1]
    RING, IDX = 4, 8
    CHUNKS = [(c, min(P, HIDDEN - c)) for c in range(0, HIDDEN, P)]

    ctx = ExitStack()
    with ctx:
        def sb(name, shape, dt=F32):
            return ctx.enter_context(nc.sbuf_tensor(name, shape, dt))

        def sem(name):
            return ctx.enter_context(nc.semaphore(name))

        idx = sb("idx", [P, IDX, 2], I32)
        xg = sb("xg", [P, RING, D])
        x_high, x_low = (sb(k, [P, 2, P], F32R) for k in ("x_high", "x_low"))
        act_a = sb("act_a", [P, 2, HIDDEN])
        h = sb("h", [P, 2, len(CHUNKS) * P])
        h_t = sb("h_t", [P, 2, len(CHUNKS) * P])
        rows_out = sb("rows_out", [P, RING, D])
        ps_a = ctx.enter_context(nc.psum_tensor("ps_a", [P, 2, 512], F32))
        ps_b = ctx.enter_context(nc.psum_tensor("ps_b", [P, 2, 512], F32))
        ps_h = ctx.enter_context(nc.psum_tensor("ps_h", [P, 2, 512], F32))
        ps_x = ctx.enter_context(nc.psum_tensor("ps_x", [P, 512], F32))
        ps_y = ctx.enter_context(nc.psum_tensor("ps_y", [P, 512], F32))

        padded = sem("padded")
        idx_ready, x_turned, high_taken, x_taken, a_done, b_done, a_taken, h_ready, h_turned, h_taken, y_done, y_taken = map(
            sem, ("idx_ready", "x_turned", "high_taken", "x_taken", "a_done", "b_done", "a_taken", "h_ready", "h_turned", "h_taken",
                  "y_done", "y_taken"))
        gathered = [sem(f"gathered{i}") for i in range(RING)]
        scattered = [sem(f"scattered{i}") for i in range(RING)]

        block = ctx.enter_context(nc.Block())
        pace = dict(unroll=IDX, lead=4, tail=2, ahead=4)

        @block.gpsimd
        def _(pool):
            def visit(it):
                if it.has(3):
                    it.wait(idx_ready, 3)
                    it.wait(x_turned, 3 - RING)
                    pool.indirect_dma_start(
                        out=xg[:, it.ring(3, RING), :], out_offset=None, in_=x1_rows,
                        in_offset=bass.IndirectOffsetOnAxis(ap=idx[:, it.ring(3, IDX), 0:1], axis=0),
                    ).then_inc(gathered[it.ring(3, RING)], 16)
                if it.has(-2):
                    it.wait(y_taken, -2)
                    pool.indirect_dma_start(
                        out=out_rows, out_offset=bass.IndirectOffsetOnAxis(ap=idx[:, it.ring(-2, IDX), 1:2], axis=0),
                        in_=rows_out[:, it.ring(-2, RING), :], in_offset=None,
                    ).then_inc(scattered[it.ring(-2, RING)], 16)

            visits(pool, n, visit, **pace)
            for i in range(RING):
                pool.wait_ge(scattered[i], 16 * (n // RING))

        @block.scalar
        def _(act):
            def visit(it):
                if it.has(0):
                    it.wait(a_done, 0)
                    it.wait(h_ready, -2)
                    act.activation(act_a[:, it.ring(0), :], ps_a[:, it.ring(0), 0:HIDDEN], ACT.Silu).then_inc(a_taken, 1)
                if it.has(1):
                    it.wait(x_turned, 1)
                    it.wait(b_done, -1)
                    act.activation(x_high[:, it.ring(1), :], ps_x[:, 0:P], ACT.Copy).then_inc(high_taken, 1)
                if it.has(-2):
                    it.wait(y_done, -2)
                    it.wait_landed(scattered, -2 - RING)
                    act.activation(rows_out[:, it.ring(-2, RING), :], ps_y[:, 0:D], ACT.Copy).then_inc(y_taken, 1)

            visits(act, n, visit, **pace)

        @block.vector
        def _(dve):
            for u in range(2):
                nc.vector.memset(h[:, u, HIDDEN:], 0.0).then_inc(padded, 1)

            def visit(it):
                if it.has(4):
                    it.wait_landed(scattered, 4 - IDX)
                    nc.vector.tensor_copy(idx[:, it.ring(4, IDX), :].rearrange("p (o s) -> p o s", o=1),
                                          pairs[:, bass.ds(it.index(4), 1), :]).then_inc(idx_ready, 1)
                if it.has(1):
                    it.wait(high_taken, 1)
                    it.wait(b_done, -1)
                    nc.vector.tensor_tensor(x_low[:, it.ring(1), :], ps_x[:, 0:P], x_high[:, it.ring(1), :].bitcast(F32),
                                            ALU.subtract).then_inc(x_taken, 1)
                if it.has(-1):
                    it.wait(h_turned, -1)
                    it.wait(y_done, -3)
                    nc.vector.tensor_copy(h_t[:, it.ring(-1), :], ps_h[:, it.ring(-1), 0:len(CHUNKS) * P]).then_inc(
                        h_taken, 1)
                if it.has(0):
                    it.wait(a_taken, 0)
                    it.wait(b_done, 0)
                    it.wait(h_turned, -2)
                    nc.vector.tensor_tensor(h[:, it.ring(0), 0:HIDDEN], act_a[:, it.ring(0), :],
                                            ps_b[:, it.ring(0), 0:HIDDEN], ALU.mult).then_inc(h_ready, 1)

            visits(dve, n, visit, **pace)

        @block.tensor
        def _(pe):
            mm = nc.tensor.matmul
            pe.wait_ge(padded, 2)
            in_range = "the routing bounds each tile's expert by EXPERTS - 1"
            bounds = dict(engines=[mybir.EngineType.PE], min_val=0, max_val=EXPERTS - 1,
                          skip_runtime_bounds_check_because=in_range)
            held = {}

            def expert(it, off):
                if it.b is not None:
                    return nc.values_load(expert_of[0:1, it.b + off:it.b + off + 1], **bounds)
                if not held:
                    first = it.index(-2)
                    _, values = nc.values_load_multi_w_load_instructions(
                        expert_of[0:1, bass.ds(first, IDX + 2)], **bounds)
                    held.update(enumerate(values, -2))
                return held[it.u + off]

            def wide(it, out, w, e):
                cols = bass.ds(e * HIDDEN, HIDDEN)
                x_parts = (x_high, x_high, x_low)
                w_parts = (kept["w_high"][w], kept["w_low"][w], kept["w_high"][w])
                for i, (x_part, w_part) in enumerate(zip(x_parts, w_parts)):
                    last = mm(out, x_part[:, it.ring(0), :], w_part[:, cols], start=i == 0, stop=i == PARTS - 1)
                return last

            def visit(it):
                if it.has(0):
                    e = expert(it, 0)
                    it.wait(x_taken, 0)
                    it.wait(a_taken, -2)
                    wide(it, ps_a[:, it.ring(0), 0:HIDDEN], 0, e).then_inc(a_done, 1)
                if it.has(1):
                    it.wait_landed(gathered, 1)
                    it.wait(x_taken, 0)
                    nc.tensor.transpose(ps_x[:, 0:P], xg[:, it.ring(1, RING), :], ident).then_inc(x_turned, 1)
                if it.has(0):
                    it.wait(h_ready, -2)
                    wide(it, ps_b[:, it.ring(0), 0:HIDDEN], 1, e).then_inc(b_done, 1)
                if it.has(-2):
                    e = expert(it, -2)
                    it.wait(h_taken, -2)
                    it.wait(y_taken, -3)
                    for i, (c, rows) in enumerate(CHUNKS):
                        last = mm(ps_y[:, 0:D], h_t[0:rows, it.ring(-2), c:c + P],
                                  w2[0:rows, bass.ds(e * D + i * EXPERTS * D, D)],
                                  start=(i == 0), stop=(i == len(CHUNKS) - 1))
                    last.then_inc(y_done, 1)
                if it.has(-1):
                    it.wait(h_ready, -1)
                    it.wait(h_taken, -3)
                    for c, _ in CHUNKS:
                        last = nc.tensor.transpose(ps_h[:, it.ring(-1), c:c + P], h[:, it.ring(-1), c:c + P], ident)
                    last.then_inc(h_turned, 1)

            visits(pe, n, visit, **pace)


def combine(nc, eps, kept, picked_rows, out):
    x1, weight = kept["y"], kept["weight"]
    tiles = x1.shape[1]
    C = 4
    BY_ACT = 1
    RING, LOADS = 4, 8
    AHEAD = 6
    n = tiles // C
    x1_flat = x1[:].rearrange("p t d -> p (t d)")
    picked = [picked_rows[k * tiles * P:(k + 1) * tiles * P, :].rearrange("(c t p) d -> c p t d", p=P, t=C)
              for k in range(TOPK)]
    out_v = out.rearrange("(c t p) d -> c p t d", p=P, t=C)

    ctx = ExitStack()
    with ctx:
        def sb(name, shape, dt=F32):
            return ctx.enter_context(nc.sbuf_tensor(name, shape, dt))

        def sem(name):
            return ctx.enter_context(nc.semaphore(name))

        pick = sb("pick", [P, LOADS, TOPK, C, D])
        w_chunk = sb("w_chunk", [P, RING, TOPK, C])
        weighed = sb("weighed", [P, RING, TOPK, C, D])
        part, z, normal = (sb(k, [P, RING, C, D]) for k in ("part", "z", "normal"))
        z_stats = sb("z_stats", [P, RING, C, 6])
        z_mv = sb("z_mv", [P, RING, C, 2])
        deviation, scale, offset = (sb(k, [P, RING, C]) for k in ("deviation", "scale", "offset"))
        landed = [sem(f"landed{i}") for i in range(LOADS)]
        stored = [sem(f"stored{i}") for i in range(RING)]
        weighed_ready = [sem(f"weighed_ready{k}") for k in range(TOPK)]
        w_ready, part_ready, z_ready, z_stats_ready, z_mv_ready = map(
            sem, ("w_ready", "part_ready", "z_ready", "z_stats_ready", "z_mv_ready"))
        deviation_ready, scale_ready, offset_ready, act_normal, dve_normal = map(
            sem, ("deviation_ready", "scale_ready", "offset_ready", "act_normal", "dve_normal"))
        block = ctx.enter_context(nc.Block())
        pace = dict(unroll=LOADS, lead=AHEAD, tail=2, ahead=AHEAD)

        @block.sync
        def _(sp):
            def visit(it):
                if it.has(AHEAD):
                    it.wait(weighed_ready[TOPK - 1], AHEAD - LOADS)
                    for k in range(TOPK):
                        sp.dma_start(pick[:, it.ring(AHEAD, LOADS), k, :, :], picked[k][it.index(AHEAD)]).then_inc(
                            landed[it.ring(AHEAD, LOADS)], 16)
                if it.has(-1):
                    it.wait(act_normal, -1)
                    it.wait(dve_normal, -1)
                    sp.dma_start(out_v[it.index(-1)], normal[:, it.ring(-1, RING), :, :]).then_inc(
                        stored[it.ring(-1, RING)], 16)

            visits(sp, n, visit, **pace)
            for i in range(RING):
                sp.wait_ge(stored[i], 16 * len(range(i, n, RING)))

        @block.gpsimd
        def _(pool):
            def visit(it):
                if it.has(3):
                    it.wait(weighed_ready[TOPK - 1], 3 - RING)
                    pool.tensor_copy(w_chunk[:, it.ring(3, RING), :, :],
                                     weight[:, :, bass.ds(it.index(3, C), C)]).then_inc(w_ready, 1)
                if it.has(1):
                    r = it.ring(1, RING)
                    it.wait(weighed_ready[0], 1)
                    it.wait(z_ready, 1 - RING)
                    pool.tensor_tensor(part[:, r, :, :].rearrange("p t d -> p (t d)"),
                                       weighed[:, r, 0, :, :].rearrange("p t d -> p (t d)"),
                                       x1_flat[:, bass.ds(it.index(1, C * D), C * D)], ALU.add).then_inc(part_ready, 1)

            visits(pool, n, visit, **pace)

        @block.scalar
        def _(act):
            def visit(it):
                if it.has(2):
                    r = it.ring(2, RING)
                    it.wait_landed(landed, 2, TOPK)
                    it.wait(w_ready, 2)
                    it.wait(z_ready, 2 - RING)
                    for k in range(TOPK):
                        for t in range(C):
                            last = act.activation(weighed[:, r, k, t, :], pick[:, it.ring(2, LOADS), k, t, :], ACT.Copy,
                                                  scale=w_chunk[:, r, k, t:t + 1])
                        last.then_inc(weighed_ready[k], 1)
                if it.has(0):
                    r = it.ring(0, RING)
                    it.wait(z_mv_ready, 0)
                    act.activation(deviation[:, r, :], z_mv[:, r, :, 1], ACT.Sqrt, bias=eps).then_inc(deviation_ready, 1)
                if it.has(-1):
                    r = it.ring(-1, RING)
                    it.wait(offset_ready, -1)
                    it.wait_landed(stored, -1 - RING)
                    for t in range(BY_ACT):
                        last = act.activation(normal[:, r, t, :], z[:, r, t, :], ACT.Identity,
                                              scale=scale[:, r, t:t + 1], bias=offset[:, r, t:t + 1])
                    last.then_inc(act_normal, 1)

            visits(act, n, visit, **pace)

        @block.vector
        def _(dve):
            v = nc.vector

            def visit(it):
                r, before = it.ring(0, RING), it.ring(-1, RING)
                if it.has(0):
                    it.wait(part_ready, 0)
                    it.wait(act_normal, -RING)
                    it.wait(weighed_ready[1], 0)
                    v.tensor_tensor(z[:, r, :, :], weighed[:, r, 1, :, :], part[:, r, :, :], ALU.add).then_inc(z_ready, 1)
                if it.has(-1):
                    it.wait(deviation_ready, -1)
                    v.reciprocal(scale[:, before, :], deviation[:, before, :]).then_inc(scale_ready, 1)
                if it.has(0):
                    it.wait(z_ready, 0)
                    for t in range(C):
                        last = v.bn_stats(z_stats[:, r, t, :], z[:, r, t, :])
                    last.then_inc(z_stats_ready, 1)
                if it.has(-1):
                    it.wait(scale_ready, -1)
                    v.scalar_tensor_tensor(offset[:, before, :], z_mv[:, before, :, 0], -1.0, scale[:, before, :],
                                           ALU.mult, ALU.mult).then_inc(offset_ready, 1)
                if it.has(0):
                    it.wait(z_stats_ready, 0)
                    it.settle()
                    for t in range(C):
                        last = v.bn_aggr(z_mv[:, r, t, :], z_stats[:, r, t, :])
                    last.then_inc(z_mv_ready, 1)
                if it.has(-1):
                    it.wait(offset_ready, -1)
                    it.wait_landed(stored, -1 - RING)
                    for t in range(BY_ACT, C):
                        last = v.tensor_scalar(normal[:, before, t, :], z[:, before, t, :], scale[:, before, t:t + 1],
                                               offset[:, before, t:t + 1], ALU.mult, ALU.add)
                    last.then_inc(dve_normal, 1)

            visits(dve, n, visit, **pace)


def build(nc, x, xt, wqkv, bqk, bv, wo, bo, wg, sel, consts, w1, w3, w2, out):
    tokens = x.shape[0]
    tiles = tokens // P
    places = -(-(tiles * TOPK + EXPERTS - 1) // 8) * 8
    x1_rows = nc.dram_tensor("x1_rows", (tokens, D), F32).ap()
    picked_rows = nc.dram_tensor("picked_rows", (TOPK * tokens + places * P, D), F32).ap()

    ctx = ExitStack()
    with ctx:
        def sb(name, shape, dt=F32):
            return ctx.enter_context(nc.sbuf_tensor(name, shape, dt))

        cst = sb("cst", [P, consts.shape[1]])
        at = columns(tiles, places)

        def consts_at(name):
            return cst[:, at[name][0]:at[name][1]]

        kept = {
            "spent": [],
            "y": sb("y_all", [P, tiles, D]), "mv": sb("mv_all", [P, tiles, 2]),
            "choice": sb("choice", [P, tiles, EXPERTS + 2 * TOPK]), "less_8": consts_at("less_8"),
            "weight": sb("weight", [P, TOPK, tiles]),
            "pairs": sb("pairs", [P, places, 2], I32), "expert_of": sb("expert_of", [P, places], I32),
        }
        attention(nc, x, xt, wqkv, bqk, bv, wo, bo, wg, sel, cst, consts, kept)
        kept.update(w_high=[sb(f"w{k}_high", [P, EXPERTS * HIDDEN], F32R) for k in (1, 3)],
                    w_low=[sb(f"w{k}_low", [P, EXPERTS * HIDDEN], F32R) for k in (1, 3)],
                    w2=sb("w2_sb", [P, -(-HIDDEN // P) * EXPERTS * D]))
        routing(nc, consts_at, w1, w3, w2, kept, x1_rows)
        experts(nc, consts_at("ident"), kept, x1_rows, picked_rows)
        combine(nc, consts_at("eps"), kept, picked_rows, out)


def columns(tiles, places):
    widths = {"ident": P, "mask": P, "shift_rows": 1, "before": P, "iota": max(P, places), "less_8": EXPERTS,
              "numbers": TOPK * tiles, "partition": 1, "spare": places, "eps": 1}
    at, out = 0, {}
    for name, width in widths.items():
        out[name] = (at, at + width)
        at += width
    out["end"] = (at, at)
    return out


def table(tiles, places):
    at = columns(tiles, places)
    out = np.zeros((P, at["end"][0]), np.float32)

    def put(name, value):
        out[:, at[name][0]:at[name][1]] = value

    put("ident", np.eye(P))
    put("mask", np.triu(np.full((P, P), MASKED), 1))
    out[SHIFT_ROW:SHIFT_ROW + 2, at["shift_rows"][0]] = 1
    put("before", np.triu(np.ones((P, P)), 1) - 1)
    put("iota", np.arange(at["iota"][1] - at["iota"][0]))
    put("less_8", np.arange(EXPERTS) - EXPERTS)
    tile, pick = np.divmod(np.arange(TOPK * tiles), TOPK)
    put("numbers", (1 + tile + tiles * pick) * P + np.arange(P)[:, None])
    put("eps", EPS)
    put("partition", np.arange(P)[:, None])
    put("spare", P + TOPK * tiles * P + np.arange(P)[:, None] + P * np.arange(places))
    return out


def layout(inputs):
    def f(a):
        return np.ascontiguousarray(np.asarray(a))

    x = f(inputs["L0_attn_x"]).reshape(-1, D)
    tiles = x.shape[0] // P
    places = -(-(tiles * TOPK + EXPERTS - 1) // 8) * 8
    w = f(inputs["L0_attn_qkv_w"])
    b = f(inputs["L0_attn_qkv_b"])
    return {
        "x": x, "xt": f(x.T), "wqkv": f(w.T), "bqk": f(b[:2 * D].reshape(2, D).T),
        "bv": f(np.broadcast_to(b[2 * D:], (P, D))), "wo": f(np.asarray(inputs["L0_attn_out_w"]).T),
        "bo": f(np.broadcast_to(np.tile(np.asarray(inputs["L0_attn_out_b"]), BLOCKS), (P, BLOCKS * D))),
        "wg": f(np.asarray(inputs["L0_ffn_Wg"]).T), "sel": selectors(), "consts": table(tiles, places),
        "w1": f(np.asarray(inputs["L0_ffn_W1"]).transpose(2, 0, 1).reshape(D, -1)),
        "w3": f(np.asarray(inputs["L0_ffn_W3"]).transpose(2, 0, 1).reshape(D, -1)),
        "w2": f(np.asarray(inputs["L0_ffn_W2"]).transpose(2, 0, 1).reshape(HIDDEN, -1)),
    }


def kernel(**inputs):
    import concourse.bacc as bacc
    from concourse.bass_utils import run_bass_kernel_spmd

    nc = bacc.Bacc("TRN2", target_bir_lowering=False, num_devices=1)
    arrays = layout(inputs)
    shape = np.asarray(inputs["L0_attn_x"]).shape
    args = {name: nc.dram_tensor(name, a.shape, mybir.dt.from_np(a.dtype), kind="ExternalInput").ap()
            for name, a in arrays.items()}
    out = nc.dram_tensor("out", (shape[0] * shape[1], D), F32, kind="ExternalOutput").ap()
    build(nc, out=out, **args)
    got = run_bass_kernel_spmd(nc, [arrays], core_ids=[0])
    return np.asarray(got.results[0]["out"]).reshape(shape)
```

```python
import numpy as np
from contextlib import ExitStack

import concourse.bass as bass
from concourse import mybir

F32 = mybir.dt.float32
F32R = mybir.dt.float32r
BF16 = mybir.dt.bfloat16
I32 = mybir.dt.int32
ALU = mybir.AluOpType
ACT = mybir.ActivationFunctionType
AX = mybir.AxisListType

P = 128
D = 128
L = 256
BLOCKS = L // P
HEADS, HEAD_DIM = 16, 8
GROUP = 4
GROUPS = HEADS // GROUP
QUAD = 32
PARTS = 3
ROWS = PARTS * HEAD_DIM
SHIFT_ROW = ROWS
MASKED = -1.0e30
EXPERTS, TOPK, HIDDEN = 8, 2, 352
TAKEN = -3.0e38
EPS = 1e-5
LAG = 2


def selectors():
    parts = {"qh": (0, 1), "ql": (2,), "kh": (0, 2), "kl": (1,)}
    out = np.zeros((P, GROUPS, len(parts), P), np.float32)
    for g in range(GROUPS):
        for s, rows in enumerate(parts.values()):
            for j in range(GROUP):
                for r in rows:
                    for d in range(HEAD_DIM):
                        out[(g * GROUP + j) * HEAD_DIM + d, g, s, j * QUAD + r * HEAD_DIM + d] = 1
    return out.reshape(P, -1)


class Visit:

    def __init__(self, eng, n, b=None, base=None, u=0):
        self.eng, self.n, self.b, self.base, self.u = eng, n, b, base, u
        self.values = {}
        self.alone = eng.engine in (mybir.EngineType.SP, mybir.EngineType.Pool)

    def ring(self, off, size=2):
        return ((self.b if self.b is not None else self.u) + off) % size

    def has(self, off):
        return self.b is None or 0 <= self.b + off < self.n

    def value(self, scale, plus):
        if (scale, plus) not in self.values:
            self.values[scale, plus] = self.eng.snap(self.base * scale + plus)
        return self.values[scale, plus]

    def index(self, off, scale=1):
        if self.b is not None:
            return (self.b + off) * scale
        return self.value(scale, (self.u + off) * scale)

    def wait(self, sem, off, per=1):
        if self.b is None or 0 <= self.b + off < self.n:
            self.eng.wait_ge(sem, self.index(off + 1, per))
            if self.alone:
                self.settle()

    def settle(self):
        if self.b is None:
            self.eng.nop(nofuse=True)

    def wait_landed(self, sems, off, dmas=1):
        size, per = len(sems), 16 * dmas
        if self.b is None:
            lap = self.value(per // size, ((self.u + off) // size + 1) * per)
            self.eng.wait_ge(sems[self.ring(off, size)], lap)
            if self.alone:
                self.settle()
        elif 0 <= self.b + off < self.n:
            self.eng.wait_ge(sems[self.ring(off, size)], ((self.b + off) // size + 1) * per)


def visits(eng, n, body, unroll, lead, tail, ahead):
    first = -(-tail // unroll) * unroll
    count = max(0, (n - ahead - first) // unroll)
    for b in range(-lead, first):
        body(Visit(eng, n, b=b))
    if count:
        with eng.Fori(0, count) as i:
            base = eng.snap(i * unroll + first)
            values = {}
            for u in range(unroll):
                turn = Visit(eng, n, base=base, u=u)
                turn.values = values
                body(turn)
    for b in range(first + count * unroll, n + tail):
        body(Visit(eng, n, b=b))


TASKS = [
    [[("pack_k1", 1)], [("project", -2)], []],
    [[("pack_q0", 1)], [("pack_q1", 1)], [("values", 1), ("heads0", -1)]],
    [[("heads1", -1)], [("split", 2)], []],
    [[], [("mixed", -1)], [("pack_k0", 2)]],
]
ORDER = [t for step in TASKS for part in step for t in part]
BANK_OF = {t[0]: i % 2 for i, t in enumerate(ORDER)}


def attention(nc, x, xt, wqkv, bqk, bv, wo, wo_rows, bo, bo_columns, wg, sel, cst, consts, kept):
    y_all, mv_all, choice = kept["y"], kept["mv"], kept["choice"]
    tokens = x.shape[0]
    n = tokens // L
    x_v = x.rearrange("(b k p) d -> b p k d", k=BLOCKS, p=P)
    xt_v = xt.rearrange("d (b t) -> b d t", t=L)

    spent = kept["spent"]
    ctx = ExitStack()
    with ctx:
        def sb(name, shape, dt=F32):
            return ctx.enter_context(nc.sbuf_tensor(name, shape, dt))

        def sem(name):
            spent.append(nc.alloc_semaphore(name=name))
            return spent[-1]

        wqkv_sb = sb("wqkv_sb", [P, 3 * D + EXPERTS])
        wc = wqkv_sb[:, 3 * D:]
        bqk_sb = sb("bqk_sb", [P, 2])
        bv_sb = sb("bv_sb", [P, D])
        wo_sb = sb("wo_sb", [P, D + EXPERTS])
        wo_rows_sb = sb("wo_rows_sb", [P, D])
        bo_columns_sb = sb("bo_columns_sb", [P, P])
        averages = sb("averages", [P, P])
        bias_logits = sb("bias_logits", [P, EXPERTS])
        bo_sb = sb("bo_sb", [P, BLOCKS * D])
        wg_sb = sb("wg_sb", [P, EXPERTS])
        sel_f = sb("sel_f", [P, GROUPS * 4 * P])
        sel_r = sb("sel_r", [P, GROUPS, 4, P], F32R)
        ident = cst[:, 0:P]
        ones_rows = cst[:, 2 * P:2 * P + 1]
        less_8 = kept["less_8"]
        ident_bf = sb("ident_bf", [P, P], BF16)
        mask_bf = sb("mask_bf", [P, GROUP, P], BF16)

        x_sb = sb("x_sb", [P, 2, BLOCKS * D])
        xt_sb = sb("xt_sb", [P, 2, L])
        xb = sb("xb", [P, BLOCKS * D])
        split = {k: sb(k, [P, L], F32R) for k in ("qh", "ql", "kh", "kl")}
        q_dense = sb("q_dense", [P, 2, GROUPS, L], F32R)
        k_dense = sb("k_dense", [P, 2, GROUPS, L], F32R)
        q_pad = sb("q_pad", [P, 2, GROUPS, GROUP, L], F32R)
        k_pad = sb("k_pad", [P, 2, GROUPS, GROUP, L], F32R)
        v_ext = sb("v_ext", [P, 2, BLOCKS, HEADS, QUAD])
        neg_max = sb("neg_max", [P, 2, BLOCKS, GROUP])
        shift = sb("shift", [P, 2, 2, GROUP, BLOCKS], F32R)
        shift_t = sb("shift_t", [2 * BLOCKS * GROUP, 2, P], F32R)
        probs = sb("probs", [P, 2, 3 * 512])
        out_t = sb("out_t", [P, 2, GROUPS, L])
        rsum = sb("rsum", [P, 2, HEADS])
        heads = sb("heads", [P, BLOCKS, D])
        heads_t = sb("heads_t", [P, L])
        y = sb("y", [P, BLOCKS, D])
        stats = sb("stats", [P, BLOCKS, 6])
        mv = sb("mv", [P, BLOCKS, 2])
        yc = sb("yc", [P, BLOCKS, D])
        chosen = sb("chosen_b", [P, 2, BLOCKS, choice.shape[2]])
        hit = sb("hit_b", [P, 2, BLOCKS, EXPERTS])
        rest = sb("rest_b", [P, BLOCKS, EXPERTS])

        ps_s = ctx.enter_context(nc.psum_tensor("ps_s", [P, 2, 512], F32))
        ps_st = ctx.enter_context(nc.psum_tensor("ps_st", [P, 3, 512], F32))
        ps_o = ctx.enter_context(nc.psum_tensor("ps_o", [P, 512], F32))
        ps_m = ctx.enter_context(nc.psum_tensor("ps_m", [P, 2, 512], F32))

        first_loaded, loaded = sem("first_loaded"), sem("loaded")
        consts_ready = sem("consts_ready")
        zeroed = sem("zeroed")
        x_landed, xt_landed, k_pad_landed, q_pad_landed = (
            [sem(f"{name}{i}") for i in range(2)] for name in ("x_landed", "xt_landed", "k_pad_landed", "q_pad_landed"))
        s_done = [[sem(f"s_done{g}{k}") for k in range(3)] for g in range(GROUPS)]
        max_done = [[sem(f"max_done{g}{k}") for k in range(3)] for g in range(GROUPS)]
        shift_hi = [sem(f"shift_hi{g}") for g in range(GROUPS)]
        shift_ready = [sem(f"shift_ready{g}") for g in range(GROUPS)]
        shift_landed = [sem(f"shift_landed{g}") for g in range(GROUPS)]
        st_done = [sem(f"st_done{g}") for g in range(GROUPS)]
        exp_done = [sem(f"exp_done{g}") for g in range(GROUPS)]
        masked = [sem(f"masked{g}") for g in range(GROUPS)]
        pv_done = [sem(f"pv_done{g}") for g in range(GROUPS)]
        out_t_ready = [sem(f"out_t_ready{g}") for g in range(GROUPS)]
        made = {t: sem(f"made_{t}") for t, _ in ORDER}
        shift_made = [sem(f"shift_made{g}") for g in range(GROUPS)]
        shift_taken = [sem(f"shift_taken{g}") for g in range(GROUPS)]
        taken = {t: sem(f"taken_{t}") for t, _ in ORDER}
        high_ready = sem("high_ready")
        rsum_ready = [sem(f"rsum_ready{i}") for i in range(BLOCKS)]
        xb_ready = sem("xb_ready")
        stats_ready, mv_ready, yc_ready, y_kept = map(sem, ("stats_ready", "mv_ready", "yc_ready", "y_kept"))

        CHOICE_STEPS = 10
        pick_marked = sem("pick_marked")
        router_step = sem("router_step")
        v_ready, y_ready = sem("v_ready"), sem("y_ready")
        choice_step = [sem(f"choice_step{i}") for i in range(CHOICE_STEPS)]

        block = ctx.enter_context(nc.Block())

        def wide_bank(bank):
            return bank[:, 0:BLOCKS * (D + EXPERTS)].rearrange("p (k d) -> p k d", k=BLOCKS)

        def scores_group(g):
            return (g + LAG) % GROUPS, (g + LAG) // GROUPS

        def shift_group(g):
            return (g - 1 + LAG) % GROUPS, (g - 1 + LAG) // GROUPS

        def two_before(sem_of, it, h, off):
            it.wait(sem_of[(h + 2) % GROUPS], off if h >= 2 else off - 1)

        def values_group(g):
            return (g - 1) % GROUPS, (g - 1) // GROUPS

        def shift_columns(h):
            return ps_o[0:2 * BLOCKS * GROUP, L + (h % 2) * P:L + (h % 2 + 1) * P]

        S_BANK = [[(3 * g + k) % 2 for k in range(3)] for g in range(GROUPS)]
        FIRST_LOADS, CONST_LOADS = 2, 8

        @block.sync
        def _(sp):
            for dst, src in ((wqkv_sb[:, 0:3 * D], wqkv), (bqk_sb[:], bqk)):
                sp.dma_start(dst, src).then_inc(first_loaded, 16)

            def visit(it):
                def load_xt(off):
                    sp.dma_start(xt_sb[:, it.ring(off), :], xt_v[it.index(off)]).then_inc(xt_landed[it.ring(off)], 16)

                if it.b == -2:
                    load_xt(2)
                    load_xt(3)
                    for dst, src in (
                            (wg_sb[:], wg), (wo_rows_sb[:], wo_rows), (bo_columns_sb[:], bo_columns),
                            (bv_sb[:], bv), (wo_sb[:, 0:D], wo), (bo_sb[:], bo)):
                        sp.dma_start(dst, src).then_inc(loaded, 16)
                for g in range(GROUPS):
                    h, off = shift_group(g)
                    if it.has(off):
                        p = it.ring(off)
                        it.wait(shift_taken[h], off)
                        it.wait(st_done[h], off - 2)
                        sp.dma_start(
                            q_pad[SHIFT_ROW:SHIFT_ROW + 2, p, h, :, :].bitcast(F32).rearrange(
                                "s j (k q) -> s (j k) q", k=BLOCKS),
                            shift_t[:, h % 2, :].bitcast(F32)).then_inc(shift_landed[h], 16)
                    if g == 0 and it.has(1):
                        p = it.ring(1)
                        it.wait(taken["pack_k0"], 1)
                        it.wait(taken["pack_k1"], 1)
                        it.wait(s_done[GROUPS - 1][2], -1)
                        if it.b == -1:
                            sp.wait_ge(zeroed, 1)
                        for j in range(GROUP):
                            r = slice(QUAD * j, QUAD * j + ROWS)
                            sp.dma_start(k_pad[r, p, :, j, :].bitcast(F32), k_dense[r, p, :, :].bitcast(F32)).then_inc(k_pad_landed[p], 16)
                    if g == 1 and it.has(1):
                        p = it.ring(1)
                        it.wait(taken["pack_q0"], 1)
                        it.wait(taken["pack_q1"], 1)
                        it.wait(st_done[GROUPS - 1], -1)
                        if it.b == -1:
                            sp.wait_ge(zeroed, 2)
                        for j in range(GROUP):
                            r = slice(QUAD * j, QUAD * j + ROWS)
                            sp.dma_start(q_pad[r, p, :, j, :].bitcast(F32), q_dense[r, p, :, :].bitcast(F32)).then_inc(q_pad_landed[p], 16)
                    if g == 2 and it.has(3) and not it.b == -2:
                        it.wait(made["values"], 1)
                        load_xt(3)
                    if g == 3 and it.has(0):
                        it.wait(xb_ready, -2)
                        sp.dma_start(x_sb[:, it.ring(0), :].rearrange("p (k d) -> p k d", k=BLOCKS),
                                     x_v[it.index(0)]).then_inc(x_landed[it.ring(0)], 16)
            visits(sp, n, visit, unroll=2, lead=2, tail=3, ahead=3)

        @block.gpsimd
        def _(pool):
            pool.memset(k_pad[:].bitcast(F32), 0.0).then_inc(zeroed, 1)
            pool.memset(q_pad[:].bitcast(F32), 0.0).then_inc(zeroed, 1)
            pool.memset(v_ext[:], 0.0).then_inc(zeroed, 1)
            pool.wait_ge(zeroed, 3)
            pool.memset(v_ext[:, :, :, :, HEAD_DIM:HEAD_DIM + 1], 1.0).then_inc(zeroed, 1)

            def visit(it):
                for g in range(GROUPS):
                    if it.has(0):
                        it.wait(exp_done[g], 0)
                        low = probs[:, g % 2, 0:GROUP * L].rearrange("p (h q) -> p h q", q=L)[:, :, 0:P]
                        high = probs[:, g % 2, GROUP * L:].rearrange("p (h q) -> p h q", q=P)
                        for part in (low, high):
                            last = pool.affine_select(out=part, in_=part, compare_op=ALU.is_ge, fill=0.0, base=0,
                                                      pattern=[[0, GROUP], [1, P]], channel_multiplier=-1)
                        last.then_inc(masked[g], 1)
                    if g == 0 and it.has(-2):
                        it.wait(mv_ready, -2)
                        for k in range(BLOCKS):
                            last = pool.tensor_scalar(yc[:, k, :], y[:, k, :], mv[:, k, 0:1], None, ALU.subtract)
                        last.then_inc(yc_ready, 1)
                        it.wait(yc_ready, -2)
                        pool.tensor_copy(y_all[:].rearrange("p t d -> p (t d)")[
                            :, bass.ds(it.index(-2, BLOCKS * D), BLOCKS * D)],
                            yc[:].rearrange("p k d -> p (k d)"))
                        pool.tensor_copy(mv_all[:].rearrange("p t d -> p (t d)")[
                            :, bass.ds(it.index(-2, BLOCKS * 2), BLOCKS * 2)],
                            mv[:].rearrange("p k d -> p (k d)")).then_inc(y_kept, 1)
                    if g == 1 and it.has(-1):
                        it.wait_landed(x_landed, -1)
                        it.wait(taken["project"], -2)
                        pool.tensor_tensor(xb[:], x_sb[:, it.ring(-1), :], bo_sb[:], ALU.add).then_inc(xb_ready, 1)

            pool.wait_ge(loaded, 16 * CONST_LOADS)
            visits(pool, n, visit, unroll=2, lead=2, tail=3, ahead=3)

        @block.scalar
        def _(act):
            for dst, src in ((sel_f[:], sel), (cst[:], consts)):
                act.dma_start(dst, src).then_inc(loaded, 16)
            act.wait_ge(first_loaded, 16 * FIRST_LOADS)

            def copy_out(it, task, off, dst, src, bias=None):
                it.wait(made[task], off)
                if bias is None:
                    act.activation(dst, src, ACT.Copy).then_inc(taken[task], 1)
                else:
                    act.activation(dst, src, ACT.Identity, bias=bias).then_inc(taken[task], 1)

            def task(it, name, off):
                p = it.ring(off)
                bank = ps_m[:, BANK_OF[name], :]
                if name == "pack_k0" and it.b == -2:
                    act.wait_ge(loaded, 16 * CONST_LOADS)
                if name in ("pack_k0", "pack_k1"):
                    h = 2 * int(name[-1])
                    it.wait_landed(k_pad_landed, off - 2, GROUP)
                    it.wait(st_done[GROUPS - 1], off - 2)
                    copy_out(it, name, off, k_dense[:, p, h:h + 2, :].rearrange("p g t -> p (g t)"), bank, ones_rows)
                if name in ("pack_q0", "pack_q1"):
                    h = 2 * int(name[-1])
                    it.wait_landed(q_pad_landed, off - 2, GROUP)
                    it.wait(s_done[GROUPS - 1][2], off - 2)
                    copy_out(it, name, off, q_dense[:, p, h:h + 2, :].rearrange("p g t -> p (g t)"), bank)
                if name == "split":
                    it.wait(made["split"], off)
                    it.wait(made["pack_q1"], off - 1)
                    act.activation(split["qh"][:], bank[:, 0:L], ACT.Identity, bias=bqk_sb[:, 0:1])
                    act.activation(split["kh"][:], bank[:, L:2 * L], ACT.Identity,
                                   bias=bqk_sb[:, 1:2]).then_inc(high_ready, 1)
                if name == "mixed":
                    it.wait(made["project"], off - 1)
                    copy_out(it, name, off, heads_t[:], bank[:, 0:L])

            def take_shift(it, h, off):
                it.wait(shift_made[h], off)
                it.wait(shift_landed[(h + 2) % GROUPS], off if h >= 2 else off - 1, 16)
                act.activation(shift_t[:, h % 2, :], shift_columns(h), ACT.Copy).then_inc(shift_taken[h], 1)

            def visit(it):
                for g in range(GROUPS):
                    h, off = shift_group(g)
                    if it.has(off):
                        take_shift(it, h, off)
                    if it.has(0):
                        it.wait(st_done[g], 0)
                        it.wait(pv_done[(g + 2) % GROUPS], 0 if g >= 2 else -1)
                        act.activation(probs[:, g % 2, :], ps_st[:].rearrange("p k f -> p (k f)"), ACT.Exp,
                                       scale=float(HEAD_DIM) ** -0.5).then_inc(exp_done[g], 1)
                    for name, off in TASKS[g][0] + TASKS[g][1]:
                        if it.has(off):
                            task(it, name, off)
                    h, off = values_group(g)
                    if it.has(off):
                        p = it.ring(off)
                        it.wait(pv_done[h], off)
                        it.wait(made["heads1"], off - 2)
                        act.activation(out_t[:, p, h, :], ps_o[:, 0:L], ACT.Copy).then_inc(out_t_ready[h], 1)
                    for name, off in TASKS[g][2]:
                        if it.has(off):
                            task(it, name, off)
            visits(act, n, visit, unroll=2, lead=2, tail=3, ahead=3)

        @block.vector
        def _(dve):
            dve.wait_ge(first_loaded, 16 * FIRST_LOADS)
            dve.wait_ge(loaded, 16 * CONST_LOADS)
            nc.vector.memset(averages[:], 1.0 / D).then_inc(consts_ready, 1)
            nc.vector.tensor_copy(sel_r[:].rearrange("p g s m -> p (g s m)"), sel_f[:]).then_inc(consts_ready, 1)
            nc.vector.tensor_copy(ident_bf[:], ident).then_inc(consts_ready, 1)
            for j in range(GROUP):
                nc.vector.tensor_copy(mask_bf[:, j, :], cst[:, P:2 * P]).then_inc(consts_ready, 1)

            def task(it, name, off):
                p = it.ring(off)
                bank = ps_m[:, BANK_OF[name], :]
                if name == "split":
                    it.wait(high_ready, off)
                    nc.vector.scalar_tensor_tensor(split["ql"][:], bank[:, 0:L], bqk_sb[:, 0:1],
                                                   split["qh"][:].bitcast(F32), ALU.add, ALU.subtract)
                    nc.vector.scalar_tensor_tensor(split["kl"][:], bank[:, L:2 * L], bqk_sb[:, 1:2],
                                                   split["kh"][:].bitcast(F32), ALU.add,
                                                   ALU.subtract).then_inc(taken[name], 1)
                if name == "values":
                    it.wait(made[name], off)
                    it.wait(pv_done[GROUPS - 1], off - 2)
                    if it.b is not None and it.b + off < 2:
                        dve.wait_ge(zeroed, 4)
                    for k in range(BLOCKS):
                        last = nc.vector.tensor_tensor(
                            v_ext[:, p, k, :, 0:HEAD_DIM],
                            wide_bank(bank)[:, k, 0:D].rearrange("p (h d) -> p h d", d=HEAD_DIM),
                            bv_sb[:].rearrange("p (h d) -> p h d", d=HEAD_DIM), ALU.add)
                    last.then_inc(v_ready, 1)
                    nc.vector.tensor_tensor(
                        choice[:, bass.ds(it.index(off, BLOCKS), BLOCKS), 0:EXPERTS], wide_bank(bank)[:, :, D:],
                        bias_logits[:].rearrange("p (o e) -> p o e", o=1).to_broadcast([P, BLOCKS, EXPERTS]),
                        ALU.add).then_inc(taken[name], 1)
                if name in ("heads0", "heads1"):
                    k = int(name[-1])
                    it.wait(made[name], off)
                    v = bank.rearrange("p (h d) -> p h d", d=QUAD)
                    nc.vector.reciprocal(rsum[:, k, :].rearrange("p (h o) -> p h o", o=1),
                                         v[:, :, HEAD_DIM:HEAD_DIM + 1]).then_inc(rsum_ready[k], 1)
                    it.wait(rsum_ready[k], off)
                    it.wait(made["mixed"], off - 1)
                    nc.vector.tensor_tensor(
                        heads[:, k, :].rearrange("p (h d) -> p h d", d=HEAD_DIM), v[:, :, 0:HEAD_DIM],
                        rsum[:, k, :].rearrange("p (h o) -> p h o", o=1).to_broadcast([P, HEADS, HEAD_DIM]),
                        ALU.mult).then_inc(taken[name], 1)
                if name == "project":
                    it.wait(made[name], off)
                    it.wait(xb_ready, off)
                    it.wait(y_kept, off - 1)
                    nc.vector.tensor_tensor(y[:], wide_bank(bank)[:, :, 0:D], xb[:].rearrange("p (k d) -> p k d", d=D),
                                            ALU.add).then_inc(y_ready, 1)
                    it.wait(choice_step[-1], off - 2)
                    it.wait(taken["values"], off)
                    nc.vector.tensor_tensor(
                        chosen[:, p, :, 0:EXPERTS], wide_bank(bank)[:, :, D:],
                        choice[:, bass.ds(it.index(off, BLOCKS), BLOCKS), 0:EXPERTS], ALU.add).then_inc(taken[name], 1)
                    it.wait(y_ready, off)
                    for k in range(BLOCKS):
                        last = nc.vector.bn_stats(stats[:, k, :], y[:, k, :])
                    last.then_inc(stats_ready, 1)
                    it.wait(stats_ready, off)
                    it.settle()
                    for k in range(BLOCKS):
                        last = nc.vector.bn_aggr(mv[:, k, :], stats[:, k, :])
                    last.then_inc(mv_ready, 1)

            numbers = less_8.rearrange("p (o e) -> p o e", o=1).to_broadcast([P, BLOCKS, EXPERTS])

            EARLY = {(3, 0): [("split", 2)], (2, 1): [("heads1", -1)]}

            def choose(it, step):
                off = -3
                if not it.has(off) or step >= CHOICE_STEPS:
                    return
                v, p = nc.vector, it.ring(off)
                lg = chosen[:, p, :, 0:EXPERTS]
                k, what = divmod(step, 5) if step < CHOICE_STEPS - 1 else (None, None)
                it.wait(choice_step[step - 1] if step else taken["project"], off)

                def column(c):
                    return chosen[:, p, :, EXPERTS + c:EXPERTS + c + 1]

                def over_experts(a):
                    return a.to_broadcast([P, BLOCKS, EXPERTS])

                cur = rest[:] if k == 1 else lg
                if k is None:
                    last = v.tensor_copy(choice[:].rearrange("p t c -> p (t c)")[
                        :, bass.ds(it.index(off, BLOCKS * choice.shape[2]), BLOCKS * choice.shape[2])],
                        chosen[:, p, :, :].rearrange("p k c -> p (k c)"))
                elif what == 0:
                    last = v.tensor_reduce(out=column(k), in_=cur, axis=AX.X, op=ALU.max)
                elif what == 1:
                    last = v.tensor_tensor(hit[:, 0, :, :], cur, over_experts(column(k)), ALU.is_equal)
                elif what == 2:
                    last = v.tensor_tensor(hit[:, 1, :, :], hit[:, 0, :, :], numbers, ALU.mult)
                elif what == 3:
                    last = v.tensor_reduce(out=column(2 + k), in_=hit[:, 1, :, :], axis=AX.X, op=ALU.min)
                elif k == 0:
                    v.tensor_tensor(hit[:, 0, :, :], numbers, over_experts(column(2)), ALU.is_equal).then_inc(
                        pick_marked, 1)
                    it.wait(pick_marked, off)
                    last = v.scalar_tensor_tensor(rest[:], hit[:, 0, :, :], TAKEN, lg, ALU.mult, ALU.add)
                last.then_inc(choice_step[step], 1)

            def visit(it):
                for g in range(GROUPS):
                    h, off = scores_group(g)
                    for k in range(3):
                        if it.has(off):
                            it.wait(s_done[h][k], off)
                            bank = ps_s[:, S_BANK[h][k], :]
                            src = bank.rearrange("p (h t) -> p h t", t=P if k == 0 else L)
                            dst = neg_max[:, h % 2, 0, :] if k == 0 else neg_max[:, h % 2, 1, 2 * k - 2:2 * k]
                            nc.vector.tensor_reduce(out=dst, in_=src, axis=AX.X, op=ALU.max,
                                                    negate=True).then_inc(max_done[h][k], 1)
                        choose(it, 3 * g + k)
                        for name, toff in EARLY.get((g, k), ()):
                            if it.has(toff):
                                task(it, name, toff)
                    if it.has(off):
                        two_before(shift_made, it, h, off)
                        it.wait(max_done[h][2], off)
                        m = neg_max[:, h % 2, :, :].rearrange("p k j -> p j k")
                        nc.vector.tensor_copy(shift[:, h % 2, 0, :, :], m).then_inc(shift_hi[h], 1)
                        it.wait(shift_hi[h], off)
                        nc.vector.tensor_tensor(shift[:, h % 2, 1, :, :], m, shift[:, h % 2, 0, :, :].bitcast(F32),
                                                ALU.subtract).then_inc(shift_ready[h], 1)
                    for name, off in TASKS[g][0] + TASKS[g][1] + TASKS[g][2]:
                        if it.has(off) and name in ("values", "heads0", "project"):
                            task(it, name, off)

                if it.b == -2:
                    dve.wait_ge(router_step, 1)
                    nc.vector.tensor_tensor(wc, wg_sb[:], ps_st[:, 0, 0:EXPERTS], ALU.subtract).then_inc(router_step, 1)
                    dve.wait_ge(router_step, 3)
                    nc.vector.tensor_copy(wo_sb[:, D:], ps_st[:, 1, 0:EXPERTS])
                    nc.vector.tensor_copy(bias_logits[:], ps_st[:, 1, EXPERTS:2 * EXPERTS]).then_inc(router_step, 1)
                    dve.wait_ge(router_step, 4)

            visits(dve, n, visit, unroll=2, lead=2, tail=3, ahead=3)

        @block.tensor
        def _(pe):
            pe.wait_ge(first_loaded, 16 * FIRST_LOADS)
            mm = nc.tensor.matmul

            def task(it, name, off):
                p = it.ring(off)
                bank = ps_m[:, BANK_OF[name], :]
                at = ORDER.index((name, off))
                if it.b is None:
                    before, boff = ORDER[(at - 2) % len(ORDER)]
                    it.wait(taken[before], boff if at >= 2 else boff - 1)
                else:
                    found = False
                    for back in range(2, 4 * len(ORDER), 2):
                        before, boff = ORDER[(at - back) % len(ORDER)]
                        boff += (at - back) // len(ORDER)
                        if not found and it.has(boff):
                            it.wait(taken[before], boff)
                            found = True
                if name == "split":
                    it.wait_landed(xt_landed, off)
                    for i in range(2):
                        last = mm(bank[:, i * L:(i + 1) * L], wqkv_sb[:, i * D:(i + 1) * D], xt_sb[:, p, :],
                                  start=True, stop=True)
                if name == "values":
                    for k in range(BLOCKS):
                        last = mm(wide_bank(bank)[:, k, :], xt_sb[:, p, k * P:(k + 1) * P], wqkv_sb[:, 2 * D:],
                                  start=True, stop=True)
                if name.startswith("pack"):
                    if name == "pack_k0" and it.b == -2:
                        pe.wait_ge(loaded, 16 * CONST_LOADS)
                        pe.wait_ge(consts_ready, 3 + GROUP)
                    it.wait(taken["split"], off)
                    hi, lo, s = ("kh", "kl", 2) if "k" in name[5:] else ("qh", "ql", 0)
                    for i in range(2):
                        g = 2 * int(name[-1]) + i
                        mm(bank[:, i * L:(i + 1) * L], sel_r[:, g, s, :], split[hi][:], start=True, stop=False)
                        last = mm(bank[:, i * L:(i + 1) * L], sel_r[:, g, s + 1, :], split[lo][:], start=False,
                                  stop=True)
                if name in ("heads0", "heads1"):
                    k = int(name[-1])
                    it.wait(out_t_ready[GROUPS - 1], off)
                    for g in range(GROUPS):
                        last = nc.tensor.transpose(bank[:, g * P:(g + 1) * P], out_t[:, p, g, k * P:(k + 1) * P], ident)
                if name == "mixed":
                    it.wait(taken["heads0"], off)
                    it.wait(taken["heads1"], off)
                    for k in range(BLOCKS):
                        last = nc.tensor.transpose(bank[:, k * P:(k + 1) * P], heads[:, k, :], ident)
                if name == "project":
                    it.wait(taken["mixed"], off)
                    for k in range(BLOCKS):
                        last = mm(wide_bank(bank)[:, k, :], heads_t[:, k * P:(k + 1) * P], wo_sb[:], start=True,
                                  stop=True)
                last.then_inc(made[name], 1)

            def turn_shift(it, g, h, off):
                it.wait(shift_ready[h], off)
                it.wait(out_t_ready[(g - 2) % GROUPS], (g - 2) // GROUPS)
                if not it.has((g - 2) // GROUPS):
                    before, boff = shift_group(g - 1)
                    it.wait(shift_taken[before], boff)
                nc.tensor.transpose(shift_columns(h), shift[:, h % 2, :, :, :].rearrange("p s j k -> p (s j k)").bitcast(F32),
                                    ident).then_inc(shift_made[h], 1)

            def scores(it, h, off, k):
                p = it.ring(off)
                if k == 0:
                    if h == 0:
                        it.wait_landed(k_pad_landed, off, GROUP)
                        it.wait(taken["pack_q0"], off)
                    if h == 2:
                        it.wait(taken["pack_q1"], off)
                back = 3 * h + k - 2
                it.wait(max_done[(back // 3) % GROUPS][back % 3], off if back >= 0 else off - 1)
                bank = ps_s[:, S_BANK[h][k], :]
                if k == 0:
                    mm(bank, q_dense[:, p, h, 0:P], k_pad[:, p, h, :, 0:P], start=True, stop=False)
                    last = mm(bank, ident_bf[:], mask_bf[:], start=False, stop=True)
                else:
                    mm(bank, q_dense[:, p, h, P:L], k_pad[:, p, h, 2 * k - 2:2 * k, :], start=True, stop=False)
                    last = mm(bank.rearrange("p (j t) -> p j t", t=L)[:, :, P:L], ident_bf[:], mask_bf[:, 0:2, :],
                              start=False, stop=True)
                last.then_inc(s_done[h][k], 1)

            def products(it, g):
                p = it.ring(0)
                if g == 0:
                    it.wait_landed(q_pad_landed, 0, GROUP)
                it.wait(shift_landed[g], 0, 16)
                it.wait(exp_done[g - 1], 0 if g else -1)
                for i in range(2):
                    mm(ps_st[:, i, :], k_dense[:, p, g, 0:P], q_pad[:, p, g, 2 * i:2 * i + 2, :], start=True, stop=True)
                mm(ps_st[:, 2, :], k_dense[:, p, g, P:L], q_pad[:, p, g, :, P:L], start=True,
                   stop=True).then_inc(st_done[g], 1)

            def weighted(it, g, h, off):
                p = it.ring(off)
                it.wait(masked[h], off)
                if h == 0:
                    it.wait(taken["values"], off)
                it.wait(out_t_ready[h - 1], off if h else off - 1)
                sh, soff = shift_group(g)
                it.wait(shift_taken[sh], soff)
                for k in range(BLOCKS):
                    for j in range(GROUP):
                        cols = slice(j * L, (j + 1) * L) if k == 0 else slice(GROUP * L + j * P, GROUP * L + (j + 1) * P)
                        last = mm(ps_o[QUAD * j:QUAD * (j + 1), k * P:L], v_ext[:, p, k, h * GROUP + j, :],
                                  probs[:, h % 2, cols], start=(k == 0), stop=(k == BLOCKS - 1))
                last.then_inc(pv_done[h], 1)

            def tasks(it, g, part):
                for name, off in TASKS[g][part]:
                    if it.has(off):
                        task(it, name, off)

            def visit(it):
                for g in range(GROUPS):
                    h, off = scores_group(g)
                    if it.has(off):
                        scores(it, h, off, 0)
                        scores(it, h, off, 1)
                    sh, soff = shift_group(g)
                    if it.has(soff):
                        turn_shift(it, g, sh, soff)
                    if it.has(0):
                        products(it, g)
                    tasks(it, g, 0)
                    if it.has(off):
                        scores(it, h, off, 2)
                    tasks(it, g, 1)
                    vh, voff = values_group(g)
                    if it.has(voff):
                        weighted(it, g, vh, voff)
                    tasks(it, g, 2)

                if it.b == -2:
                    mm(ps_st[:, 0, 0:EXPERTS], averages[:], wg_sb[:], start=True, stop=True).then_inc(router_step, 1)
                    pe.wait_ge(router_step, 2)
                    mm(ps_st[:, 1, 0:EXPERTS], wo_rows_sb[:], wc, start=True, stop=True)
                    mm(ps_st[:, 1, EXPERTS:2 * EXPERTS], bo_columns_sb[:], wc, start=True,
                       stop=True).then_inc(router_step, 1)
                    pe.wait_ge(router_step, 4)

            visits(pe, n, visit, unroll=2, lead=2, tail=3, ahead=3)


def routing(nc, consts_at, w1, w3, w2, kept, x1_rows):
    y_all, mv_all, choice = kept["y"], kept["mv"], kept["choice"]
    weight, pairs, expert_of = kept["weight"], kept["pairs"], kept["expert_of"]
    tiles = choice.shape[1]
    places = pairs.shape[1]
    tokens = tiles * P
    E = EXPERTS
    STORE = 8
    TURN = 4
    turns = tiles // TURN
    BY_ACT = 3

    ctx = ExitStack()
    with ctx:
        def sb(name, shape, dt=F32):
            return ctx.enter_context(nc.sbuf_tensor(name, shape, dt))

        def sem(name):
            return ctx.enter_context(nc.semaphore(name))

        std, rstd = (sb(k, [P, tiles]) for k in ("std", "rstd"))
        hit, diff = (sb(k, [P, tiles, E]) for k in ("hit", "diff"))
        expo, e_gap = kept["expo"], kept["e_gap"]
        oh = [sb(f"oh{k}", [P, tiles, E]) for k in range(TOPK)]
        gap = sb("gap", [P, tiles])
        chosen = sb("chosen", [P, E, tiles], BF16)
        ones_bf = sb("ones_bf", [P, P], BF16)
        behind_bf = sb("behind_bf", [P, P], BF16)
        ones = sb("ones", [P, tiles])
        prior = sb("prior", [P, E, tiles])
        place = sb("place", [P, E, tiles])
        count, needed, ends, starts = (sb(k, [P, E]) for k in ("count", "needed", "ends", "starts"))
        needed_i = sb("needed_i", [P, E], I32)
        at_place = sb("at_place", [P, tiles, TOPK])
        at_i, low_i, high_i = (sb(k, [P, tiles, TOPK], I32) for k in ("at_i", "low_i", "high_i"))
        TILE, NUMBER, NEGATED, POSITION = range(4)
        facts = sb("facts", [P, 4, tiles * TOPK])
        ge_end = sb("ge_end", [P, places, E])
        expert_f = sb("expert_f", [P, places])
        facts_turn = sb("facts_turn", [P, 2, 4, TURN * TOPK])
        distance = sb("distance", [P, 2, BY_ACT * P])
        square = sb("square", [P, 2, BY_ACT * P])
        numbered = sb("numbered", [P, 2, TURN * TOPK, P])
        marked = sb("marked", [P, 2, TURN * TOPK, places])
        found, empty, row, over = (sb(k, [P, places]) for k in ("found", "empty", "row", "over"))
        w_high, w_low = kept["w_high"], kept["w_low"]
        w_raw = sb("w_raw", [P, w_high.shape[1]])
        WIDE = E * HIDDEN
        PIECE = 2 * WIDE // turns

        ps_behind = ctx.enter_context(nc.psum_tensor("ps_behind", [P, 512], F32))
        ps_total = ctx.enter_context(nc.psum_tensor("ps_total", [P, 512], F32))
        ps_pairs = ctx.enter_context(nc.psum_tensor("ps_pairs", [P, 512], F32))

        step = sem("step")
        ones_ready, picks_marked, std_ready, rstd_ready, gaps_ready, exps_ready = map(
            sem, ("ones_ready", "picks_marked", "std_ready", "rstd_ready", "gaps_ready", "exps_ready"))
        chosen_ready, counted, facts_ready, pairs_done = map(
            sem, ("chosen_ready", "counted", "facts_ready", "pairs_done"))
        copied, distance_ready, squared, numbered_by_act, numbered_by_dve, marked_ready, rows_used = map(
            sem, ("copied", "distance_ready", "squared", "numbered_by_act", "numbered_by_dve", "marked_ready", "rows_used"))
        scaled, scaled_by_pool, x1_stored, w2_landed, high_done = map(
            sem, ("scaled", "scaled_by_pool", "x1_stored", "w2_landed", "high_done"))
        raw_landed = [sem(f"raw_landed{k}") for k in (1, 3)]

        block = ctx.enter_context(nc.Block())
        pace = dict(unroll=2, lead=1, tail=2, ahead=1)

        @block.sync
        def _(sp):
            for i, (w, landed) in enumerate(zip((w1, w3), raw_landed)):
                sp.dma_start(w_raw[:, i * WIDE:(i + 1) * WIDE], w).then_inc(landed, 16)
            for i, c in enumerate(range(0, HIDDEN, P)):
                n = min(P, HIDDEN - c)
                sp.dma_start(kept["w2"][0:n, i * EXPERTS * D:(i + 1) * EXPERTS * D], w2[c:c + n, :]).then_inc(
                    w2_landed, 16)
            rows = x1_rows.rearrange("(c t p) d -> c p t d", p=P, t=STORE)
            with sp.Fori(0, tiles // STORE) as c:
                ready, landed = sp.snap(c * (STORE // TURN) + STORE // TURN), sp.snap(c * 16 + 16)
                sp.wait_ge(scaled, ready)
                sp.nop(nofuse=True)
                sp.wait_ge(scaled_by_pool, ready)
                sp.dma_start(rows[c], y_all[:].rearrange("p (c t) d -> p c t d", t=STORE)[:, c, :, :]).then_inc(
                    x1_stored, 16)
                sp.wait_ge(x1_stored, landed)
                sp.nop(nofuse=True)
            sp.wait_ge(w2_landed, 16 * -(-HIDDEN // P))

        @block.gpsimd
        def _(pool):
            pool.memset(ones_bf[:], 1.0).then_inc(ones_ready, 1)
            pool.tensor_copy(behind_bf[:], consts_at("behind")).then_inc(ones_ready, 1)
            pool.memset(ones[:], 1.0).then_inc(ones_ready, 1)
            pool.tensor_copy(facts[:, NUMBER, :], consts_at("numbers")).then_inc(facts_ready, 1)
            pool.tensor_scalar(facts[:, NEGATED, :], consts_at("numbers"), -1.0, None, ALU.mult).then_inc(facts_ready, 1)
            nc.clear_and_free_semaphores(kept["spent"])
            pool.wait_ge(facts_ready, 4)
            pool.wait_ge(rstd_ready, 1)

            def visit(it):
                if it.has(1):
                    r = it.ring(1)
                    it.wait(numbered_by_dve, -1)
                    it.wait(numbered_by_act, -1)
                    pool.tensor_copy(facts_turn[:, r, :, :],
                                     facts[:, :, bass.ds(it.index(1, TURN * TOPK), TURN * TOPK)]).then_inc(copied, 1)
                    it.wait(squared, -1)
                    it.wait(copied, 1)
                    pool.tensor_tensor(
                        distance[:, r, :].rearrange("p (j q) -> p j q", q=P),
                        consts_at("iota")[:, 0:P].rearrange("p (o q) -> p o q", o=1).to_broadcast([P, BY_ACT, P]),
                        facts_turn[:, r, POSITION, 0:BY_ACT].rearrange("p (j o) -> p j o", o=1).to_broadcast(
                            [P, BY_ACT, P]), ALU.subtract).then_inc(distance_ready, 1)

                if it.has(0):
                    rows = y_all[:, TURN - 1:, :][:, bass.ds(it.index(0, TURN), 1), :]
                    pool.tensor_tensor(rows, rows, rstd[:, TURN - 1:][:, bass.ds(it.index(0, TURN), 1)].rearrange(
                        "p (t o) -> p t o", o=1).to_broadcast([P, 1, D]), ALU.mult).then_inc(scaled_by_pool, 1)
                    if it.b == 0:
                        pool.wait_ge(high_done, 2)
                    piece = bass.ds(it.index(0, PIECE), PIECE)
                    pool.tensor_tensor(w_low[:, piece], w_raw[:, piece], w_high[:, piece].bitcast(F32), ALU.subtract)

            visits(pool, turns, visit, **pace)

        @block.scalar
        def _(act):
            act.activation(std[:], mv_all[:, :, 1], ACT.Sqrt, bias=consts_at("eps")).then_inc(std_ready, 1)
            act.wait_ge(gaps_ready, 1)
            act.activation(expo[:].rearrange("p t e -> p (t e)"), diff[:].rearrange("p t e -> p (t e)"),
                           ACT.Exp).then_inc(exps_ready, 1)
            act.activation(e_gap[:], gap[:], ACT.Exp).then_inc(exps_ready, 1)
            y_flat = y_all[:].rearrange("p t d -> p (t d)")
            for i, landed in enumerate(raw_landed):
                act.wait_ge(landed, 16)
                part = slice(i * WIDE, (i + 1) * WIDE)
                act.activation(w_high[:, part], w_raw[:, part], ACT.Copy).then_inc(high_done, 1)

            def visit(it):
                if it.has(0):
                    for t in range(TURN - 1):
                        rows = y_flat[:, t * D:][:, bass.ds(it.index(0, TURN * D), D)]
                        last = act.activation(rows, rows, ACT.Identity,
                                              scale=rstd[:, t:][:, bass.ds(it.index(0, TURN), 1)])
                    last.then_inc(scaled, 1)
                    r = it.ring(0)
                    it.wait(distance_ready, 0)
                    act.activation(square[:, r, :], distance[:, r, :], ACT.Square).then_inc(squared, 1)
                    it.wait(squared, 0)
                    it.wait(rows_used, -2)
                    for j in range(BY_ACT):
                        last = act.activation(numbered[:, r, j, :], square[:, r, j * P:(j + 1) * P], ACT.Relu,
                                              scale=facts_turn[:, r, NEGATED, j:j + 1],
                                              bias=facts_turn[:, r, NUMBER, j:j + 1])
                    last.then_inc(numbered_by_act, 1)

            visits(act, turns, visit, **pace)

        @block.vector
        def _(dve):
            v = nc.vector
            done = [0]

            def chain(instruction):
                done[0] += 1
                instruction.then_inc(step, 1)
                dve.wait_ge(step, done[0])

            def over_experts(a):
                return a.to_broadcast([P, tiles, E])

            def column(c):
                return choice[:, :, E + c:E + c + 1]

            def spread(a):
                return a.rearrange("p (t o) -> p t o", o=1).to_broadcast([P, tiles, E])

            numbers = consts_at("less_8").rearrange("p (o e) -> p o e", o=1).to_broadcast([P, tiles, E])
            for k in range(TOPK):
                v.tensor_tensor(oh[k][:], numbers, over_experts(column(TOPK + k)), ALU.is_equal).then_inc(picks_marked, 1)
            dve.wait_ge(picks_marked, TOPK)
            v.tensor_tensor(chosen[:].rearrange("p e t -> p t e"), oh[0][:], oh[1][:], ALU.add).then_inc(chosen_ready, 1)
            dve.wait_ge(std_ready, 1)
            v.reciprocal(rstd[:], std[:]).then_inc(rstd_ready, 1)
            v.tensor_tensor(diff[:], choice[:, :, 0:E], over_experts(column(0)), ALU.subtract)
            chain(v.tensor_tensor(gap[:].rearrange("p (t o) -> p t o", o=1), column(1), column(0), ALU.subtract))
            dve.wait_ge(rstd_ready, 1)
            v.tensor_tensor(gap[:], gap[:], rstd[:], ALU.mult)
            v.tensor_tensor(diff[:], diff[:], spread(rstd[:]), ALU.mult).then_inc(gaps_ready, 1)

            dve.wait_ge(counted, 2)
            dve.wait_ge(ones_ready, 3)
            in_tile = ps_total[:, 0:E * tiles].rearrange("p (e t) -> p e t", t=tiles)
            chain(v.tensor_reduce(out=count[:], in_=in_tile, axis=AX.X, op=ALU.add))
            chain(v.tensor_scalar(needed_i[:], count[:], 1.0 / P, (P - 1.0) / (2 * P), ALU.mult, ALU.add))
            chain(v.tensor_copy(needed[:], needed_i[:]))
            chain(v.tensor_tensor_scan(ends[:], ones[:, 0:E], needed[:], 0.0, ALU.mult, ALU.add))
            chain(v.tensor_tensor(starts[:], ends[:], needed[:], ALU.subtract))
            chain(v.tensor_scalar(starts[:], starts[:], float(P), None, ALU.mult))
            for e in range(E):
                last = v.tensor_tensor_scan(prior[:, e, :], ones[:], in_tile[:, e, :], starts[:, e:e + 1],
                                            ALU.mult, ALU.add)
            chain(last)
            flat = "p e t -> p (e t)"
            chain(v.tensor_tensor(place[:].rearrange(flat), prior[:].rearrange(flat), ps_behind[:, 0:E * tiles], ALU.add))
            for k in range(TOPK):
                chain(v.tensor_tensor(hit[:], oh[k][:], place[:].rearrange("p e t -> p t e"), ALU.mult))
                chain(v.tensor_reduce(out=at_place[:, :, k], in_=hit[:], axis=AX.X, op=ALU.add))
            chain(v.tensor_copy(at_i[:], at_place[:]))
            v.tensor_single_scalar(out=low_i[:], in_=at_i[:], scalar=P - 1, op=ALU.bitwise_and)
            chain(v.tensor_single_scalar(out=high_i[:], in_=at_i[:], scalar=7, op=ALU.arith_shift_right))
            v.tensor_copy(facts[:, POSITION, :], low_i[:].rearrange("p t k -> p (t k)")).then_inc(facts_ready, 1)
            v.tensor_copy(facts[:, TILE, :], high_i[:].rearrange("p t k -> p (t k)")).then_inc(facts_ready, 1)

            def visit(it):
                if it.has(0):
                    r = it.ring(0)
                    it.wait(copied, 0)
                    it.wait(rows_used, -2)
                    v.tensor_tensor(
                        marked[:, r, :, :],
                        consts_at("iota")[:, 0:places].rearrange("p (o i) -> p o i", o=1).to_broadcast(
                            [P, TURN * TOPK, places]),
                        facts_turn[:, r, TILE, :].rearrange("p (j o) -> p j o", o=1).to_broadcast(
                            [P, TURN * TOPK, places]), ALU.is_equal).then_inc(marked_ready, 1)
                    for j in range(BY_ACT, TURN * TOPK):
                        last = v.tensor_scalar(numbered[:, r, j, :], consts_at("iota")[:, 0:P],
                                               facts_turn[:, r, POSITION, j:j + 1],
                                               facts_turn[:, r, NUMBER, j:j + 1],
                                               ALU.is_equal, ALU.mult)
                    last.then_inc(numbered_by_dve, 1)

            visits(dve, turns, visit, **pace)

            chain(v.tensor_tensor(
                ge_end[:], consts_at("iota")[:, 0:places].rearrange("p (i o) -> p i o", o=1).to_broadcast([P, places, E]),
                ends[:].rearrange("p (o e) -> p o e", o=1).to_broadcast([P, places, E]), ALU.is_ge))
            chain(v.tensor_reduce(out=expert_f[:], in_=ge_end[:], axis=AX.X, op=ALU.add))
            v.tensor_scalar(expert_of[:], expert_f[:], E - 1.0, None, ALU.min)

            dve.wait_ge(pairs_done, 1)
            chain(v.tensor_copy(found[:], ps_pairs[:, 0:places]))
            v.tensor_scalar(empty[:], found[:], 0.0, None, ALU.is_equal)
            chain(v.tensor_scalar(over[:], found[:], float(P + tokens), -float(tokens), ALU.is_ge, ALU.mult))
            chain(v.scalar_tensor_tensor(over[:], found[:], -float(P), over[:], ALU.add, ALU.add))
            v.tensor_scalar(pairs[:, :, 0], over[:], 0.0, None, ALU.max)
            chain(v.tensor_tensor(empty[:], empty[:], consts_at("spare"), ALU.mult))
            chain(v.tensor_tensor(row[:], found[:], empty[:], ALU.add))
            v.tensor_scalar(pairs[:, :, 1], row[:], -float(P), None, ALU.add)

        @block.tensor
        def _(pe):
            mm = nc.tensor.matmul
            pe.wait_ge(ones_ready, 2)
            pe.wait_ge(chosen_ready, 1)
            rhs = chosen[:].rearrange("p e t -> p (e t)")
            mm(ps_total[:, 0:E * tiles], ones_bf[:], rhs, start=True, stop=True).then_inc(counted, 1)
            mm(ps_behind[:, 0:E * tiles], behind_bf[:], rhs, start=True, stop=True).then_inc(counted, 1)

            def visit(it):
                if it.has(0):
                    r = it.ring(0)
                    it.wait(marked_ready, 0)
                    it.wait(numbered_by_act, 0)
                    it.wait(numbered_by_dve, 0)
                    for j in range(TURN * TOPK):
                        last = mm(ps_pairs[:, 0:places], numbered[:, r, j, :], marked[:, r, j, :],
                                  start=it.b == 0 and j == 0, stop=it.b == turns - 1 and j == TURN * TOPK - 1)
                    last.then_inc(rows_used, 1)
                    if it.b == turns - 1:
                        pe.wait_ge(rows_used, turns)
                        pe.nop().then_inc(pairs_done, 1)

            visits(pe, turns, visit, unroll=2, lead=0, tail=2, ahead=1)


def experts(nc, ident, kept, x1_rows, out_rows):
    expo, e_gap, weight = kept["expo"], kept["e_gap"], kept["weight"]
    w2, pairs, expert_of = (kept[k] for k in ("w2", "pairs", "expert_of"))
    n = pairs.shape[1]
    RING, IDX = 4, 8
    CHUNKS = [(c, min(P, HIDDEN - c)) for c in range(0, HIDDEN, P)]

    ctx = ExitStack()
    with ctx:
        def sb(name, shape, dt=F32):
            return ctx.enter_context(nc.sbuf_tensor(name, shape, dt))

        def sem(name):
            return ctx.enter_context(nc.semaphore(name))

        idx = sb("idx", [P, IDX, 2], I32)
        xg = sb("xg", [P, RING, D])
        x_high, x_low = (sb(k, [P, 2, P], F32R) for k in ("x_high", "x_low"))
        act_a = sb("act_a", [P, 2, HIDDEN])
        h = sb("h", [P, 2, len(CHUNKS) * P])
        h_t = sb("h_t", [P, 2, len(CHUNKS) * P])
        rows_out = sb("rows_out", [P, RING, D])
        ps_a = ctx.enter_context(nc.psum_tensor("ps_a", [P, 2, 512], F32))
        ps_b = ctx.enter_context(nc.psum_tensor("ps_b", [P, 2, 512], F32))
        ps_h = ctx.enter_context(nc.psum_tensor("ps_h", [P, 2, 512], F32))
        ps_x = ctx.enter_context(nc.psum_tensor("ps_x", [P, 512], F32))
        ps_y = ctx.enter_context(nc.psum_tensor("ps_y", [P, 512], F32))

        total, rtotal, den = (sb(k, list(e_gap.shape)) for k in ("total", "rtotal", "den"))
        score = [sb(f"score{k}", list(e_gap.shape)) for k in range(TOPK)]
        warm = sb("warm", [P, 1])

        padded, weigh_step = sem("padded"), sem("weigh_step")
        idx_ready, x_turned, high_taken, x_taken, a_done, b_done, a_taken, h_ready, h_turned, h_taken, y_done, y_taken = map(
            sem, ("idx_ready", "x_turned", "high_taken", "x_taken", "a_done", "b_done", "a_taken", "h_ready", "h_turned", "h_taken",
                  "y_done", "y_taken"))
        gathered = [sem(f"gathered{i}") for i in range(RING)]
        scattered = [sem(f"scattered{i}") for i in range(RING)]

        block = ctx.enter_context(nc.Block())
        pace = dict(unroll=IDX, lead=4, tail=2, ahead=4)

        @block.gpsimd
        def _(pool):
            def visit(it):
                if it.has(3):
                    it.wait(idx_ready, 3)
                    it.wait(x_turned, 3 - RING)
                    pool.indirect_dma_start(
                        out=xg[:, it.ring(3, RING), :], out_offset=None, in_=x1_rows,
                        in_offset=bass.IndirectOffsetOnAxis(ap=idx[:, it.ring(3, IDX), 0:1], axis=0),
                    ).then_inc(gathered[it.ring(3, RING)], 16)
                if it.has(-2):
                    it.wait(y_taken, -2)
                    pool.indirect_dma_start(
                        out=out_rows, out_offset=bass.IndirectOffsetOnAxis(ap=idx[:, it.ring(-2, IDX), 1:2], axis=0),
                        in_=rows_out[:, it.ring(-2, RING), :], in_offset=None,
                    ).then_inc(scattered[it.ring(-2, RING)], 16)

            visits(pool, n, visit, **pace)
            for i in range(RING):
                pool.wait_ge(scattered[i], 16 * (n // RING))

        @block.scalar
        def _(act):
            act.activation(warm[:], ident[:, 0:1], ACT.Silu)

            def visit(it):
                if it.has(0):
                    it.wait(a_done, 0)
                    it.wait(h_ready, -2)
                    act.activation(act_a[:, it.ring(0), :], ps_a[:, it.ring(0), 0:HIDDEN], ACT.Silu).then_inc(a_taken, 1)
                if it.has(1):
                    it.wait(x_turned, 1)
                    it.wait(b_done, -1)
                    act.activation(x_high[:, it.ring(1), :], ps_x[:, 0:P], ACT.Copy).then_inc(high_taken, 1)
                if it.has(-2):
                    it.wait(y_done, -2)
                    it.wait_landed(scattered, -2 - RING)
                    act.activation(rows_out[:, it.ring(-2, RING), :], ps_y[:, 0:D], ACT.Copy).then_inc(y_taken, 1)

            visits(act, n, visit, **pace)

        @block.vector
        def _(dve):
            for u in range(2):
                nc.vector.memset(h[:, u, HIDDEN:], 0.0).then_inc(padded, 1)

            def visit(it):
                if it.has(4):
                    it.wait_landed(scattered, 4 - IDX)
                    nc.vector.tensor_copy(idx[:, it.ring(4, IDX), :].rearrange("p (o s) -> p o s", o=1),
                                          pairs[:, bass.ds(it.index(4), 1), :]).then_inc(idx_ready, 1)
                if it.has(1):
                    it.wait(high_taken, 1)
                    it.wait(b_done, -1)
                    nc.vector.tensor_tensor(x_low[:, it.ring(1), :], ps_x[:, 0:P], x_high[:, it.ring(1), :].bitcast(F32),
                                            ALU.subtract).then_inc(x_taken, 1)
                if it.has(-1):
                    it.wait(h_turned, -1)
                    it.wait(y_done, -3)
                    nc.vector.tensor_copy(h_t[:, it.ring(-1), :], ps_h[:, it.ring(-1), 0:len(CHUNKS) * P]).then_inc(
                        h_taken, 1)
                if it.has(0):
                    it.wait(a_taken, 0)
                    it.wait(b_done, 0)
                    it.wait(h_turned, -2)
                    nc.vector.tensor_tensor(h[:, it.ring(0), 0:HIDDEN], act_a[:, it.ring(0), :],
                                            ps_b[:, it.ring(0), 0:HIDDEN], ALU.mult).then_inc(h_ready, 1)

            visits(dve, n, visit, **pace)

            v = nc.vector
            score_of = [
                lambda: v.tensor_reduce(out=total[:], in_=expo[:], axis=AX.X, op=ALU.add),
                lambda: v.reciprocal(score[0][:], total[:]),
                lambda: v.tensor_tensor(score[1][:], e_gap[:], score[0][:], ALU.mult),
                lambda: v.tensor_tensor(den[:], score[0][:], score[1][:], ALU.add),
                lambda: v.tensor_scalar(den[:], den[:], 1e-20, None, ALU.add),
                lambda: v.reciprocal(rtotal[:], den[:]),
            ]
            for i, compute in enumerate(score_of):
                compute().then_inc(weigh_step, 1)
                dve.wait_ge(weigh_step, i + 1)
            for k in range(TOPK):
                v.tensor_tensor(weight[:, k, :], score[k][:], rtotal[:], ALU.mult)

        @block.tensor
        def _(pe):
            mm = nc.tensor.matmul
            pe.wait_ge(padded, 2)
            in_range = "the routing bounds each tile's expert by EXPERTS - 1"
            bounds = dict(engines=[mybir.EngineType.PE], min_val=0, max_val=EXPERTS - 1,
                          skip_runtime_bounds_check_because=in_range)
            held = {}

            def expert(it, off):
                if it.b is not None:
                    return nc.values_load(expert_of[0:1, it.b + off:it.b + off + 1], **bounds)
                if not held:
                    first = it.index(-2)
                    _, values = nc.values_load_multi_w_load_instructions(
                        expert_of[0:1, bass.ds(first, IDX + 2)], **bounds)
                    held.update(enumerate(values, -2))
                return held[it.u + off]

            def wide(it, out, w, e):
                cols = bass.ds(e * HIDDEN + w * EXPERTS * HIDDEN, HIDDEN)
                x_parts = (x_high, x_high, x_low)
                w_parts = (kept["w_high"], kept["w_low"], kept["w_high"])
                for i, (x_part, w_part) in enumerate(zip(x_parts, w_parts)):
                    last = mm(out, x_part[:, it.ring(0), :], w_part[:, cols], start=i == 0, stop=i == PARTS - 1)
                return last

            def visit(it):
                if it.has(0):
                    e = expert(it, 0)
                    it.wait(x_taken, 0)
                    it.wait(a_taken, -2)
                    wide(it, ps_a[:, it.ring(0), 0:HIDDEN], 0, e).then_inc(a_done, 1)
                if it.has(1):
                    it.wait_landed(gathered, 1)
                    it.wait(x_taken, 0)
                    nc.tensor.transpose(ps_x[:, 0:P], xg[:, it.ring(1, RING), :], ident).then_inc(x_turned, 1)
                if it.has(0):
                    it.wait(h_ready, -2)
                    wide(it, ps_b[:, it.ring(0), 0:HIDDEN], 1, e).then_inc(b_done, 1)
                if it.has(-2):
                    e = expert(it, -2)
                    it.wait(h_taken, -2)
                    it.wait(y_taken, -3)
                    for i, (c, rows) in enumerate(CHUNKS):
                        last = mm(ps_y[:, 0:D], h_t[0:rows, it.ring(-2), c:c + P],
                                  w2[0:rows, bass.ds(e * D + i * EXPERTS * D, D)],
                                  start=(i == 0), stop=(i == len(CHUNKS) - 1))
                    last.then_inc(y_done, 1)
                if it.has(-1):
                    it.wait(h_ready, -1)
                    it.wait(h_taken, -3)
                    for c, _ in CHUNKS:
                        last = nc.tensor.transpose(ps_h[:, it.ring(-1), c:c + P], h[:, it.ring(-1), c:c + P], ident)
                    last.then_inc(h_turned, 1)

            visits(pe, n, visit, **pace)


def combine(nc, eps, kept, picked_rows, out):
    x1, weight = kept["y"], kept["weight"]
    tiles = x1.shape[1]
    C = 4
    BY_ACT = 2
    BY_POOL = 2
    RING, LOADS = 4, 8
    AHEAD = 6
    n = tiles // C
    x1_flat = x1[:].rearrange("p t d -> p (t d)")
    picked = [picked_rows[k * tiles * P:(k + 1) * tiles * P, :].rearrange("(c t p) d -> c p t d", p=P, t=C)
              for k in range(TOPK)]
    out_v = out.rearrange("(c t p) d -> c p t d", p=P, t=C)

    ctx = ExitStack()
    with ctx:
        def sb(name, shape, dt=F32):
            return ctx.enter_context(nc.sbuf_tensor(name, shape, dt))

        def sem(name):
            return ctx.enter_context(nc.semaphore(name))

        pick = sb("pick", [P, LOADS, TOPK, C, D])
        w_chunk = sb("w_chunk", [P, RING, TOPK, C])
        weighed = sb("weighed", [P, RING, TOPK, C, D])
        part, z, normal = (sb(k, [P, RING, C, D]) for k in ("part", "z", "normal"))
        z_stats = sb("z_stats", [P, RING, C, 6])
        z_mv = sb("z_mv", [P, RING, C, 2])
        deviation, scale, offset = (sb(k, [P, RING, C]) for k in ("deviation", "scale", "offset"))
        landed = [sem(f"landed{i}") for i in range(LOADS)]
        stored = [sem(f"stored{i}") for i in range(RING)]
        pool_weighed = sem("pool_weighed")
        weighed_ready = [sem(f"weighed_ready{k}") for k in range(TOPK)]
        w_ready, part_ready, z_ready, z_stats_ready, z_mv_ready = map(
            sem, ("w_ready", "part_ready", "z_ready", "z_stats_ready", "z_mv_ready"))
        deviation_ready, scale_ready, offset_ready, act_normal, dve_normal = map(
            sem, ("deviation_ready", "scale_ready", "offset_ready", "act_normal", "dve_normal"))
        block = ctx.enter_context(nc.Block())
        pace = dict(unroll=LOADS, lead=AHEAD, tail=2, ahead=AHEAD)

        @block.sync
        def _(sp):
            def visit(it):
                if it.has(AHEAD):
                    it.wait(weighed_ready[TOPK - 1], AHEAD - LOADS)
                    it.wait(pool_weighed, AHEAD - LOADS)
                    for k in range(TOPK):
                        sp.dma_start(pick[:, it.ring(AHEAD, LOADS), k, :, :], picked[k][it.index(AHEAD)]).then_inc(
                            landed[it.ring(AHEAD, LOADS)], 16)
                if it.has(-1):
                    it.wait(act_normal, -1)
                    it.wait(dve_normal, -1)
                    sp.dma_start(out_v[it.index(-1)], normal[:, it.ring(-1, RING), :, :]).then_inc(
                        stored[it.ring(-1, RING)], 16)

            visits(sp, n, visit, **pace)
            for i in range(RING):
                sp.wait_ge(stored[i], 16 * len(range(i, n, RING)))

        @block.gpsimd
        def _(pool):
            def visit(it):
                if it.has(3):
                    it.wait(weighed_ready[TOPK - 1], 3 - RING)
                    pool.tensor_copy(w_chunk[:, it.ring(3, RING), :, :],
                                     weight[:, :, bass.ds(it.index(3, C), C)]).then_inc(w_ready, 1)
                if it.has(1):
                    r = it.ring(1, RING)
                    it.wait(z_ready, 1 - RING)
                    it.wait_landed(landed, 1, TOPK)
                    it.wait(w_ready, 1)
                    pool.tensor_tensor(
                        weighed[:, r, 0, 0:BY_POOL, :], pick[:, it.ring(1, LOADS), 0, 0:BY_POOL, :],
                        w_chunk[:, r, 0, 0:BY_POOL].rearrange("p (t o) -> p t o", o=1).to_broadcast([P, BY_POOL, D]),
                        ALU.mult).then_inc(pool_weighed, 1)
                    it.wait(pool_weighed, 1)
                    it.wait(weighed_ready[0], 1)
                    pool.tensor_tensor(part[:, r, :, :].rearrange("p t d -> p (t d)"),
                                       weighed[:, r, 0, :, :].rearrange("p t d -> p (t d)"),
                                       x1_flat[:, bass.ds(it.index(1, C * D), C * D)], ALU.add).then_inc(part_ready, 1)

            visits(pool, n, visit, **pace)

        @block.scalar
        def _(act):
            def visit(it):
                if it.has(2):
                    r = it.ring(2, RING)
                    it.wait_landed(landed, 2, TOPK)
                    it.wait(w_ready, 2)
                    it.wait(z_ready, 2 - RING)
                    for k in range(TOPK):
                        for t in range(0 if k else BY_POOL, C):
                            last = act.activation(weighed[:, r, k, t, :], pick[:, it.ring(2, LOADS), k, t, :], ACT.Copy,
                                                  scale=w_chunk[:, r, k, t:t + 1])
                        last.then_inc(weighed_ready[k], 1)
                if it.has(0):
                    r = it.ring(0, RING)
                    it.wait(z_mv_ready, 0)
                    act.activation(deviation[:, r, :], z_mv[:, r, :, 1], ACT.Sqrt, bias=eps).then_inc(deviation_ready, 1)
                if it.has(-1):
                    r = it.ring(-1, RING)
                    it.wait(offset_ready, -1)
                    it.wait_landed(stored, -1 - RING)
                    for t in range(BY_ACT):
                        last = act.activation(normal[:, r, t, :], z[:, r, t, :], ACT.Identity,
                                              scale=scale[:, r, t:t + 1], bias=offset[:, r, t:t + 1])
                    last.then_inc(act_normal, 1)

            visits(act, n, visit, **pace)

        @block.vector
        def _(dve):
            v = nc.vector

            def visit(it):
                r, before = it.ring(0, RING), it.ring(-1, RING)
                if it.has(0):
                    it.wait(part_ready, 0)
                    it.wait(act_normal, -RING)
                    it.wait(weighed_ready[1], 0)
                    v.tensor_tensor(z[:, r, :, :], weighed[:, r, 1, :, :], part[:, r, :, :], ALU.add).then_inc(z_ready, 1)
                if it.has(-1):
                    it.wait(deviation_ready, -1)
                    v.reciprocal(scale[:, before, :], deviation[:, before, :]).then_inc(scale_ready, 1)
                if it.has(0):
                    it.wait(z_ready, 0)
                    for t in range(C):
                        last = v.bn_stats(z_stats[:, r, t, :], z[:, r, t, :])
                    last.then_inc(z_stats_ready, 1)
                if it.has(-1):
                    it.wait(scale_ready, -1)
                    v.scalar_tensor_tensor(offset[:, before, :], z_mv[:, before, :, 0], -1.0, scale[:, before, :],
                                           ALU.mult, ALU.mult).then_inc(offset_ready, 1)
                if it.has(0):
                    it.wait(z_stats_ready, 0)
                    it.settle()
                    for t in range(C):
                        last = v.bn_aggr(z_mv[:, r, t, :], z_stats[:, r, t, :])
                    last.then_inc(z_mv_ready, 1)
                if it.has(-1):
                    it.wait(offset_ready, -1)
                    it.wait_landed(stored, -1 - RING)
                    for t in range(BY_ACT, C):
                        last = v.tensor_scalar(normal[:, before, t, :], z[:, before, t, :], scale[:, before, t:t + 1],
                                               offset[:, before, t:t + 1], ALU.mult, ALU.add)
                    last.then_inc(dve_normal, 1)

            visits(dve, n, visit, **pace)


def build(nc, x, xt, wqkv, bqk, bv, wo, wo_rows, bo, bo_columns, wg, sel, consts, w1, w3, w2, out):
    tokens = x.shape[0]
    tiles = tokens // P
    places = -(-(tiles * TOPK + EXPERTS - 1) // 8) * 8
    x1_rows = nc.dram_tensor("x1_rows", (tokens, D), F32).ap()
    picked_rows = nc.dram_tensor("picked_rows", (TOPK * tokens + places * P, D), F32).ap()

    ctx = ExitStack()
    with ctx:
        def sb(name, shape, dt=F32):
            return ctx.enter_context(nc.sbuf_tensor(name, shape, dt))

        cst = sb("cst", [P, consts.shape[1]])
        at = columns(tiles, places)

        def consts_at(name):
            return cst[:, at[name][0]:at[name][1]]

        kept = {
            "spent": [],
            "y": sb("y_all", [P, tiles, D]), "mv": sb("mv_all", [P, tiles, 2]),
            "expo": sb("expo", [P, tiles, EXPERTS]), "e_gap": sb("e_gap", [P, tiles]),
            "choice": sb("choice", [P, tiles, EXPERTS + 2 * TOPK]), "less_8": consts_at("less_8"),
            "weight": sb("weight", [P, TOPK, tiles]),
            "pairs": sb("pairs", [P, places, 2], I32), "expert_of": sb("expert_of", [P, places], I32),
        }
        attention(nc, x, xt, wqkv, bqk, bv, wo, wo_rows, bo, bo_columns, wg, sel, cst, consts, kept)
        kept.update(w_high=sb("w_high", [P, 2 * EXPERTS * HIDDEN], F32R), w_low=sb("w_low", [P, 2 * EXPERTS * HIDDEN], F32R),
                    w2=sb("w2_sb", [P, -(-HIDDEN // P) * EXPERTS * D]))
        routing(nc, consts_at, w1, w3, w2, kept, x1_rows)
        experts(nc, consts_at("ident"), kept, x1_rows, picked_rows)
        combine(nc, consts_at("eps"), kept, picked_rows, out)


def columns(tiles, places):
    widths = {"ident": P, "mask": P, "shift_rows": 1, "behind": P, "iota": max(P, places), "less_8": EXPERTS,
              "numbers": TOPK * tiles, "partition": 1, "spare": places, "eps": 1}
    at, out = 0, {}
    for name, width in widths.items():
        out[name] = (at, at + width)
        at += width
    out["end"] = (at, at)
    return out


def table(tiles, places):
    at = columns(tiles, places)
    out = np.zeros((P, at["end"][0]), np.float32)

    def put(name, value):
        out[:, at[name][0]:at[name][1]] = value

    put("ident", np.eye(P))
    put("mask", np.triu(np.full((P, P), MASKED), 1))
    out[SHIFT_ROW:SHIFT_ROW + 2, at["shift_rows"][0]] = 1
    put("behind", np.triu(np.ones((P, P)), 1) - 1)
    put("iota", np.arange(at["iota"][1] - at["iota"][0]))
    put("less_8", np.arange(EXPERTS) - EXPERTS)
    tile, pick = np.divmod(np.arange(TOPK * tiles), TOPK)
    put("numbers", (1 + tile + tiles * pick) * P + np.arange(P)[:, None])
    put("eps", EPS)
    put("partition", np.arange(P)[:, None])
    put("spare", P + TOPK * tiles * P + np.arange(P)[:, None] + P * np.arange(places))
    return out


def layout(inputs):
    def f(a):
        return np.ascontiguousarray(np.asarray(a))

    x = f(inputs["L0_attn_x"]).reshape(-1, D)
    tiles = x.shape[0] // P
    places = -(-(tiles * TOPK + EXPERTS - 1) // 8) * 8
    w = f(inputs["L0_attn_qkv_w"])
    b = f(inputs["L0_attn_qkv_b"])
    return {
        "x": x, "xt": f(x.T), "wqkv": f(w.T), "bqk": f(b[:2 * D].reshape(2, D).T),
        "bv": f(np.broadcast_to(b[2 * D:], (P, D))), "wo": f(np.asarray(inputs["L0_attn_out_w"]).T),
        "wo_rows": f(inputs["L0_attn_out_w"]),
        "bo_columns": f(np.broadcast_to(np.asarray(inputs["L0_attn_out_b"])[:, None], (D, P))),
        "bo": f(np.broadcast_to(np.tile(np.asarray(inputs["L0_attn_out_b"]), BLOCKS), (P, BLOCKS * D))),
        "wg": f(np.asarray(inputs["L0_ffn_Wg"]).T), "sel": selectors(), "consts": table(tiles, places),
        "w1": f(np.asarray(inputs["L0_ffn_W1"]).transpose(2, 0, 1).reshape(D, -1)),
        "w3": f(np.asarray(inputs["L0_ffn_W3"]).transpose(2, 0, 1).reshape(D, -1)),
        "w2": f(np.asarray(inputs["L0_ffn_W2"]).transpose(2, 0, 1).reshape(HIDDEN, -1)),
    }


def kernel(**inputs):
    import concourse.bacc as bacc
    from concourse.bass_utils import run_bass_kernel_spmd

    nc = bacc.Bacc("TRN2", target_bir_lowering=False, num_devices=1)
    arrays = layout(inputs)
    shape = np.asarray(inputs["L0_attn_x"]).shape
    args = {name: nc.dram_tensor(name, a.shape, mybir.dt.from_np(a.dtype), kind="ExternalInput").ap()
            for name, a in arrays.items()}
    out = nc.dram_tensor("out", (shape[0] * shape[1], D), F32, kind="ExternalOutput").ap()
    build(nc, out=out, **args)
    got = run_bass_kernel_spmd(nc, [arrays], core_ids=[0])
    return np.asarray(got.results[0]["out"]).reshape(shape)
```
